# Optimizing a Trainium2 kernel written in Bass

```python
import numpy as np
import jax
import jax.numpy as jnp

def _softmax(x, axis=-1):
    return jax.nn.softmax(x, axis=axis)

def _gelu(x):
    return jax.nn.gelu(x, approximate=True)

def _silu(x):
    return jax.nn.silu(x)

def _sigmoid(x):
    return jax.nn.sigmoid(x)

def _layernorm(x, axis=-1, eps=1e-05):
    m = jnp.mean(x, axis=axis, keepdims=True)
    v = jnp.var(x, axis=axis, keepdims=True)
    return (x - m) / jnp.sqrt(v + eps)

def _scatter_add(tgt, idx, src, axis=0):
    return tgt.at[idx].add(src)

def _segment_sum(src, seg, n):
    return jax.ops.segment_sum(src, seg, n)
kernel_name = 'mk_gps_d1_gnn_r8_8de486'

def setup_inputs(seed: int=0):
    np.random.seed(seed)
    _w = jnp.asarray

    def _rec_inputs():
        import jax
        import jax.numpy as jnp
        _gk = jax.random.key(seed)
        x = -0.0002117 + 1 * jax.random.normal(jax.random.fold_in(_gk, 1), (6250, 512), jnp.float32)
        src = jax.random.randint(jax.random.fold_in(_gk, 2), (100000,), 0, 6250, jnp.int32)
        dst = jax.random.randint(jax.random.fold_in(_gk, 3), (100000,), 0, 6250, jnp.int32)
        _o = jnp.argsort(dst, stable=True)
        src = src[_o]
        dst = dst[_o]
        return (x, src, dst)
    x, src, dst = _rec_inputs()

    def _L0_gnn_setup():
        import jax, jax.numpy as jnp
        import numpy as np
        N_NODES = 6250
        DIM = 512
        N_EDGES = 20000
        key = jax.random.key(seed)
        k_x, k_e, k_ws, k_bs, k_wn, k_bn = jax.random.split(key, 6)
        scale = 1.0 / np.sqrt(DIM)
        return {'x': jax.random.normal(k_x, (N_NODES, DIM), dtype=jnp.float32), 'edge_index': jax.random.randint(k_e, (2, N_EDGES), 0, N_NODES, dtype=jnp.int64), 'self_w': jax.random.uniform(k_ws, (DIM, DIM), jnp.float32, -scale, scale), 'self_b': jax.random.uniform(k_bs, (DIM,), jnp.float32, -scale, scale), 'neigh_w': jax.random.uniform(k_wn, (DIM, DIM), jnp.float32, -scale, scale), 'neigh_b': jax.random.uniform(k_bn, (DIM,), jnp.float32, -scale, scale)}
    _L0_gnn_all = _L0_gnn_setup()
    _L0_gnn_in = {k: v for k, v in _L0_gnn_all.items() if k in ('self_w', 'self_b', 'neigh_w', 'neigh_b')}
    del _L0_gnn_all

    def _L0_mix_setup():
        import jax, jax.numpy as jnp
        import numpy as np
        EPS = 1e-06
        H = 8
        DH = 64
        LN_EPS = 1e-05

        def _layernorm(x, g, b):
            m = jnp.mean(x, axis=-1, keepdims=True)
            v = jnp.mean(jnp.square(x - m), axis=-1, keepdims=True)
            return (x - m) / jnp.sqrt(v + LN_EPS) * g + b

        def _flow_attention(x, Wq, bq, Wk, bk, Wv, bv, Wo, bo):
            B, L, D = x.shape
            S = L
            q = jax.nn.sigmoid((x @ Wq + bq).reshape(B, L, H, DH).transpose(0, 2, 1, 3))
            k = jax.nn.sigmoid((x @ Wk + bk).reshape(B, S, H, DH).transpose(0, 2, 1, 3))
            v = (x @ Wv + bv).reshape(B, S, H, DH).transpose(0, 2, 1, 3)
            sink_incoming = 1.0 / jnp.einsum('nhld,nhd->nhl', q + EPS, k.sum(axis=2) + EPS)
            source_outgoing = 1.0 / jnp.einsum('nhld,nhd->nhl', k + EPS, q.sum(axis=2) + EPS)
            conserved_sink = jnp.einsum('nhld,nhd->nhl', q + EPS, (k * source_outgoing[..., None]).sum(axis=2) + EPS)
            conserved_source = jnp.einsum('nhld,nhd->nhl', k + EPS, (q * sink_incoming[..., None]).sum(axis=2) + EPS)
            conserved_source = jnp.clip(conserved_source, -1.0, 1.0)
            sink_allocation = jax.nn.sigmoid(conserved_sink * (float(L) / float(S)))
            source_competition = jax.nn.softmax(conserved_source, axis=-1) * float(S)
            kv = jnp.einsum('nhld,nhlm->nhdm', k, v * source_competition[..., None])
            o = jnp.einsum('nhld,nhdm->nhlm', q * sink_incoming[..., None], kv)
            o = o * sink_allocation[..., None]
            o = o.transpose(0, 2, 1, 3).reshape(B, L, D)
            return o @ Wo + bo
        key = jax.random.key(seed)
        ks = jax.random.split(key, 16)
        B, L, D, F = (2, 2048, 512, 256)
        s = 0.02
        inp = {'x': jax.random.normal(ks[0], (B, L, D), dtype=jnp.float32), 'Wq': jax.random.normal(ks[1], (D, D), dtype=jnp.float32) * s, 'bq': jnp.zeros((D,), jnp.float32), 'Wk': jax.random.normal(ks[2], (D, D), dtype=jnp.float32) * s, 'bk': jnp.zeros((D,), jnp.float32), 'Wv': jax.random.normal(ks[3], (D, D), dtype=jnp.float32) * s, 'bv': jnp.zeros((D,), jnp.float32), 'Wo': jax.random.normal(ks[4], (D, D), dtype=jnp.float32) * s, 'bo': jnp.zeros((D,), jnp.float32), 'W1': jax.random.normal(ks[5], (D, F), dtype=jnp.float32) * s, 'b1': jnp.zeros((F,), jnp.float32), 'W2': jax.random.normal(ks[6], (F, D), dtype=jnp.float32) * s, 'b2': jnp.zeros((D,), jnp.float32), 'g1': jnp.ones((D,), jnp.float32), 'be1': jnp.zeros((D,), jnp.float32), 'g2': jnp.ones((D,), jnp.float32), 'be2': jnp.zeros((D,), jnp.float32)}
        return inp
    _L0_mix_all = _L0_mix_setup()
    _L0_mix_in = {k: v for k, v in _L0_mix_all.items() if k in ('Wq', 'bq', 'Wk', 'bk', 'Wv', 'bv', 'Wo', 'bo', 'W1', 'b1', 'W2', 'b2', 'g1', 'be1', 'g2', 'be2')}
    del _L0_mix_all

    def _L0_ffn_setup():
        import jax, jax.numpy as jnp
        import numpy as np
        B, T, D, F, E, K = (8, 1024, 512, 256, 8, 2)

        def _moe_forward(x, Wr, br, W1, b1, W2, b2):
            Bx, Tx, Dx = x.shape
            xf = x.reshape(-1, Dx)
            logits = xf @ Wr + br
            probs = jax.nn.softmax(logits, axis=-1)
            vals, idx = jax.lax.top_k(probs, K)
            cw = (jax.nn.one_hot(idx, E, dtype=x.dtype) * vals[..., None]).sum(axis=1)

            def body(acc, params):
                W1e, b1e, W2e, b2e, cwe = params
                h = jax.nn.relu(xf @ W1e + b1e)
                y = h @ W2e + b2e
                return (acc + cwe[:, None] * y, None)
            out, _ = jax.lax.scan(body, jnp.zeros_like(xf), (W1, b1, W2, b2, cw.T))
            return out.reshape(Bx, Tx, Dx)
        key = jax.random.key(seed)
        k0, k1, k2, k3 = jax.random.split(key, 4)
        s_d = 1.0 / np.sqrt(D)
        s_f = 1.0 / np.sqrt(F)
        return {'x': jax.random.normal(k0, (B, T, D), jnp.float32), 'Wr': jax.random.uniform(k1, (D, E), jnp.float32, -s_d, s_d), 'br': jnp.zeros((E,), jnp.float32), 'W1': jax.random.uniform(k2, (E, D, F), jnp.float32, -s_d, s_d), 'b1': jnp.zeros((E, F), jnp.float32), 'W2': jax.random.uniform(k3, (E, F, D), jnp.float32, -s_f, s_f), 'b2': jnp.zeros((E, D), jnp.float32)}
    _L0_ffn_all = _L0_ffn_setup()
    _L0_ffn_in = {k: v for k, v in _L0_ffn_all.items() if k in ('Wr', 'br', 'W1', 'b1', 'W2', 'b2')}
    del _L0_ffn_all
    return {'x': x, 'src': src, 'dst': dst, 'L0_gnn_self_w': _L0_gnn_in['self_w'], 'L0_gnn_self_b': _L0_gnn_in['self_b'], 'L0_gnn_neigh_w': _L0_gnn_in['neigh_w'], 'L0_gnn_neigh_b': _L0_gnn_in['neigh_b'], 'L0_mix_Wq': _L0_mix_in['Wq'], 'L0_mix_bq': _L0_mix_in['bq'], 'L0_mix_Wk': _L0_mix_in['Wk'], 'L0_mix_bk': _L0_mix_in['bk'], 'L0_mix_Wv': _L0_mix_in['Wv'], 'L0_mix_bv': _L0_mix_in['bv'], 'L0_mix_Wo': _L0_mix_in['Wo'], 'L0_mix_bo': _L0_mix_in['bo'], 'L0_mix_W1': _L0_mix_in['W1'], 'L0_mix_b1': _L0_mix_in['b1'], 'L0_mix_W2': _L0_mix_in['W2'], 'L0_mix_b2': _L0_mix_in['b2'], 'L0_mix_g1': _L0_mix_in['g1'], 'L0_mix_be1': _L0_mix_in['be1'], 'L0_mix_g2': _L0_mix_in['g2'], 'L0_mix_be2': _L0_mix_in['be2'], 'L0_ffn_Wr': _L0_ffn_in['Wr'], 'L0_ffn_br': _L0_ffn_in['br'], 'L0_ffn_W1': _L0_ffn_in['W1'], 'L0_ffn_b1': _L0_ffn_in['b1'], 'L0_ffn_W2': _L0_ffn_in['W2'], 'L0_ffn_b2': _L0_ffn_in['b2']}

def reference(x, src, dst, L0_gnn_self_w, L0_gnn_self_b, L0_gnn_neigh_w, L0_gnn_neigh_b, L0_mix_Wq, L0_mix_bq, L0_mix_Wk, L0_mix_bk, L0_mix_Wv, L0_mix_bv, L0_mix_Wo, L0_mix_bo, L0_mix_W1, L0_mix_b1, L0_mix_W2, L0_mix_b2, L0_mix_g1, L0_mix_be1, L0_mix_g2, L0_mix_be2, L0_ffn_Wr, L0_ffn_br, L0_ffn_W1, L0_ffn_b1, L0_ffn_W2, L0_ffn_b2):
    import jax
    import jax.numpy as jnp

    def _L0_gnn_ref(x, edge_index, self_w, self_b, neigh_w, neigh_b):
        import jax, jax.numpy as jnp
        import numpy as np
        N_NODES = 6250
        DIM = 512
        N_EDGES = 20000
        row, col = (edge_index[0], edge_index[1])
        agg = jax.ops.segment_sum(x[col], row, num_segments=x.shape[0])
        out = jnp.dot(x, self_w.T) + self_b + jnp.dot(agg, neigh_w.T) + neigh_b
        return jax.nn.relu(out)

    def _L0_mix_ref(x, Wq, bq, Wk, bk, Wv, bv, Wo, bo, W1, b1, W2, b2, g1, be1, g2, be2):
        import jax, jax.numpy as jnp
        import numpy as np
        EPS = 1e-06
        H = 8
        DH = 64
        LN_EPS = 1e-05

        def _layernorm(x, g, b):
            m = jnp.mean(x, axis=-1, keepdims=True)
            v = jnp.mean(jnp.square(x - m), axis=-1, keepdims=True)
            return (x - m) / jnp.sqrt(v + LN_EPS) * g + b

        def _flow_attention(x, Wq, bq, Wk, bk, Wv, bv, Wo, bo):
            B, L, D = x.shape
            S = L
            q = jax.nn.sigmoid((x @ Wq + bq).reshape(B, L, H, DH).transpose(0, 2, 1, 3))
            k = jax.nn.sigmoid((x @ Wk + bk).reshape(B, S, H, DH).transpose(0, 2, 1, 3))
            v = (x @ Wv + bv).reshape(B, S, H, DH).transpose(0, 2, 1, 3)
            sink_incoming = 1.0 / jnp.einsum('nhld,nhd->nhl', q + EPS, k.sum(axis=2) + EPS)
            source_outgoing = 1.0 / jnp.einsum('nhld,nhd->nhl', k + EPS, q.sum(axis=2) + EPS)
            conserved_sink = jnp.einsum('nhld,nhd->nhl', q + EPS, (k * source_outgoing[..., None]).sum(axis=2) + EPS)
            conserved_source = jnp.einsum('nhld,nhd->nhl', k + EPS, (q * sink_incoming[..., None]).sum(axis=2) + EPS)
            conserved_source = jnp.clip(conserved_source, -1.0, 1.0)
            sink_allocation = jax.nn.sigmoid(conserved_sink * (float(L) / float(S)))
            source_competition = jax.nn.softmax(conserved_source, axis=-1) * float(S)
            kv = jnp.einsum('nhld,nhlm->nhdm', k, v * source_competition[..., None])
            o = jnp.einsum('nhld,nhdm->nhlm', q * sink_incoming[..., None], kv)
            o = o * sink_allocation[..., None]
            o = o.transpose(0, 2, 1, 3).reshape(B, L, D)
            return o @ Wo + bo
        sa = _flow_attention(_layernorm(x, g1, be1), Wq, bq, Wk, bk, Wv, bv, Wo, bo)[0]
        x = x + sa
        h = _layernorm(x, g2, be2)
        h = jax.nn.gelu(h @ W1 + b1, approximate=False) @ W2 + b2
        return x + h

    def _L0_ffn_ref(x, Wr, br, W1, b1, W2, b2):
        import jax, jax.numpy as jnp
        import numpy as np
        B, T, D, F, E, K = (8, 1024, 512, 256, 8, 2)

        def _moe_forward(x, Wr, br, W1, b1, W2, b2):
            Bx, Tx, Dx = x.shape
            xf = x.reshape(-1, Dx)
            logits = xf @ Wr + br
            probs = jax.nn.softmax(logits, axis=-1)
            vals, idx = jax.lax.top_k(probs, K)
            cw = (jax.nn.one_hot(idx, E, dtype=x.dtype) * vals[..., None]).sum(axis=1)

            def body(acc, params):
                W1e, b1e, W2e, b2e, cwe = params
                h = jax.nn.relu(xf @ W1e + b1e)
                y = h @ W2e + b2e
                return (acc + cwe[:, None] * y, None)
            out, _ = jax.lax.scan(body, jnp.zeros_like(xf), (W1, b1, W2, b2, cw.T))
            return out.reshape(Bx, Tx, Dx)
        return _moe_forward(x, Wr, br, W1, b1, W2, b2)
    edge_index = jnp.stack([src, dst])
    xn = _layernorm(x, axis=-1)
    x = x + _L0_gnn_ref(xn, edge_index, L0_gnn_self_w, L0_gnn_self_b, L0_gnn_neigh_w, L0_gnn_neigh_b) + _L0_mix_ref(xn[None], L0_mix_Wq, L0_mix_bq, L0_mix_Wk, L0_mix_bk, L0_mix_Wv, L0_mix_bv, L0_mix_Wo, L0_mix_bo, L0_mix_W1, L0_mix_b1, L0_mix_W2, L0_mix_b2, L0_mix_g1, L0_mix_be1, L0_mix_g2, L0_mix_be2)[0]
    x = x + _L0_ffn_ref(_layernorm(x, axis=-1)[None], L0_ffn_Wr, L0_ffn_br, L0_ffn_W1, L0_ffn_b1, L0_ffn_W2, L0_ffn_b2)[0]
    return x

_drawn_inputs = setup_inputs


def setup_inputs(seed=0):
    import zlib

    import numpy as np

    out = dict(_drawn_inputs(seed))
    spreads = {'L0_mix_bq': (0.0, 2.0),
     'L0_mix_bk': (0.0, 2.0),
     'L0_mix_bv': (0.0, 0.605),
     'L0_mix_bo': (0.0, 0.361),
     'L0_mix_b1': (0.0, 0.8),
     'L0_mix_b2': (0.0, 0.372),
     'L0_mix_g1': (1.0, 0.6),
     'L0_mix_be1': (0.0, 0.8),
     'L0_mix_g2': (1.0, 0.6),
     'L0_mix_be2': (0.0, 2.0),
     'L0_ffn_br': (0.0, 0.533),
     'L0_ffn_b1': (0.0, 2.0),
     'L0_ffn_b2': (0.0, 0.636)}
    factors = {'L0_gnn_self_b': 8.0,
     'L0_gnn_neigh_b': 7.76,
     'L0_mix_Wq': 8.0,
     'L0_mix_Wk': 8.0,
     'L0_mix_Wv': 8.0,
     'L0_mix_Wo': 3.988,
     'L0_ffn_W1': 3.16}
    for name, (base, spread) in spreads.items():
        noise = np.random.default_rng([zlib.crc32(name.encode()), seed]).standard_normal(out[name].shape)
        drawn = base * np.exp(spread * noise) if base else spread * noise
        out[name] = jnp.asarray(drawn.astype(out[name].dtype))
    for name, factor in factors.items():
        out[name] = (out[name] * factor).astype(out[name].dtype)
    return out
```

```python
from contextlib import ExitStack

import concourse.bass as bass
from concourse import mybir

F32 = mybir.dt.float32
F32R = mybir.dt.float32r
I32 = mybir.dt.int32
U32 = mybir.dt.uint32
ALU = mybir.AluOpType
ACT = mybir.ActivationFunctionType
AX = mybir.AxisListType

P = 128
EPS_LN = 1e-5
EPS_FLOW = 1e-6


class Flow:

    def __init__(self, sem, n=1):
        self.sem, self.n, self.credit = sem, n, 2 * n

    def after(self, t, k=None):
        return self.n * t + self.credit + (self.n if k is None else k)

    def freed(self, t):
        return self.n * t + self.n


class Transfers:

    def __init__(self, sems, k=1, credit=1):
        self.sems, self.k = sems, k
        self.credit = 16 * k * credit

    def after(self, t, s):
        return 8 * self.k * (t - s) + 16 * self.k + self.credit

    def freed(self, t, s):
        return 8 * self.k * (t - s) + self.credit


def give_credit(eng, flows):
    for f in flows:
        for sem in (f.sems if isinstance(f, Transfers) else [f.sem]):
            if f.credit:
                eng.sem_inc(sem, f.credit)


def stages(eng, tiles, *parts, first=0):
    low, high = min(a for a, _ in parts), max(a for a, _ in parts)

    def turn(t, parity):
        for ahead, step in parts:
            if not isinstance(t, int) or first <= t + ahead < tiles:
                step(t + ahead, (parity + ahead) % 2)

    start = first - low
    looped = max(0, (tiles - 1 - high - start) // 2 * 2)
    for t in range(first - high, start):
        turn(t, t % 2)
    with eng.Fori(start, start + looped - 1, 2) as i:
        turn(i, start % 2)
        turn(i + 1, (start + 1) % 2)
    for t in range(start + looped, tiles - low):
        turn(t, t % 2)


def gps_layer_kernel(nc, x, src, dst, self_wT, self_b, neigh_wT, neigh_b, Wq, bq, Wk, bk, Wv, bv, Wo, bo,
                     W1, b1, W2, b2, g1, be1, g2, be2, Wr, br, E1, e1b, E2, e2b, out):
    N, D = x.shape
    EDGES = src.shape[0]
    TILES = (N + P - 1) // P
    NP = TILES * P
    TAIL = N - (TILES - 1) * P
    C = D // P
    H = 8
    DH = D // H
    HID = W1.shape[1]
    HC = HID // P
    EXPERTS = E1.shape[0]
    EP = 125
    EJ = EDGES // EP
    PAIR = 2 * P
    PAIRS = (EDGES - TILES) // PAIR + TILES + 1
    PAIRS += -PAIRS % 4
    ETILES = 2 * PAIRS
    NOROW = 200
    assert EP * EJ == EDGES and TILES % 2 == 1 and PAIRS % 4 == 0

    def rows_of(t):
        return TAIL if isinstance(t, int) and t == TILES - 1 else P

    def tile_rows(d, t, rows=P):
        return d[bass.ds(t * P, rows), :]

    def dram(name, shape, dt=F32):
        return nc.dram_tensor(name, shape, dt, kind="Internal").ap()

    xn_d = dram("xn_d", [NP, D])
    self_d = dram("self_d", [NP, D])
    y_d = dram("y_d", [NP, D])
    q_d = dram("q_d", [NP, D])
    k_d = dram("k_d", [NP, D])
    v_d = dram("v_d", [NP, D])
    qs_d = dram("qs_d", [NP, D])
    x1_d = dram("x1_d", [NP, D])
    rec_d = dram("rec_d", [ETILES * P, 2], I32)

    top = ExitStack()

    live = []

    def sem(name):
        live.append(nc.alloc_semaphore(name=name))
        return live[-1]

    def clear_semaphores():
        with nc.Block() as block:

            @block.gpsimd
            def _(e):
                nc.clear_and_free_semaphores(live)
        live.clear()

    def flow(name, n=1):
        return Flow(sem(name), n)

    def transfers(name, k=1, credit=1):
        return Transfers([sem(f"{name}{s}") for s in range(2)], k, credit)

    class Scope:
        def __init__(self):
            self.stack = ExitStack()

        def sb(self, name, shape, dt=F32):
            return self.stack.enter_context(nc.sbuf_tensor(name, shape, dt))

        def ps(self, name, shape, dt=F32):
            return self.stack.enter_context(nc.psum_tensor(name, shape, dt))

        def two(self, name, shape, dt=F32):
            return [self.sb(f"{name}{s}", shape, dt) for s in range(2)]

        def close(self):
            self.stack.close()

    def split_products(eng, bank, hi, lo, whi, wlo, n):
        last = None
        for c in range(n):
            for a, b in ((hi, whi), (hi, wlo), (lo, whi)):
                last = eng.matmul(bank, a[:, c, :], b[:, c, :], start=(c == 0 and a is hi and b is whi),
                                  stop=(c == n - 1 and a is lo))
        return last

    def scatter_edges(e, first, turns, scat, f_slot):

        def scatter(t, s):
            if not (isinstance(t, int) and t < 2):
                e.wait_ge(scat.sems[s], scat.freed(t, s))
            column = bass.ds(SCAT * (t + first), SCAT)
            e.tensor_copy(to8[s][0:EP, :], place_i[0:EP, column]).then_inc(f_slot.sem, 1)
            e.tensor_copy(rec8[s][0:EP, :], records[0:EP, column, :].rearrange("p j w -> p (j w)"))\
                .then_inc(f_slot.sem, 1)
            e.wait_ge(f_slot.sem, f_slot.after(t))
            e.tensor_tensor(pace[:, 1:2], zeros[:, 0:1], zeros[:, 1:2], ALU.add)
            for j in range(SCAT):
                e.indirect_dma_start(rec_d, bass.IndirectOffsetOnAxis(to8[s][0:EP, j:j + 1], 0),
                                     rec8[s][0:EP, 2 * j:2 * j + 2], None).then_inc(scat.sems[s], 16)

        scatter(0, 0)
        scatter(1, 1)
        stages(e, turns, (0, scatter), first=2)
        for s in range(2):
            e.wait_ge(scat.sems[s], scat.after(turns - 1 - s, (turns - 1 - s) % 2))

    with top:
        G = Scope()
        Held = Scope()
        SCAT = 8
        SCAT_TURNS = EJ // SCAT
        SCAT_FIRST = 76
        ident = G.sb("ident", [P, P])
        ones = G.sb("ones", [P, P])
        zeros = G.sb("zeros", [P, D])
        consts = G.sb("consts", [P, 4])
        eps_c, mhalf = consts[:, 0:1], consts[:, 1:2]
        pace = G.sb("pace", [P, 2])
        block_mask = G.sb("block_mask", [P, P])
        qsum = G.sb("qsum", [P, D])
        ksum = G.sb("ksum", [P, D])
        rs_all = G.sb("rs_all", [P, TILES])
        mean_all = G.sb("mean_all", [P, TILES])
        r2_all = G.sb("r2_all", [P, TILES])
        bucket_of_pair = G.sb("bucket_of_pair", [1, PAIRS], I32)

        place_i = Held.sb("place_i", [P, EJ], I32)
        records = Held.sb("records", [P, EJ, 2], I32)
        to8 = Held.two("to8", [P, SCAT], I32)
        rec8 = Held.two("rec8", [P, 2 * SCAT], I32)

        A = Scope()
        names = ("neigh", "self", "q", "k", "v")
        whi = {n: A.sb(f"whi_{n}", [P, C, D], F32R) for n in names}
        wlo = {n: A.sb(f"wlo_{n}", [P, C, D], F32R) for n in names}
        bias_all = A.sb("bias_all", [P, 4, D])
        bucket = A.sb("bucket", [P, EJ])
        bucket_ids = A.sb("bucket_ids", [P, TILES])
        ones_e = A.sb("ones_e", [P, EJ])
        counts = A.sb("counts", [P, TILES])
        base = A.sb("base", [P, TILES])
        S = Scope()
        raw = [S.sb(f"raw{s}", [P, C, D]) for s in range(2)]
        gcol = S.sb("gcol", [P, C])
        bcol = S.sb("bcol", [P, C])
        be_wide = S.sb("be_wide", [P, C, P])
        brow = S.sb("brow", [1, 5, D])
        rec_pad = S.sb("rec_pad", [P, ETILES, 2], I32)
        srcs = S.sb("srcs", [P, EJ], I32)
        dsts = S.sb("dsts", [P, EJ], I32)
        high = S.sb("high", [P, EJ], I32)
        pos = S.sb("pos", [P, EJ])
        rmatch = S.sb("rmatch", [P, EJ])
        rank = S.sb("rank", [P, EJ])
        placed = S.two("placed", [P, EJ])
        XG = 4
        x_turns = TILES // XG
        xs = S.two("xs", [P, XG, D])
        stats = S.sb("stats", [P, TILES, 6])
        st_a = S.sb("st_a", [P, TILES])
        st_b = S.sb("st_b", [P, TILES])
        match = S.sb("match", [P, EJ])
        upper = S.sb("upper", [P, P])
        upper_incl = S.sb("upper_incl", [P, P])
        pair_no = S.sb("pair_no", [P, PAIRS])
        padded = S.sb("padded", [P, TILES])
        padded_i = S.sb("padded_i", [P, TILES], I32)
        ends = S.sb("ends", [P, TILES])
        pad_col = S.sb("pad_col", [P, 1])
        pad_col_i = S.sb("pad_col_i", [P, 1], I32)
        end_col = S.sb("end_col", [P, 1])
        past = S.sb("past", [P, PAIRS])
        ps_bias = S.ps("ps_bias", [P, 4, D])
        ps_e = S.ps("ps_e", [P, D])
        ps_e2 = S.ps("ps_e2", [P, D])

        s_cons = sem("s_cons")
        s_consd = sem("s_consd")
        s_raw = [sem(f"s_raw{s}") for s in range(2)]
        s_small = sem("s_small")
        s_src = sem("s_src")
        s_pad = sem("s_pad")
        s_padout = sem("s_padout")
        s_wide = sem("s_wide")
        s_biasmm = sem("s_biasmm")
        s_hi = sem("s_hi")
        s_lo = sem("s_lo")
        s_biasv = sem("s_biasv")
        s_edge = sem("s_edge")
        s_count = sem("s_count")
        s_emm = sem("s_emm")
        s_stat = sem("s_stat")
        s_pow = sem("s_pow")
        s_rec = sem("s_rec")
        xs_in = transfers("xs_in")
        f_xs = flow("f_xs", XG)
        f_rank = flow("f_rank", 3)
        f_pos = flow("f_pos")
        weights = {"neigh": neigh_wT, "self": self_wT, "q": Wq, "k": Wk, "v": Wv}
        folded = {"neigh": False, "self": False, "q": True, "k": True, "v": True}

        with nc.Block() as block:

            @block.sync
            def _(e):
                give_credit(e, [xs_in, f_xs, f_rank, f_pos])
                e.dma_start(srcs[0:EP, :], src.rearrange("(p j) -> p j", p=EP)).then_inc(s_src, 16)
                e.dma_start(dsts[0:EP, :], dst.rearrange("(p j) -> p j", p=EP)).then_inc(s_src, 16)
                e.dma_start(gcol[:, :], g1).then_inc(s_small, 16)
                e.dma_start(bcol[:, :], be1).then_inc(s_small, 16)
                for i, b in enumerate((self_b, neigh_b, bq, bk, bv)):
                    e.dma_start(brow[:, i, :], b.rearrange("(a n) -> a n", a=1)).then_inc(s_small, 16)

                def load_x(t, s):
                    e.wait_ge(f_xs.sem, f_xs.freed(t))
                    e.dma_start(xs[s][:, :, :], x[bass.ds(XG * P * t, XG * P), :]
                                .rearrange("(g p) d -> p g d", p=P)).then_inc(xs_in.sems[s], 16)

                stages(e, x_turns, (0, load_x))
                e.wait_ge(f_xs.sem, f_xs.freed(x_turns))
                e.dma_start(xs[x_turns % 2][0:TAIL, 0, :], x[(TILES - 1) * P:N, :])\
                    .then_inc(xs_in.sems[x_turns % 2], 16)
                for i, n in enumerate(names):
                    if i >= 2:
                        e.wait_ge(s_hi, C * (i - 1))
                        e.wait_ge(s_lo, C * (i - 1))
                    if i == 4:
                        e.wait_ge(s_biasmm, 2)
                    e.dma_start(raw[i % 2][:, :, :], weights[n].rearrange("(c p) n -> p c n", p=P))\
                        .then_inc(s_raw[i % 2], 16)
                e.wait_ge(s_pad, 2)
                e.dma_start(rec_d.rearrange("(p t) w -> p (t w)", p=P),
                            rec_pad[:, :, :].rearrange("p t w -> p (t w)")).then_inc(s_padout, 16)
                e.wait_ge(s_padout, 16)

            @block.gpsimd
            def _(e):
                e.memset(ones[:, :], 1.0).then_inc(s_cons, 1)
                e.memset(ident[:, :], 0.0).then_inc(s_cons, 1)
                e.memset(zeros[:, :], 0.0).then_inc(s_cons, 1)
                e.memset(eps_c, EPS_LN).then_inc(s_cons, 1)
                e.memset(mhalf, -0.5).then_inc(s_cons, 1)
                e.memset(pace[:, :], 0.0).then_inc(s_cons, 1)
                e.memset(qsum[:, :], 0.0).then_inc(s_cons, 1)
                e.memset(ksum[:, :], 0.0).then_inc(s_cons, 1)
                e.memset(pos[:, :], 0.0).then_inc(s_cons, 1)
                e.memset(stats[:, :, :], 0.0).then_inc(s_cons, 1)
                e.memset(ones_e[:, :], 1.0).then_inc(s_cons, 1)
                e.memset(rec_pad[:, :, 0], 0).then_inc(s_pad, 1)
                e.memset(rec_pad[:, :, 1], NOROW).then_inc(s_pad, 1)
                e.iota(bucket_ids[:, :], pattern=[[1, TILES]], base=0, channel_multiplier=0,
                       allow_small_or_imprecise_dtypes=True).then_inc(s_cons, 1)
                e.iota(pair_no[:, :], pattern=[[1, PAIRS]], base=0, channel_multiplier=0,
                       allow_small_or_imprecise_dtypes=True).then_inc(s_cons, 1)
                e.wait_ge(s_cons, 13)
                e.affine_select(out=ident[:, :], in_=ident[:, :], compare_op=ALU.not_equal, fill=1.0, base=0,
                                pattern=[[-1, P]], channel_multiplier=1).then_inc(s_consd, 1)
                e.affine_select(out=upper[:, :], in_=ones[:, :], compare_op=ALU.is_gt, fill=0.0, base=0,
                                pattern=[[1, P]], channel_multiplier=-1).then_inc(s_consd, 1)
                e.affine_select(out=upper_incl[:, :], in_=ones[:, :], compare_op=ALU.is_ge, fill=0.0, base=0,
                                pattern=[[1, P]], channel_multiplier=-1).then_inc(s_consd, 1)
                ops = ((st_b, st_a, eps_c, ALU.add), (rs_all, st_b, mhalf, ALU.pow),
                       (st_b, st_a, rs_all, ALU.mult), (st_b, st_b, rs_all, ALU.mult),
                       (st_b, st_b, eps_c, ALU.add), (r2_all, st_b, mhalf, ALU.pow))
                e.wait_ge(s_stat, 7)
                for k, (o, a, b, op) in enumerate(ops):
                    b = b.broadcast_to([P, TILES]) if b is eps_c or b is mhalf else b[:, :]
                    e.tensor_tensor(o[:, :], a[:, :], b, op).then_inc(s_pow, 1)
                    e.wait_ge(s_pow, k + 1)

                def add_places(t, s):
                    e.wait_ge(f_pos.sem, f_pos.after(t - 1))
                    e.wait_ge(f_rank.sem, f_rank.after(t, 3))
                    e.tensor_tensor(pos[0:EP, :], pos[0:EP, :], placed[s][0:EP, :], ALU.add)\
                        .then_inc(f_pos.sem, 1)

                stages(e, TILES, (0, add_places))

            @block.tensor
            def _(e):
                e.wait_ge(s_consd, 3)
                e.wait_ge(s_small, 16 * 7)
                e.wait_ge(s_wide, C)
                e.matmul(ps_bias[:, 0, :], ones[0:1, :], brow[:, 0, :], start=True, stop=False)
                e.matmul(ps_bias[:, 0, :], ones[0:1, :], brow[:, 1, :], start=False, stop=True)
                for i in range(2, 5):
                    e.wait_ge(s_raw[i % 2], 16 * (i // 2 + 1))
                    e.matmul(ps_bias[:, i - 1, :], ones[0:1, :], brow[:, i, :], start=True, stop=False)
                    for c in range(C):
                        mm = e.matmul(ps_bias[:, i - 1, :], be_wide[:, c, :], raw[i % 2][:, c, :], start=False,
                                      stop=(c == C - 1))
                    mm.then_inc(s_biasmm, 2)
                e.wait_ge(s_count, TILES + 1)
                e.matmul(ps_e[:, 0:TILES], upper[0:EP, :], counts[0:EP, :], start=True, stop=True)
                e.matmul(ps_e[:, 64:64 + TILES], ones[0:EP, :], counts[0:EP, :], start=True, stop=True)
                e.matmul(ps_e[0:TILES, 128:129], counts[0:EP, :], ones[0:EP, 0:1], start=True, stop=True)\
                    .then_inc(s_emm, 1)
                e.wait_ge(s_edge, 8)
                e.matmul(ps_e2[0:TILES, 0:1], upper_incl[0:TILES, 0:TILES], pad_col[0:TILES, :], start=True,
                         stop=True).then_inc(s_emm, 1)
                e.wait_ge(s_edge, 11)
                e.matmul(ps_e2[0:1, 0:PAIRS], ones[0:TILES, 0:1], past[0:TILES, :], start=True, stop=True)\
                    .then_inc(s_emm, 1)

            @block.scalar
            def _(e):
                e.wait_ge(s_small, 16 * 7)
                for i, n in enumerate(names):
                    e.wait_ge(s_raw[i % 2], 16 * (i // 2 + 1))
                    for c in range(C):
                        e.activation(whi[n][:, c, :], raw[i % 2][:, c, :], ACT.Copy,
                                     scale=gcol[:, c:c + 1] if folded[n] else 1.0).then_inc(s_hi, 1)

            @block.vector
            def _(e):
                for h in range(P // DH):
                    for g in range(P // DH):
                        e.memset(block_mask[h * DH:(h + 1) * DH, g * DH:(g + 1) * DH], float(h == g))
                e.wait_ge(s_small, 16 * 7)
                e.wait_ge(s_cons, 13)
                for c in range(C):
                    e.tensor_scalar(be_wide[:, c, :], ones[:, :], bcol[:, c:c + 1], None, ALU.mult)\
                        .then_inc(s_wide, 1)
                e.wait_ge(s_src, 32)
                e.tensor_scalar(high[0:EP, :], srcs[0:EP, :], 7, None, ALU.logical_shift_right)\
                    .then_inc(s_edge, 1)
                e.wait_ge(s_edge, 1)
                e.tensor_copy(bucket[0:EP, :], high[0:EP, :]).then_inc(s_edge, 1)
                e.wait_ge(s_edge, 2)
                e.memset(match[0:EP, :], 0.0).then_inc(s_count, 1)
                with e.Fori(0, TILES, 1) as b:
                    e.wait_ge(s_count, b + 1)
                    e.tensor_scalar(match[0:EP, :], bucket[0:EP, :], bucket_ids[0:EP, bass.ds(b, 1)], 0.0,
                                    ALU.is_equal, ALU.add, accum_out=counts[0:EP, bass.ds(b, 1)])\
                        .then_inc(s_count, 1)

                def statistics(t, s):
                    e.wait_ge(xs_in.sems[s], xs_in.after(t, s))
                    for g in range(XG):
                        e.bn_stats(stats[:, bass.ds(XG * t + g, 1), :].rearrange("p t k -> p (t k)"),
                                   xs[s][:, g, :]).then_inc(f_xs.sem, 1)

                stages(e, x_turns, (0, statistics))
                e.wait_ge(xs_in.sems[x_turns % 2], xs_in.after(x_turns, x_turns % 2))
                e.bn_stats(stats[0:TAIL, TILES - 1, :], xs[x_turns % 2][0:TAIL, 0, :]).then_inc(f_xs.sem, 1)
                e.wait_ge(f_xs.sem, f_xs.after(x_turns - 1) + 1)
                me, mo = stats[:, :, 1], stats[:, :, 4]
                e.tensor_tensor(mean_all[:, :], me, mo, ALU.add).then_inc(s_stat, 1)
                e.tensor_tensor(st_b[:, :], me, mo, ALU.subtract).then_inc(s_stat, 1)
                e.tensor_tensor(st_a[:, :], stats[:, :, 2], stats[:, :, 5], ALU.add).then_inc(s_stat, 1)
                e.wait_ge(s_stat, 3)
                e.tensor_scalar(mean_all[:, :], mean_all[:, :], 0.5, None, ALU.mult).then_inc(s_stat, 1)
                e.scalar_tensor_tensor(out=st_b[:, :], in0=st_b[:, :], scalar=D / 4.0, in1=st_b[:, :],
                                       op0=ALU.mult, op1=ALU.mult).then_inc(s_stat, 1)
                e.wait_ge(s_stat, 5)
                e.tensor_tensor(st_a[:, :], st_a[:, :], st_b[:, :], ALU.add).then_inc(s_stat, 1)
                e.wait_ge(s_stat, 6)
                e.tensor_scalar(st_a[:, :], st_a[:, :], 1.0 / D, None, ALU.mult).then_inc(s_stat, 1)
                for i, n in enumerate(names):
                    for c in range(C):
                        e.wait_ge(s_hi, C * i + c + 1)
                        e.scalar_tensor_tensor(out=wlo[n][:, c, :], in0=raw[i % 2][:, c, :],
                                               scalar=gcol[:, c:c + 1] if folded[n] else 1.0,
                                               in1=whi[n][:, c, :].bitcast(F32), op0=ALU.mult,
                                               op1=ALU.subtract).then_inc(s_lo, 1)
                e.wait_ge(s_emm, 1)
                e.tensor_scalar(padded_i[:, :], ps_e[:, 64:64 + TILES], float(PAIR - 1), None, ALU.add)\
                    .then_inc(s_edge, 1)
                e.tensor_scalar(pad_col_i[0:TILES, :], ps_e[0:TILES, 128:129], float(PAIR - 1), None, ALU.add)\
                    .then_inc(s_edge, 1)
                e.wait_ge(s_edge, 4)
                e.tensor_scalar(padded_i[:, :], padded_i[:, :], 8, 8, ALU.logical_shift_right,
                                ALU.logical_shift_left).then_inc(s_edge, 1)
                e.tensor_scalar(pad_col_i[0:TILES, :], pad_col_i[0:TILES, :], 8, None,
                                ALU.logical_shift_right).then_inc(s_edge, 1)
                e.wait_ge(s_edge, 6)
                e.tensor_copy(padded[:, :], padded_i[:, :]).then_inc(s_edge, 1)
                e.tensor_copy(pad_col[0:TILES, :], pad_col_i[0:TILES, :]).then_inc(s_edge, 1)
                e.wait_ge(s_edge, 8)
                e.tensor_tensor_scan(ends[:, :], ones_e[:, 0:TILES], padded[:, :], 0.0, ALU.mult, ALU.add)\
                    .then_inc(s_edge, 1)
                e.wait_ge(s_emm, 2)
                e.tensor_copy(end_col[0:TILES, :], ps_e2[0:TILES, 0:1]).then_inc(s_edge, 1)
                e.wait_ge(s_edge, 10)
                e.tensor_scalar(past[0:TILES, :], pair_no[0:TILES, :], end_col[0:TILES, :], None, ALU.is_ge)\
                    .then_inc(s_edge, 1)
                e.tensor_tensor(ends[:, :], ends[:, :], padded[:, :], ALU.subtract).then_inc(s_edge, 1)
                e.wait_ge(s_edge, 12)
                e.tensor_tensor(base[:, :], ps_e[:, 0:TILES], ends[:, :], ALU.add).then_inc(s_edge, 1)
                e.wait_ge(s_emm, 3)
                e.tensor_scalar(bucket_of_pair[:, :], ps_e2[0:1, 0:PAIRS], float(TILES - 1), None, ALU.min)\
                    .then_inc(s_edge, 1)

                def rank_bucket(t, s):
                    e.wait_ge(f_rank.sem, f_rank.after(t - 1))
                    e.tensor_scalar(rmatch[0:EP, :], bucket[0:EP, :], bucket_ids[0:EP, bass.ds(t, 1)], None,
                                    ALU.is_equal).then_inc(f_rank.sem, 1)
                    e.wait_ge(f_rank.sem, f_rank.after(t, 1))
                    e.tensor_tensor_scan(rank[0:EP, :], ones_e[0:EP, :], rmatch[0:EP, :],
                                         base[0:EP, bass.ds(t, 1)], ALU.mult, ALU.add).then_inc(f_rank.sem, 1)
                    e.wait_ge(f_rank.sem, f_rank.after(t, 2))
                    e.wait_ge(f_pos.sem, f_pos.freed(t))
                    e.tensor_tensor(placed[s][0:EP, :], rank[0:EP, :], rmatch[0:EP, :], ALU.mult)\
                        .then_inc(f_rank.sem, 1)

                e.wait_ge(s_edge, 14)
                stages(e, TILES, (0, rank_bucket))
                e.wait_ge(f_pos.sem, f_pos.after(TILES - 1))
                e.tensor_scalar(place_i[0:EP, :], pos[0:EP, :], -1.0, None, ALU.add).then_inc(s_rec, 1)
                e.tensor_scalar(records[0:EP, :, 1], srcs[0:EP, :], P - 1, None, ALU.bitwise_and)\
                    .then_inc(s_rec, 1)
                e.tensor_copy(records[0:EP, :, 0], dsts[0:EP, :]).then_inc(s_rec, 1)
                e.wait_ge(s_rec, 3)
                e.tensor_scalar(high[0:EP, :], place_i[0:EP, :], 7, None, ALU.logical_shift_right)\
                    .then_inc(s_rec, 1)
                e.tensor_scalar(place_i[0:EP, :], place_i[0:EP, :], P - 1, None, ALU.bitwise_and)\
                    .then_inc(s_rec, 1)
                e.wait_ge(s_rec, 5)
                e.scalar_tensor_tensor(out=place_i[0:EP, :], in0=place_i[0:EP, :], scalar=float(ETILES),
                                       in1=high[0:EP, :], op0=ALU.mult, op1=ALU.add).then_inc(s_rec, 1)
                e.wait_ge(s_biasmm, 6)
                e.tensor_copy(bias_all[:, :, :], ps_bias[:, :, :]).then_inc(s_biasv, 1)
        S.close()

        B = Scope()
        X = B.two("X", [P, D])
        XN = B.two("XN", [P, D])
        XH = B.two("XH", [P, C, P], F32R)
        XL = B.two("XL", [P, C, P], F32R)
        SO = B.two("SO", [P, D])
        YO = B.two("YO", [P, D])
        QT = B.two("QT", [P, D])
        KT = B.two("KT", [P, D])
        Q = B.two("Q", [P, D])
        K = B.two("K", [P, D])
        V = B.two("V", [P, D])
        PT = [B.ps(f"PT{s}", [P, C, P]) for s in range(2)]
        PB = {n: B.ps(f"PB_{n}", [P, D]) for n in names}

        x_in = transfers("x_in")
        xn_out = transfers("xn_out")
        outs = {n: transfers(f"o_{n}") for n in names}
        f_xn = flow("f_xn")
        f_pt = flow("f_pt")
        f_hi = flow("f_hi")
        f_lo = flow("f_lo")
        f_prod = flow("f_prod", 5)
        f_pre = flow("f_pre", 2)
        f_made = {n: flow(f"f_made_{n}") for n in names}
        f_acc = flow("f_acc", 2)
        f_slot = flow("f_slot", 2)
        scat = transfers("scat", SCAT, credit=0)
        flows = [x_in, xn_out, *outs.values(), f_xn, f_pt, f_hi, f_lo, f_prod, f_pre,
                 *f_made.values(), f_acc, f_slot, scat]
        made_in = {"neigh": YO, "self": SO, "q": Q, "k": K, "v": V}
        stored = {"neigh": y_d, "self": self_d, "q": q_d, "k": k_d, "v": v_d}

        with nc.Block() as block:

            @block.sync
            def _(e):
                give_credit(e, flows)

                def front(t, s):
                    rows = rows_of(t)
                    e.wait_ge(f_xn.sem, f_xn.freed(t))
                    e.dma_start(X[s][0:rows, :], tile_rows(x, t, rows)).then_inc(x_in.sems[s], 16)

                def back(t, s):
                    e.wait_ge(f_xn.sem, f_xn.after(t))
                    e.dma_start(tile_rows(xn_d, t), XN[s][:, :]).then_inc(xn_out.sems[s], 16)
                    for n in names:
                        e.wait_ge(f_made[n].sem, f_made[n].after(t))
                        e.dma_start(tile_rows(stored[n], t), made_in[n][s][:, :]).then_inc(outs[n].sems[s], 16)

                stages(e, TILES, (2, front), (0, back))
                for f in (xn_out, *outs.values()):
                    for s in range(2):
                        e.wait_ge(f.sems[s], f.after(TILES - 1 - s, (TILES - 1 - s) % 2))

            @block.vector
            def _(e):
                def front(t, s):
                    e.wait_ge(x_in.sems[s], x_in.after(t, s))
                    e.wait_ge(xn_out.sems[s], xn_out.freed(t, s))
                    e.tensor_scalar(XN[s][:, :], X[s][:, :], mean_all[:, bass.ds(t, 1)], rs_all[:, bass.ds(t, 1)], ALU.subtract,
                                    ALU.mult).then_inc(f_xn.sem, 1)
                    e.wait_ge(f_pt.sem, f_pt.after(t))
                    e.wait_ge(f_hi.sem, f_hi.after(t))
                    e.tensor_tensor(XL[s][:, :, :], PT[s][:, :, :], XH[s][:, :, :].bitcast(F32), ALU.subtract)\
                        .then_inc(f_lo.sem, 1)

                def back(t, s):
                    e.wait_ge(f_prod.sem, f_prod.after(t, 2))
                    e.wait_ge(outs["self"].sems[s], outs["self"].freed(t, s))
                    e.tensor_tensor(SO[s][:, :], PB["self"][:, :], bias_all[:, 0, :], ALU.add)\
                        .then_inc(f_made["self"].sem, 1)
                    for k, (n, to, fr) in enumerate((("q", QT, f_made["q"]), ("k", KT, f_made["k"]))):
                        e.wait_ge(f_prod.sem, f_prod.after(t, 3 + k))
                        e.wait_ge(fr.sem, fr.freed(t))
                        e.scalar_tensor_tensor(out=to[s][:, :], in0=PB[n][:, :], scalar=r2_all[:, bass.ds(t, 1)],
                                               in1=bias_all[:, 1 + k, :], op0=ALU.mult, op1=ALU.add)\
                            .then_inc(f_pre.sem, 1)
                    e.wait_ge(f_prod.sem, f_prod.after(t, 5))
                    e.wait_ge(outs["v"].sems[s], outs["v"].freed(t, s))
                    e.scalar_tensor_tensor(out=V[s][:, :], in0=PB["v"][:, :], scalar=r2_all[:, bass.ds(t, 1)],
                                           in1=bias_all[:, 3, :], op0=ALU.mult, op1=ALU.add)\
                        .then_inc(f_made["v"].sem, 1)

                def sums(t, s):
                    rows = rows_of(t)
                    e.wait_ge(f_acc.sem, f_acc.after(t - 1))
                    e.wait_ge(f_made["q"].sem, f_made["q"].after(t))
                    e.tensor_tensor(qsum[0:rows, :], qsum[0:rows, :], Q[s][0:rows, :], ALU.add)\
                        .then_inc(f_acc.sem, 1)
                    e.wait_ge(f_made["k"].sem, f_made["k"].after(t))
                    e.tensor_tensor(ksum[0:rows, :], ksum[0:rows, :], K[s][0:rows, :], ALU.add)\
                        .then_inc(f_acc.sem, 1)

                stages(e, TILES, (1, front), (-1, sums), (0, back))

            @block.gpsimd
            def _(e):
                scatter_edges(e, 0, SCAT_FIRST, scat, f_slot)

            @block.tensor
            def _(e):
                def front(t, s):
                    e.wait_ge(f_xn.sem, f_xn.after(t))
                    e.wait_ge(f_lo.sem, f_lo.freed(t))
                    for c in range(C):
                        mm = e.transpose(PT[s][:, c, :], XN[s][:, c * P:(c + 1) * P], ident[:, :])
                    mm.then_inc(f_pt.sem, 1)

                def back(t, s):
                    e.wait_ge(f_lo.sem, f_lo.after(t))
                    for n in names:
                        ready = {"q": (f_pre, 1), "k": (f_pre, 2)}.get(n, (f_made[n], 1))
                        e.wait_ge(ready[0].sem, ready[0].after(t - 1, ready[1]))
                        split_products(e, PB[n][:, :], XH[s], XL[s], whi[n], wlo[n], C).then_inc(f_prod.sem, 1)

                stages(e, TILES, (1, front), (0, back))

            @block.scalar
            def _(e):
                def front(t, s):
                    e.wait_ge(f_pt.sem, f_pt.after(t))
                    e.wait_ge(f_prod.sem, f_prod.freed(t))
                    e.activation(XH[s][:, :, :], PT[s][:, :, :], ACT.Copy).then_inc(f_hi.sem, 1)

                def back(t, s):
                    e.wait_ge(f_prod.sem, f_prod.after(t, 1))
                    e.wait_ge(outs["neigh"].sems[s], outs["neigh"].freed(t, s))
                    e.activation(YO[s][:, :], PB["neigh"][:, :], ACT.Copy).then_inc(f_made["neigh"].sem, 1)
                    for k, (n, fr, to) in enumerate((("q", QT, Q), ("k", KT, K))):
                        e.wait_ge(f_pre.sem, f_pre.after(t, k + 1))
                        e.wait_ge(outs[n].sems[s], outs[n].freed(t, s))
                        e.wait_ge(f_acc.sem, f_acc.freed(t))
                        e.activation(to[s][:, :], fr[s][:, :], ACT.Sigmoid).then_inc(f_made[n].sem, 1)

                stages(e, TILES, (1, front), (0, back))
        B.close()
        A.close()
        clear_semaphores()

        M = Scope()
        wmix_hi = M.sb("wmix_hi", [P, C, D], F32R)
        wmix_lo = M.sb("wmix_lo", [P, C, D], F32R)
        Cs = Scope()
        Q = Cs.two("Qc", [P, D])
        K = Cs.two("Kc", [P, D])
        V = Cs.two("Vc", [P, D])
        QA = Cs.two("QA", [P, D])
        KA = Cs.two("KA", [P, D])
        QS = Cs.two("QSc", [P, D])
        VE = Cs.two("VE", [P, D])
        q_row = Cs.sb("q_row", [P, D])
        k_row = Cs.sb("k_row", [P, D])
        dots = Cs.two("dots", [P, 2 * H])
        inv = Cs.two("inv", [P, 2 * H])
        si_all = Cs.sb("si_all", [P, TILES * H])
        ex = Cs.two("ex", [P, 2 * H])
        alloc = Cs.two("alloc", [P, H])
        alloc_inv = Cs.two("alloc_inv", [P, H])
        scale8 = Cs.two("scale8", [P, H])
        e_sum = Cs.sb("e_sum", [P, H])
        head_mask = Cs.sb("head_mask", [H, D])
        picked = Cs.sb("picked", [H, 2, D])
        wo_raw = Cs.sb("wo_raw", [P, C, D])
        kv_blocks = Cs.sb("kv_blocks", [P, C, P])
        e_inv = Cs.sb("e_inv", [P, H])
        PQ = Cs.ps("PQ", [P, D])
        PK = Cs.ps("PK", [P, D])
        PSI = Cs.ps("PSI", [P, D])
        PSO = Cs.ps("PSO", [P, D])
        PKV = Cs.ps("PKV", [P, C, P])
        PW = [Cs.ps(f"PW{s}", [P, D]) for s in range(2)]

        s_wo = sem("s_wo")
        s_mask = sem("s_mask")
        s_row = sem("s_row")
        s_rowmm = sem("s_rowmm")
        s_sums = sem("s_sums")
        s_kvn = sem("s_kvn")
        s_wmm = sem("s_wmm")
        s_whi = sem("s_whi")
        s_wlo = sem("s_wlo")
        f_slot = flow("f_slot_b", 2)
        scat = transfers("scat_b", SCAT, credit=0)
        q_in, k_in = transfers("q_in"), transfers("k_in")
        f_sum = flow("f_sum", 6)
        f_use = flow("f_use", 2)
        q_in3, k_in3, v_in3 = transfers("q_in3"), transfers("k_in3"), transfers("v_in3")
        qs_out = transfers("qs_out")
        f_dot = flow("f_dot", 5)
        f_exp = flow("f_exp", 2)
        f_mul = flow("f_mul", 6)
        f_kv = flow("f_kv")
        flows = [f_slot, scat, q_in, k_in, f_sum, f_use, q_in3, k_in3, v_in3, qs_out, f_dot, f_exp, f_mul, f_kv]

        with nc.Block() as block:

            @block.sync
            def _(e):
                give_credit(e, flows)

                def load_sums(t, s):
                    e.wait_ge(f_use.sem, f_use.freed(t))
                    e.dma_start(Q[s][:, :], tile_rows(q_d, t)).then_inc(q_in.sems[s], 16)
                    e.dma_start(K[s][:, :], tile_rows(k_d, t)).then_inc(k_in.sems[s], 16)

                stages(e, TILES, (0, load_sums))
                e.dma_start(wo_raw[:, :, :], Wo.rearrange("(c p) n -> p c n", p=P)).then_inc(s_wo, 16)
                e.wait_ge(f_use.sem, f_use.after(TILES - 1))

                def load_mix(t, s):
                    e.wait_ge(f_kv.sem, f_kv.freed(t))
                    e.wait_ge(f_mul.sem, f_mul.freed(t))
                    e.dma_start(Q[s][:, :], tile_rows(q_d, t)).then_inc(q_in3.sems[s], 16)
                    e.dma_start(K[s][:, :], tile_rows(k_d, t)).then_inc(k_in3.sems[s], 16)
                    e.dma_start(V[s][:, :], tile_rows(v_d, t)).then_inc(v_in3.sems[s], 16)

                def store_qs(t, s):
                    e.wait_ge(f_mul.sem, f_mul.after(t, 4))
                    e.dma_start(tile_rows(qs_d, t), QS[s][:, :]).then_inc(qs_out.sems[s], 16)

                stages(e, TILES, (1, load_mix), (0, store_qs))
                for s in range(2):
                    e.wait_ge(qs_out.sems[s], qs_out.after(TILES - 1 - s, (TILES - 1 - s) % 2))

            @block.gpsimd
            def _(e):
                e.memset(e_sum[:, :], 0.0).then_inc(s_mask, 1)
                e.memset(head_mask[:, :], 1.0).then_inc(s_mask, 1)
                e.wait_ge(s_mask, 2)
                e.affine_select(out=head_mask[:, :], in_=head_mask[:, :], compare_op=ALU.is_ge, fill=0.0, base=0,
                                pattern=[[1, D]], channel_multiplier=-DH).then_inc(s_mask, 1)
                e.wait_ge(s_mask, 3)
                e.affine_select(out=head_mask[:, :], in_=head_mask[:, :], compare_op=ALU.is_ge, fill=0.0,
                                base=DH - 1, pattern=[[-1, D]], channel_multiplier=DH).then_inc(s_mask, 1)
                scatter_edges(e, SCAT_FIRST, SCAT_TURNS - SCAT_FIRST, scat, f_slot)

            @block.tensor
            def _(e):
                e.matmul(PQ[:, :], ones[:, :], qsum[:, :], start=True, stop=True).then_inc(s_rowmm, 1)
                e.matmul(PK[:, :], ones[:, :], ksum[:, :], start=True, stop=True).then_inc(s_rowmm, 1)
                for bank in (PSI, PSO):
                    e.matmul(bank[0:H, :], zeros[:, 0:H], zeros[:, :], start=True, stop=False)

                def sums(t, s):
                    rows = rows_of(t)
                    last = isinstance(t, int) and t == TILES - 1
                    e.wait_ge(f_sum.sem, f_sum.after(t, 5))
                    e.matmul(PSI[0:H, :], inv[s][0:rows, 0:H], Q[s][0:rows, :], start=False, stop=last)\
                        .then_inc(f_use.sem, 1)
                    e.matmul(PSO[0:H, :], inv[s][0:rows, H:2 * H], K[s][0:rows, :], start=False, stop=last)\
                        .then_inc(f_use.sem, 1)

                stages(e, TILES, (0, sums))
                e.wait_ge(s_sums, 2)
                e.matmul(PQ[:, :], ones[0:H, :], picked[:, 0, :], start=True, stop=True).then_inc(s_rowmm, 1)
                e.matmul(PK[:, :], ones[0:H, :], picked[:, 1, :], start=True, stop=True).then_inc(s_rowmm, 1)
                e.matmul(PKV[:, :, :].rearrange("p c m -> p (c m)"), zeros[:, 0:P], zeros[:, :], start=True,
                         stop=False)

                def kv(t, s):
                    rows = rows_of(t)
                    e.wait_ge(f_mul.sem, f_mul.after(t, 5))
                    for c in range(C):
                        mm = e.matmul(PKV[:, c, :], VE[s][0:rows, c * P:(c + 1) * P],
                                      K[s][0:rows, c * P:(c + 1) * P], start=False, stop=False,
                                      skip_group_check=True)
                    mm.then_inc(f_kv.sem, 1)

                stages(e, TILES, (0, kv))
                e.matmul(PKV[:, :, :].rearrange("p c m -> p (c m)"), zeros[:, 0:P], zeros[:, :], start=False,
                         stop=True)
                e.wait_ge(f_mul.sem, f_mul.after(TILES - 1))
                e.matmul(PSI[:, 0:H], ones[:, :], e_sum[:, :], start=True, stop=True).then_inc(s_rowmm, 1)
                e.wait_ge(s_wo, 16)
                for c in range(C):
                    e.wait_ge(s_kvn, 2 + c + 1)
                    if c >= 2:
                        e.wait_ge(s_wlo, c - 1)
                    e.matmul(PW[c % 2][:, :], kv_blocks[:, c, :], wo_raw[:, c, :], start=True, stop=True)\
                        .then_inc(s_wmm, 1)

            @block.scalar
            def _(e):
                def exps(t, s):
                    e.wait_ge(f_dot.sem, f_dot.after(t))
                    e.activation(ex[s][:, 0:H], dots[s][:, 0:H], ACT.Exp, scale=-1.0).then_inc(f_exp.sem, 1)
                    e.activation(ex[s][:, H:2 * H], dots[s][:, H:2 * H], ACT.Exp).then_inc(f_exp.sem, 1)

                stages(e, TILES, (0, exps))
                for c in range(C):
                    e.wait_ge(s_wmm, c + 1)
                    e.activation(wmix_hi[:, c, :], PW[c % 2][:, :], ACT.Copy).then_inc(s_whi, 1)

            @block.vector
            def _(e):
                e.wait_ge(s_rowmm, 2)
                e.tensor_scalar(q_row[:, :], PQ[:, :], EPS_FLOW, None, ALU.add).then_inc(s_row, 1)
                e.tensor_scalar(k_row[:, :], PK[:, :], EPS_FLOW, None, ALU.add).then_inc(s_row, 1)
                e.wait_ge(s_row, 2)

                def heads(a):
                    return a[:, :].rearrange("p (h d) -> p h d", h=H)

                def dot(t, s, ins, f, k, row_of_q, row_of_k):
                    e.wait_ge(ins[0].sems[s], ins[0].after(t, s))
                    e.wait_ge(ins[1].sems[s], ins[1].after(t, s))
                    for a, b, row in ((QA, Q, row_of_q), (KA, K, row_of_k)):
                        e.scalar_tensor_tensor(out=a[s][:, :], in0=b[s][:, :], scalar=EPS_FLOW, in1=row[:, :],
                                               op0=ALU.add, op1=ALU.mult).then_inc(f.sem, 1)
                    for i, a in enumerate((QA, KA)):
                        e.wait_ge(f.sem, f.after(t, i + 1))
                        e.tensor_reduce(dots[s][:, i * H:(i + 1) * H], heads(a[s]), AX.X, ALU.add)\
                            .then_inc(f.sem, 1)
                    e.wait_ge(f.sem, f.after(t, 4))

                def sums(t, s):
                    dot(t, s, (q_in, k_in), f_sum, 5, k_row, q_row)
                    e.wait_ge(f_use.sem, f_use.freed(t))
                    e.reciprocal(inv[s][:, :], dots[s][:, :]).then_inc(f_sum.sem, 1)
                    e.wait_ge(f_sum.sem, f_sum.after(t, 5))
                    e.tensor_copy(si_all[:, bass.ds(H * t, H)], inv[s][:, 0:H]).then_inc(f_sum.sem, 1)

                stages(e, TILES, (0, sums))
                e.wait_ge(f_use.sem, f_use.after(TILES - 1))
                e.wait_ge(s_mask, 4)
                e.tensor_tensor(picked[:, 0, :], PSI[0:H, :], head_mask[:, :], ALU.mult).then_inc(s_sums, 1)
                e.tensor_tensor(picked[:, 1, :], PSO[0:H, :], head_mask[:, :], ALU.mult).then_inc(s_sums, 1)
                e.wait_ge(s_rowmm, 4)
                e.tensor_scalar(q_row[:, :], PQ[:, :], EPS_FLOW, None, ALU.add).then_inc(s_row, 1)
                e.tensor_scalar(k_row[:, :], PK[:, :], EPS_FLOW, None, ALU.add).then_inc(s_row, 1)
                e.wait_ge(s_row, 4)

                def dots3(t, s):
                    e.wait_ge(f_exp.sem, f_exp.freed(t))
                    dot(t, s, (q_in3, k_in3), f_dot, 5, k_row, q_row)
                    e.tensor_scalar(dots[s][:, H:2 * H], dots[s][:, H:2 * H], -1.0, 1.0, ALU.max, ALU.min)\
                        .then_inc(f_dot.sem, 1)

                def wide(a):
                    return a.unsqueeze(2).broadcast_to([P, H, DH])

                def mix(t, s):
                    rows = rows_of(t)
                    e.wait_ge(f_exp.sem, f_exp.after(t))
                    e.tensor_scalar(alloc[s][:, :], ex[s][:, 0:H], 1.0, None, ALU.add).then_inc(f_mul.sem, 1)
                    e.wait_ge(f_mul.sem, f_mul.after(t, 1))
                    e.reciprocal(alloc_inv[s][:, :], alloc[s][:, :]).then_inc(f_mul.sem, 1)
                    e.wait_ge(f_mul.sem, f_mul.after(t, 2))
                    e.tensor_tensor(scale8[s][:, :], si_all[:, bass.ds(H * t, H)], alloc_inv[s][:, :], ALU.mult)\
                        .then_inc(f_mul.sem, 1)
                    e.wait_ge(f_mul.sem, f_mul.after(t, 3))
                    e.wait_ge(qs_out.sems[s], qs_out.freed(t, s))
                    e.tensor_tensor(heads(QS[s]), heads(Q[s]), wide(scale8[s][:, :]), ALU.mult)\
                        .then_inc(f_mul.sem, 1)
                    e.wait_ge(v_in3.sems[s], v_in3.after(t, s))
                    e.wait_ge(f_kv.sem, f_kv.freed(t))
                    e.tensor_tensor(heads(VE[s]), heads(V[s]), wide(ex[s][:, H:2 * H]), ALU.mult)\
                        .then_inc(f_mul.sem, 1)
                    e.tensor_tensor(e_sum[0:rows, :], e_sum[0:rows, :], ex[s][0:rows, H:2 * H], ALU.add)\
                        .then_inc(f_mul.sem, 1)

                stages(e, TILES, (1, dots3), (0, mix))
                e.wait_ge(s_rowmm, 5)
                e.reciprocal(e_inv[:, :], PSI[:, 0:H]).then_inc(s_kvn, 1)
                e.wait_ge(s_kvn, 1)
                e.tensor_scalar(e_inv[:, :], e_inv[:, :], float(N), None, ALU.mult).then_inc(s_kvn, 1)
                e.wait_ge(s_kvn, 2)
                e.wait_ge(f_kv.sem, f_kv.after(TILES - 1))
                for c in range(C):
                    for h in range(P // DH):
                        r = slice(h * DH, (h + 1) * DH)
                        ins = e.scalar_tensor_tensor(out=kv_blocks[r, c, :], in0=PKV[r, c, :],
                                                     scalar=e_inv[r, c * (P // DH) + h:c * (P // DH) + h + 1],
                                                     in1=block_mask[r, :], op0=ALU.mult, op1=ALU.mult)
                    ins.then_inc(s_kvn, 1)
                for c in range(C):
                    e.wait_ge(s_whi, c + 1)
                    e.tensor_tensor(wmix_lo[:, c, :], PW[c % 2][:, :], wmix_hi[:, c, :].bitcast(F32),
                                    ALU.subtract).then_inc(s_wlo, 1)
        Cs.close()

        R = Scope()
        agg = R.sb("agg", [P, TILES * D])
        Ds = Scope()
        GRP = 8
        turns = ETILES // GRP
        table = Ds.sb("table", [P, ETILES, 2], I32)
        row_f = Ds.sb("row_f", [P, ETILES])
        columns = Ds.sb("columns", [P, P])
        from8 = Ds.two("from8", [P, GRP], I32)
        gathered = [[Ds.sb(f"gathered{s}_{j}", [P, D]) for j in range(GRP)] for s in range(2)]
        onehot = Ds.two("onehot", [P, GRP, P])
        PA = [[Ds.ps(f"PA{s}_{p}", [P, D]) for p in range(GRP // 2)] for s in range(2)]
        s_table = sem("s_table")
        s_agg = sem("s_agg")
        s_cols = sem("s_cols")
        s_rowf = sem("s_rowf")
        f_from = flow("f_from")
        g_in = [transfers(f"g_in{j}_", credit=0) for j in range(GRP)]
        f_hot = flow("f_hot")
        f_emm = flow("f_emm", GRP // 2)
        f_add = flow("f_add", GRP // 2)
        flows = [f_from, *g_in, f_hot, f_emm, f_add]

        with nc.Block() as block:

            @block.sync
            def _(e):
                give_credit(e, flows)
                e.dma_start(table[:, :, :].rearrange("p t w -> p (t w)"),
                            rec_d.rearrange("(p t) w -> p (t w)", p=P)).then_inc(s_table, 16)
                e.dma_start(agg[:, :].rearrange("p (t d) -> p t d", d=D),
                            self_d.rearrange("(t p) d -> p t d", p=P)).then_inc(s_agg, 16)

            @block.gpsimd
            def _(e):
                e.iota(columns[:, :], pattern=[[1, P]], base=0, channel_multiplier=0,
                       allow_small_or_imprecise_dtypes=True).then_inc(s_cols, 1)
                e.wait_ge(s_table, 16)

                def gather(t, s):
                    e.wait_ge(f_emm.sem, f_emm.freed(t))
                    e.tensor_copy(from8[s][:, :], table[:, bass.ds(GRP * t, GRP), 0]).then_inc(f_from.sem, 1)
                    e.wait_ge(f_from.sem, f_from.after(t))
                    e.tensor_tensor(pace[:, 1:2], zeros[:, 0:1], zeros[:, 1:2], ALU.add)
                    for j in range(GRP):
                        e.indirect_dma_start(gathered[s][j][:, :], None, y_d,
                                             bass.IndirectOffsetOnAxis(from8[s][:, j:j + 1], 0))\
                            .then_inc(g_in[j].sems[s], 16)

                stages(e, turns, (0, gather))

            @block.tensor
            def _(e):
                def spread(t, s):
                    e.wait_ge(f_hot.sem, f_hot.after(t))
                    e.wait_ge(f_add.sem, f_add.freed(t))
                    for j in range(GRP):
                        e.wait_ge(g_in[j].sems[s], g_in[j].after(t, s))
                        mm = e.matmul(PA[s][j // 2][:, :], onehot[s][:, j, :], gathered[s][j][:, :],
                                      start=(j % 2 == 0), stop=(j % 2 == 1))
                        if j % 2:
                            mm.then_inc(f_emm.sem, 1)

                stages(e, turns, (0, spread))

            @block.vector
            def _(e):
                e.wait_ge(s_table, 16)
                e.tensor_copy(row_f[:, :], table[:, :, 1]).then_inc(s_rowf, 1)
                e.wait_ge(s_rowf, 1)
                e.wait_ge(s_cols, 1)
                e.wait_ge(s_agg, 16)

                def hot(t, s):
                    e.wait_ge(f_emm.sem, f_emm.freed(t))
                    e.tensor_tensor(onehot[s][:, :, :], columns[:, :].unsqueeze(1).broadcast_to([P, GRP, P]),
                                    row_f[:, bass.ds(GRP * t, GRP)].unsqueeze(2).broadcast_to([P, GRP, P]),
                                    ALU.is_equal).then_inc(f_hot.sem, 1)

                def add(t, s):
                    for p in range(GRP // 2):
                        b = e.value_load(bucket_of_pair[0:1, bass.ds(GRP // 2 * t + p, 1)], min_val=0,
                                         max_val=TILES - 1)
                        rows = agg[:, bass.ds(b * D, D)]
                        e.wait_ge(f_add.sem, f_add.after(t, p) if p else f_add.after(t - 1))
                        e.wait_ge(f_emm.sem, f_emm.after(t, p + 1))
                        e.tensor_tensor(rows, rows, PA[s][p][:, :], ALU.add).then_inc(f_add.sem, 1)

                stages(e, turns, (1, hot), (0, add))
        Ds.close()
        clear_semaphores()

        Es = Scope()
        w1_hi = Es.sb("w1_hi", [P, C, HID], F32R)
        w1_lo = Es.sb("w1_lo", [P, C, HID], F32R)
        w2_hi = Es.sb("w2_hi", [P, HC, D], F32R)
        w2_lo = Es.sb("w2_lo", [P, HC, D], F32R)
        b1_col = Es.sb("b1_col", [P, HC])
        rows2 = Es.sb("rows2", [P, 2, D])
        Es1 = Scope()
        raw1 = Es1.sb("w1_raw", [P, C, HID])
        raw2 = Es1.sb("w2_raw", [P, HC, D])
        g2col = Es1.sb("g2col", [P, C])
        be2col = Es1.sb("be2col", [P, C])
        b1raw = Es1.sb("b1raw", [P, HC])
        brow2 = Es1.sb("brow2", [1, 2, D])
        PR = Es1.ps("PR", [P, 2, D])
        PR2 = Es1.ps("PR2", [P, D])
        s_in4 = sem("s_in4")
        s_mm4 = sem("s_mm4")
        s_hi4 = sem("s_hi4")
        s_v4 = sem("s_v4")

        with nc.Block() as block:

            @block.sync
            def _(e):
                e.dma_start(raw1[:, :, :], W1.rearrange("(c p) n -> p c n", p=P)).then_inc(s_in4, 16)
                e.dma_start(raw2[:, :, :], W2.rearrange("(c p) n -> p c n", p=P)).then_inc(s_in4, 16)
                e.dma_start(g2col[:, :], g2).then_inc(s_in4, 16)
                e.dma_start(be2col[:, :], be2).then_inc(s_in4, 16)
                e.dma_start(b1raw[:, :], b1).then_inc(s_in4, 16)
                e.dma_start(brow2[:, 0, :], bo.rearrange("(a n) -> a n", a=1)).then_inc(s_in4, 16)
                e.dma_start(brow2[:, 1, :], b2.rearrange("(a n) -> a n", a=1)).then_inc(s_in4, 16)

            @block.tensor
            def _(e):
                e.wait_ge(s_in4, 16 * 7)
                for i in range(2):
                    e.matmul(PR[:, i, :], ones[0:1, :], brow2[:, i, :], start=True, stop=True)
                for m in range(HC):
                    for c in range(C):
                        mm = e.matmul(PR2[:, m:m + 1], raw1[:, c, m * P:(m + 1) * P], be2col[:, c:c + 1],
                                      start=(c == 0), stop=(c == C - 1))
                mm.then_inc(s_mm4, 1)

            @block.scalar
            def _(e):
                e.wait_ge(s_in4, 16 * 7)
                for c in range(C):
                    e.activation(w1_hi[:, c, :], raw1[:, c, :], ACT.Copy, scale=g2col[:, c:c + 1])\
                        .then_inc(s_hi4, 1)
                for c in range(HC):
                    e.activation(w2_hi[:, c, :], raw2[:, c, :], ACT.Copy).then_inc(s_hi4, 1)

            @block.vector
            def _(e):
                e.wait_ge(s_in4, 16 * 7)
                e.wait_ge(s_hi4, C + HC)
                for c in range(C):
                    e.scalar_tensor_tensor(out=w1_lo[:, c, :], in0=raw1[:, c, :], scalar=g2col[:, c:c + 1],
                                           in1=w1_hi[:, c, :].bitcast(F32), op0=ALU.mult, op1=ALU.subtract)
                e.tensor_tensor(w2_lo[:, :, :], raw2[:, :, :], w2_hi[:, :, :].bitcast(F32), ALU.subtract)
                e.wait_ge(s_mm4, 1)
                e.tensor_tensor(b1_col[:, :], b1raw[:, :], PR2[:, 0:HC], ALU.add)
                e.tensor_copy(rows2[:, :, :], PR[:, :, :]).then_inc(s_v4, 1)
        Es1.close()

        X = Es.two("Xe", [P, D])
        Y = Es.two("Ye", [P, D])
        QS = Es.two("QSe", [P, D])
        U = Es.two("Ue", [P, D])
        QH = Es.two("QH", [P, C, P], F32R)
        QL = Es.two("QL", [P, C, P], F32R)
        UH = Es.two("UH", [P, C, P], F32R)
        UL = Es.two("UL", [P, C, P], F32R)
        HG = Es.two("HG", [P, HC, P])
        HH = Es.two("HH", [P, HC, P], F32R)
        HL = Es.two("HL", [P, HC, P], F32R)
        stats = Es.two("stats_e", [P, 6])
        mv = Es.two("mv_e", [P, 2])
        rs = Es.two("rs_e", [P, 1])
        sc = Es.sb("sc_e", [P, 1])
        PTQ = [Es.ps(f"PTQ{s}", [P, C, P]) for s in range(2)]
        PTU = [Es.ps(f"PTU{s}", [P, C, P]) for s in range(2)]
        PO = Es.ps("PO", [P, D])
        PH = Es.ps("PH", [P, HC, P])
        PF = Es.ps("PF", [P, D])
        x_in, xn_in, qs_in, x1_out = transfers("x_in4"), transfers("xn_in4"), transfers("qs_in4"), transfers("x1_out")
        f_tq = flow("f_tq")
        f_qh = flow("f_qh")
        f_ql = flow("f_ql")
        f_po = flow("f_po")
        f_xnb = flow("f_xnb")
        f_y = flow("f_y")
        f_st = flow("f_st")
        f_mv = flow("f_mv4")
        f_rs = flow("f_rs4", 2)
        f_u = flow("f_u")
        f_tu = flow("f_tu")
        f_uh = flow("f_uh")
        f_ul = flow("f_ul")
        f_ph = flow("f_ph")
        f_hg = flow("f_hg", HC)
        f_hh = flow("f_hh")
        f_hl = flow("f_hl")
        f_pf = flow("f_pf")
        f_relu = flow("f_relu")
        f_sum = flow("f_sum4", 2)
        f_x1 = flow("f_x1")
        flows = [x_in, xn_in, qs_in, x1_out, f_tq, f_qh, f_ql, f_po, f_xnb, f_y, f_st, f_mv, f_rs, f_u, f_tu, f_uh,
                 f_ul, f_ph, f_hg, f_hh, f_hl, f_pf, f_relu, f_sum, f_x1]

        with nc.Block() as block:

            @block.sync
            def _(e):
                give_credit(e, flows)

                def load(t, s):
                    rows = rows_of(t)
                    e.wait_ge(f_tq.sem, f_tq.freed(t))
                    e.dma_start(QS[s][:, :], tile_rows(qs_d, t)).then_inc(qs_in.sems[s], 16)
                    e.wait_ge(f_u.sem, f_u.freed(t))
                    e.wait_ge(f_sum.sem, f_sum.freed(t))
                    e.dma_start(Y[s][:, :], tile_rows(xn_d, t)).then_inc(xn_in.sems[s], 16)
                    e.wait_ge(x1_out.sems[s], x1_out.freed(t, s))
                    e.dma_start(X[s][0:rows, :], tile_rows(x, t, rows)).then_inc(x_in.sems[s], 16)

                def store(t, s):
                    e.wait_ge(f_x1.sem, f_x1.after(t))
                    e.dma_start(tile_rows(x1_d, t), X[s][:, :]).then_inc(x1_out.sems[s], 16)

                stages(e, TILES, (1, load), (0, store))
                for s in range(2):
                    e.wait_ge(x1_out.sems[s], x1_out.after(TILES - 1 - s, (TILES - 1 - s) % 2))

            @block.gpsimd
            def _(e):
                def front(t, s):
                    e.wait_ge(xn_in.sems[s], xn_in.after(t, s))
                    e.tensor_tensor(Y[s][:, :], Y[s][:, :], rows2[:, 0, :], ALU.add).then_inc(f_xnb.sem, 1)
                    e.wait_ge(f_mv.sem, f_mv.after(t))
                    e.tensor_tensor(sc[:, :], mv[s][:, 1:2], eps_c, ALU.add).then_inc(f_rs.sem, 1)
                    e.wait_ge(f_rs.sem, f_rs.after(t, 1))
                    e.tensor_tensor(rs[s][:, :], sc[:, :], mhalf, ALU.pow).then_inc(f_rs.sem, 1)

                def back(t, s):
                    e.wait_ge(f_relu.sem, f_relu.after(t))
                    e.tensor_tensor(X[s][:, :], X[s][:, :], Y[s][:, :], ALU.add).then_inc(f_sum.sem, 1)
                    e.wait_ge(f_sum.sem, f_sum.after(t, 1))
                    e.tensor_tensor(X[s][:, :], X[s][:, :], rows2[:, 1, :], ALU.add).then_inc(f_sum.sem, 1)

                stages(e, TILES, (1, front), (0, back))

            @block.tensor
            def _(e):
                def front(t, s):
                    e.wait_ge(qs_in.sems[s], qs_in.after(t, s))
                    e.wait_ge(f_ql.sem, f_ql.freed(t))
                    for c in range(C):
                        mm = e.transpose(PTQ[s][:, c, :], QS[s][:, c * P:(c + 1) * P], ident[:, :])
                    mm.then_inc(f_tq.sem, 1)
                    e.wait_ge(f_ql.sem, f_ql.after(t))
                    e.wait_ge(f_y.sem, f_y.after(t - 1))
                    split_products(e, PO[:, :], QH[s], QL[s], wmix_hi, wmix_lo, C).then_inc(f_po.sem, 1)

                def back(t, s):
                    e.wait_ge(f_u.sem, f_u.after(t))
                    e.wait_ge(f_ul.sem, f_ul.freed(t))
                    for c in range(C):
                        mm = e.transpose(PTU[s][:, c, :], U[s][:, c * P:(c + 1) * P], ident[:, :])
                    mm.then_inc(f_tu.sem, 1)
                    e.wait_ge(f_ul.sem, f_ul.after(t))
                    e.wait_ge(f_hg.sem, f_hg.after(t - 1))
                    for m in range(HC):
                        mm = split_products(e, PH[:, m, :], w1_hi[:, :, m * P:(m + 1) * P],
                                            w1_lo[:, :, m * P:(m + 1) * P], UH[s], UL[s], C)
                    mm.then_inc(f_ph.sem, 1)
                    e.wait_ge(f_hl.sem, f_hl.after(t))
                    e.wait_ge(f_x1.sem, f_x1.after(t - 1))
                    split_products(e, PF[:, :], HH[s], HL[s], w2_hi, w2_lo, HC).then_inc(f_pf.sem, 1)

                stages(e, TILES, (1, front), (0, back))

            @block.scalar
            def _(e):
                def front(t, s):
                    e.wait_ge(f_tq.sem, f_tq.after(t))
                    e.wait_ge(f_po.sem, f_po.freed(t))
                    e.activation(QH[s][:, :, :], PTQ[s][:, :, :], ACT.Copy).then_inc(f_qh.sem, 1)

                def back(t, s):
                    e.wait_ge(f_tu.sem, f_tu.after(t))
                    e.wait_ge(f_ph.sem, f_ph.freed(t))
                    e.activation(UH[s][:, :, :], PTU[s][:, :, :], ACT.Copy).then_inc(f_uh.sem, 1)
                    e.wait_ge(f_ph.sem, f_ph.after(t))
                    e.wait_ge(f_hl.sem, f_hl.freed(t))
                    for m in range(HC):
                        e.activation(HG[s][:, m, :], PH[:, m, :], ACT.Gelu, bias=b1_col[:, m:m + 1])\
                            .then_inc(f_hg.sem, 1)
                    e.wait_ge(f_hg.sem, f_hg.after(t))
                    e.wait_ge(f_pf.sem, f_pf.freed(t))
                    e.activation(HH[s][:, :, :], HG[s][:, :, :], ACT.Copy).then_inc(f_hh.sem, 1)

                stages(e, TILES, (1, front), (0, back))

            @block.vector
            def _(e):
                def front(t, s):
                    e.wait_ge(f_qh.sem, f_qh.after(t))
                    e.tensor_tensor(QL[s][:, :, :], PTQ[s][:, :, :], QH[s][:, :, :].bitcast(F32), ALU.subtract)\
                        .then_inc(f_ql.sem, 1)
                    e.wait_ge(x_in.sems[s], x_in.after(t, s))
                    e.scalar_tensor_tensor(out=X[s][:, :], in0=agg[:, bass.ds(t * D, D)], scalar=0.0,
                                           in1=X[s][:, :], op0=ALU.max, op1=ALU.add).then_inc(f_relu.sem, 1)
                    e.wait_ge(f_po.sem, f_po.after(t))
                    e.wait_ge(f_xnb.sem, f_xnb.after(t))
                    e.tensor_tensor(Y[s][:, :], PO[:, :], Y[s][:, :], ALU.add).then_inc(f_y.sem, 1)
                    e.wait_ge(f_y.sem, f_y.after(t))
                    e.bn_stats(stats[s][:, :], Y[s][:, :]).then_inc(f_st.sem, 1)
                    e.wait_ge(f_st.sem, f_st.after(t))
                    e.memset(pace[:, 0:1], 0.0)
                    e.bn_aggr(mv[s][:, :], stats[s][:, :]).then_inc(f_mv.sem, 1)
                    e.wait_ge(f_rs.sem, f_rs.after(t))
                    e.wait_ge(f_tu.sem, f_tu.freed(t))
                    e.tensor_scalar(U[s][:, :], Y[s][:, :], mv[s][:, 0:1], rs[s][:, :], ALU.subtract, ALU.mult)\
                        .then_inc(f_u.sem, 1)

                def back(t, s):
                    e.wait_ge(f_uh.sem, f_uh.after(t))
                    e.tensor_tensor(UL[s][:, :, :], PTU[s][:, :, :], UH[s][:, :, :].bitcast(F32), ALU.subtract)\
                        .then_inc(f_ul.sem, 1)
                    e.wait_ge(f_hh.sem, f_hh.after(t))
                    e.tensor_tensor(HL[s][:, :, :], HG[s][:, :, :], HH[s][:, :, :].bitcast(F32), ALU.subtract)\
                        .then_inc(f_hl.sem, 1)
                    e.wait_ge(f_pf.sem, f_pf.after(t))
                    e.wait_ge(f_sum.sem, f_sum.after(t))
                    e.tensor_tensor(X[s][:, :], PF[:, :], X[s][:, :], ALU.add).then_inc(f_x1.sem, 1)

                stages(e, TILES, (1, front), (0, back))
        Es.close()
        R.close()
        M.close()
        Held.close()

        Fs = Scope()
        e1_hi = Fs.sb("e1_hi", [P, EXPERTS, C, HID], F32R)
        e1_lo = Fs.sb("e1_lo", [P, EXPERTS, C, HID], F32R)
        e2_hi = Fs.sb("e2_hi", [P, EXPERTS, HC, D], F32R)
        e2_lo = Fs.sb("e2_lo", [P, EXPERTS, HC, D], F32R)
        wr_hi = Fs.sb("wr_hi", [P, C, EXPERTS], F32R)
        wr_lo = Fs.sb("wr_lo", [P, C, EXPERTS], F32R)
        e1b_col = Fs.sb("e1b_col", [P, EXPERTS * HC])
        e2b_sb = Fs.sb("e2b_sb", [EXPERTS, D])
        br_rows = Fs.sb("br_rows", [P, EXPERTS])
        row_of = Fs.sb("row_of", [EXPERTS, EXPERTS, P])
        expert_no = Fs.sb("expert_no", [P, EXPERTS])
        Fs1 = Scope()
        rawm = Fs1.two("rawm", [P, C * HID])
        wr_raw = Fs1.sb("wr_raw", [P, C, EXPERTS])
        br_raw = Fs1.sb("br_raw", [1, EXPERTS])
        PB0 = Fs1.ps("PB0", [P, D])
        s_in5 = [sem(f"s_in5{s}") for s in range(2)]
        s_small5 = sem("s_small5")
        s_hi5 = sem("s_hi5")
        s_lo5 = sem("s_lo5")
        s_mm5 = sem("s_mm5")
        s_c5 = sem("s_c5")
        s_v5 = sem("s_v5")
        loads = [(e1_hi, e1_lo, E1, n) for n in range(EXPERTS)] + [(e2_hi, e2_lo, E2, n) for n in range(EXPERTS)]

        with nc.Block() as block:

            @block.sync
            def _(e):
                e.dma_start(wr_raw[:, :, :], Wr.rearrange("(c p) n -> p c n", p=P)).then_inc(s_small5, 16)
                e.dma_start(br_raw[:, :], br.rearrange("(a n) -> a n", a=1)).then_inc(s_small5, 16)
                e.dma_start(e1b_col[:, :], e1b).then_inc(s_small5, 16)
                e.dma_start(e2b_sb[:, :], e2b).then_inc(s_small5, 16)
                for i, (_, _, w, n) in enumerate(loads):
                    if i >= 2:
                        e.wait_ge(s_lo5, i - 1)
                    e.dma_start(rawm[i % 2][:, :].rearrange("p (c n) -> p c n", n=w.shape[2]),
                                w[n].rearrange("(c p) n -> p c n", p=P)).then_inc(s_in5[i % 2], 16)

            @block.gpsimd
            def _(e):
                e.iota(expert_no[:, :], pattern=[[1, EXPERTS]], base=0, channel_multiplier=0,
                       allow_small_or_imprecise_dtypes=True)
                e.memset(row_of[:, :, :], 0.0).then_inc(s_c5, 1)
                e.wait_ge(s_c5, 1)
                e.affine_select(out=row_of[:, :, :], in_=row_of[:, :, :], compare_op=ALU.not_equal, fill=1.0,
                                base=0, pattern=[[-1, EXPERTS], [0, P]], channel_multiplier=1).then_inc(s_c5, 1)

            @block.tensor
            def _(e):
                e.wait_ge(s_small5, 16 * 4)
                e.matmul(PB0[:, 0:EXPERTS], ones[0:1, :], br_raw[:, :], start=True, stop=True).then_inc(s_mm5, 1)

            @block.scalar
            def _(e):
                e.wait_ge(s_small5, 16 * 4)
                e.activation(wr_hi[:, :, :], wr_raw[:, :, :], ACT.Copy).then_inc(s_hi5, 1)
                for i, (hi, _, w, n) in enumerate(loads):
                    e.wait_ge(s_in5[i % 2], 16 * (i // 2 + 1))
                    e.activation(hi[:, n, :, :].rearrange("p c n -> p (c n)"), rawm[i % 2][:, :], ACT.Copy)\
                        .then_inc(s_hi5, 1)

            @block.vector
            def _(e):
                e.wait_ge(s_hi5, 1)
                e.tensor_tensor(wr_lo[:, :, :], wr_raw[:, :, :], wr_hi[:, :, :].bitcast(F32), ALU.subtract)
                e.wait_ge(s_mm5, 1)
                e.tensor_copy(br_rows[:, :], PB0[:, 0:EXPERTS])
                for i, (hi, lo, w, n) in enumerate(loads):
                    e.wait_ge(s_hi5, i + 2)
                    e.tensor_tensor(lo[:, n, :, :].rearrange("p c n -> p (c n)"), rawm[i % 2][:, :],
                                    hi[:, n, :, :].rearrange("p c n -> p (c n)").bitcast(F32), ALU.subtract)\
                        .then_inc(s_lo5, 1)
        Fs1.close()

        X = Fs.two("Xf", [P, D])
        Z = Fs.two("Zf", [P, D])
        OUT = Fs.two("OUT", [P, D])
        ZH = Fs.two("ZH", [P, C, P], F32R)
        ZL = Fs.two("ZL", [P, C, P], F32R)
        stats = Fs.two("stats_f", [P, 6])
        mv = Fs.two("mv_f", [P, 2])
        rs = Fs.two("rs_f", [P, 1])
        sc = Fs.sb("sc_f", [P, 1])
        logits = Fs.two("logits", [P, EXPERTS])
        best = Fs.two("best", [P, EXPERTS])
        neg = Fs.two("neg", [P, 1])
        expd = Fs.two("expd", [P, EXPERTS])
        total = Fs.two("total", [P, 1])
        prob = Fs.two("prob", [P, EXPERTS])
        order = Fs.two("order", [P, EXPERTS], U32)
        order_f = Fs.two("order_f", [P, 2])
        second = Fs.two("second", [P, EXPERTS])
        cw = Fs.two("cw", [P, EXPERTS])
        cwT = Fs.two("cwT", [EXPERTS, P])
        HR = Fs.two("HR", [P, HC, P])
        HS = Fs.two("HS", [P, HC, P])
        HSH = Fs.two("HSH", [P, HC, P], F32R)
        HSL = Fs.two("HSL", [P, HC, P], F32R)
        PTZ = Fs.ps("PTZ", [P, C, P])
        PLG = [Fs.ps(f"PLG{s}", [P, D]) for s in range(2)]
        PCW = Fs.ps("PCW", [P, EXPERTS, P])
        PHX = [Fs.ps(f"PHX{s}", [P, HC, P]) for s in range(2)]
        POUT = Fs.ps("POUT", [P, D])
        x_in, out_out = transfers("x_in5"), transfers("out_out")
        f_st = flow("f_st5")
        f_mv = flow("f_mv5")
        f_rs = flow("f_rs5", 2)
        f_z = flow("f_z")
        f_tz = flow("f_tz")
        f_zh = flow("f_zh")
        f_zl = flow("f_zl")
        f_lg = flow("f_lg")
        RT = 12
        f_rt = flow("f_rt", RT)
        f_ex = flow("f_ex")
        f_ct = flow("f_ct")
        f_cc = flow("f_cc")
        f_cb = flow("f_cb")
        f_ph = flow("f_ph5", EXPERTS)
        f_hr = flow("f_hr", EXPERTS * HC)
        f_hs = flow("f_hs", EXPERTS)
        f_hh = flow("f_hh5", EXPERTS)
        f_hl = flow("f_hl5", EXPERTS)
        f_po = flow("f_po5", EXPERTS)
        f_out = flow("f_out")
        flows = [x_in, out_out, f_st, f_mv, f_rs, f_z, f_tz, f_zh, f_zl, f_lg, f_rt, f_ex, f_ct, f_cc, f_cb, f_ph,
                 f_hr, f_hs, f_hh, f_hl, f_po, f_out]

        with nc.Block() as block:

            @block.sync
            def _(e):
                give_credit(e, flows)

                def load(t, s):
                    e.wait_ge(f_out.sem, f_out.freed(t))
                    e.dma_start(X[s][:, :], tile_rows(x1_d, t)).then_inc(x_in.sems[s], 16)

                def store(t, s):
                    rows = rows_of(t)
                    e.wait_ge(f_out.sem, f_out.after(t))
                    e.dma_start(tile_rows(out, t, rows), OUT[s][0:rows, :]).then_inc(out_out.sems[s], 16)

                stages(e, TILES, (1, load), (0, store))
                for s in range(2):
                    e.wait_ge(out_out.sems[s], out_out.after(TILES - 1 - s, (TILES - 1 - s) % 2))

            @block.gpsimd
            def _(e):
                def front(t, s):
                    e.wait_ge(f_mv.sem, f_mv.after(t))
                    e.tensor_tensor(sc[:, :], mv[s][:, 1:2], eps_c, ALU.add).then_inc(f_rs.sem, 1)
                    e.wait_ge(f_rs.sem, f_rs.after(t, 1))
                    e.tensor_tensor(rs[s][:, :], sc[:, :], mhalf, ALU.pow).then_inc(f_rs.sem, 1)

                stages(e, TILES, (0, front))

            @block.tensor
            def _(e):
                def front(t, s):
                    e.wait_ge(f_z.sem, f_z.after(t))
                    e.wait_ge(f_zl.sem, f_zl.after(t - 1))
                    for c in range(C):
                        mm = e.transpose(PTZ[:, c, :], Z[s][:, c * P:(c + 1) * P], ident[:, :])
                    mm.then_inc(f_tz.sem, 1)
                    e.wait_ge(f_zl.sem, f_zl.after(t))
                    e.wait_ge(f_rt.sem, f_rt.freed(t))
                    split_products(e, PLG[s][:, 0:EXPERTS], ZH[s], ZL[s], wr_hi, wr_lo, C).then_inc(f_lg.sem, 1)

                def back(t, s):
                    e.wait_ge(f_rt.sem, f_rt.after(t))
                    e.transpose(PLG[s][0:EXPERTS, P:2 * P], cw[s][:, :], ident[:, :]).then_inc(f_ct.sem, 1)
                    e.wait_ge(f_cc.sem, f_cc.after(t))
                    e.wait_ge(f_hs.sem, f_hs.after(t - 1))
                    for n in range(EXPERTS):
                        mm = e.matmul(PCW[:, n, :], row_of[:, n, :], cwT[s][:, :], start=True, stop=True)
                    mm.then_inc(f_cb.sem, 1)
                    e.wait_ge(f_out.sem, f_out.after(t - 1))
                    e.matmul(POUT[:, :], cwT[s][:, :], e2b_sb[:, :], start=True, stop=False)
                    for n in range(EXPERTS + 1):
                        if n < EXPERTS:
                            e.wait_ge(f_hr.sem, f_hr.after(t - 1, HC * (EXPERTS + n - 1)) if n < 2 else
                                      f_hr.after(t, HC * (n - 1)))
                            for m in range(HC):
                                mm = split_products(e, PHX[n % 2][:, m, :], e1_hi[:, n, :, m * P:(m + 1) * P],
                                                    e1_lo[:, n, :, m * P:(m + 1) * P], ZH[s], ZL[s], C)
                            mm.then_inc(f_ph.sem, 1)
                        if n:
                            k = n - 1
                            e.wait_ge(f_hl.sem, f_hl.after(t, n))
                            for m in range(HC):
                                for a, b in ((HSH, e2_hi), (HSH, e2_lo), (HSL, e2_hi)):
                                    mm = e.matmul(POUT[:, :], a[k % 2][:, m, :], b[:, k, m, :], start=False,
                                                  stop=(n == EXPERTS and m == HC - 1 and a is HSL))
                            mm.then_inc(f_po.sem, 1)

                stages(e, TILES, (1, front), (0, back))

            @block.scalar
            def _(e):
                def front(t, s):
                    e.wait_ge(f_tz.sem, f_tz.after(t))
                    e.wait_ge(f_ph.sem, f_ph.freed(t))
                    e.activation(ZH[s][:, :, :], PTZ[:, :, :], ACT.Copy).then_inc(f_zh.sem, 1)

                def back(t, s):
                    e.wait_ge(f_rt.sem, f_rt.after(t, 3))
                    e.activation(expd[s][:, :], logits[s][:, :], ACT.Exp, bias=neg[s][:, :])\
                        .then_inc(f_ex.sem, 1)
                    for n in range(EXPERTS + 1):
                        if n < EXPERTS:
                            e.wait_ge(f_ph.sem, f_ph.after(t, n + 1))
                            e.wait_ge(f_hs.sem, f_hs.after(t - 1, EXPERTS + n - 1) if n < 2 else f_hs.after(t, n - 1))
                            for m in range(HC):
                                e.activation(HR[n % 2][:, m, :], PHX[n % 2][:, m, :], ACT.Relu,
                                             bias=e1b_col[:, n * HC + m:n * HC + m + 1]).then_inc(f_hr.sem, 1)
                        if n:
                            k = n - 1
                            e.wait_ge(f_hs.sem, f_hs.after(t, n))
                            e.wait_ge(f_po.sem, f_po.after(t - 1, EXPERTS + k - 1) if k < 2 else f_po.after(t, k - 1))
                            e.activation(HSH[k % 2][:, :, :], HS[k % 2][:, :, :], ACT.Copy).then_inc(f_hh.sem, 1)

                stages(e, TILES, (1, front), (0, back))

            @block.vector
            def _(e):
                def front(t, s):
                    e.wait_ge(x_in.sems[s], x_in.after(t, s))
                    e.bn_stats(stats[s][:, :], X[s][:, :]).then_inc(f_st.sem, 1)
                    e.wait_ge(f_st.sem, f_st.after(t))
                    e.memset(pace[:, 0:1], 0.0)
                    e.bn_aggr(mv[s][:, :], stats[s][:, :]).then_inc(f_mv.sem, 1)
                    e.wait_ge(f_rs.sem, f_rs.after(t))
                    e.wait_ge(f_tz.sem, f_tz.freed(t))
                    e.tensor_scalar(Z[s][:, :], X[s][:, :], mv[s][:, 0:1], rs[s][:, :], ALU.subtract, ALU.mult)\
                        .then_inc(f_z.sem, 1)
                    e.wait_ge(f_zh.sem, f_zh.after(t))
                    e.tensor_tensor(ZL[s][:, :, :], PTZ[:, :, :], ZH[s][:, :, :].bitcast(F32), ALU.subtract)\
                        .then_inc(f_zl.sem, 1)

                def back(t, s):
                    step = [0]

                    def did(ins, wait=True):
                        step[0] += 1
                        ins.then_inc(f_rt.sem, 1)
                        if wait:
                            e.wait_ge(f_rt.sem, f_rt.after(t, step[0]))
                            e.memset(pace[:, 0:1], 0.0)

                    e.wait_ge(f_lg.sem, f_lg.after(t))
                    did(e.tensor_tensor(logits[s][:, :], PLG[s][:, 0:EXPERTS], br_rows[:, :], ALU.add))
                    did(e.max(best[s][:, :], logits[s][:, :]))
                    did(e.tensor_scalar(neg[s][:, :], best[s][:, 0:1], -1.0, None, ALU.mult), wait=False)
                    e.wait_ge(f_ex.sem, f_ex.after(t))
                    did(e.tensor_reduce(total[s][:, :], expd[s][:, :], AX.X, ALU.add))
                    did(e.reciprocal(total[s][:, :], total[s][:, :]))
                    did(e.tensor_scalar(prob[s][:, :], expd[s][:, :], total[s][:, :], None, ALU.mult))
                    did(e.max(best[s][:, :], prob[s][:, :]))
                    did(e.max_index(order[s][:, :], best[s][:, :], prob[s][:, :]))
                    did(e.tensor_copy(order_f[s][:, :], order[s][:, 0:2]))
                    did(e.tensor_scalar(second[s][:, :], expert_no[:, :], order_f[s][:, 1:2], best[s][:, 1:2],
                                        ALU.is_equal, ALU.mult), wait=False)
                    did(e.tensor_scalar(cw[s][:, :], expert_no[:, :], order_f[s][:, 0:1], best[s][:, 0:1],
                                        ALU.is_equal, ALU.mult))
                    did(e.tensor_tensor(cw[s][:, :], cw[s][:, :], second[s][:, :], ALU.add), wait=False)
                    assert step[0] == RT
                    e.wait_ge(f_ct.sem, f_ct.after(t))
                    e.tensor_copy(cwT[s][:, :], PLG[s][0:EXPERTS, P:2 * P]).then_inc(f_cc.sem, 1)
                    e.wait_ge(f_cb.sem, f_cb.after(t))
                    for n in range(EXPERTS + 1):
                        if n < EXPERTS:
                            e.wait_ge(f_hr.sem, f_hr.after(t, HC * (n + 1)))
                            e.wait_ge(f_hl.sem, f_hl.after(t - 1, EXPERTS + n - 1) if n < 2 else f_hl.after(t, n - 1))
                            e.tensor_tensor(HS[n % 2][:, :, :], HR[n % 2][:, :, :],
                                            PCW[:, n, :].unsqueeze(1).broadcast_to([P, HC, P]), ALU.mult)\
                                .then_inc(f_hs.sem, 1)
                        if n:
                            k = n - 1
                            e.wait_ge(f_hh.sem, f_hh.after(t, n))
                            e.tensor_tensor(HSL[k % 2][:, :, :], HS[k % 2][:, :, :],
                                            HSH[k % 2][:, :, :].bitcast(F32), ALU.subtract).then_inc(f_hl.sem, 1)
                    e.wait_ge(f_po.sem, f_po.after(t))
                    e.wait_ge(out_out.sems[s], out_out.freed(t, s))
                    e.tensor_tensor(OUT[s][:, :], POUT[:, :], X[s][:, :], ALU.add).then_inc(f_out.sem, 1)

                stages(e, TILES, (1, front), (0, back))
        Fs.close()
        G.close()


_INS = ['x', 'src', 'dst', 'L0_gnn_self_w', 'L0_gnn_self_b', 'L0_gnn_neigh_w', 'L0_gnn_neigh_b', 'L0_mix_Wq',
        'L0_mix_bq', 'L0_mix_Wk', 'L0_mix_bk', 'L0_mix_Wv', 'L0_mix_bv', 'L0_mix_Wo', 'L0_mix_bo', 'L0_mix_W1',
        'L0_mix_b1', 'L0_mix_W2', 'L0_mix_b2', 'L0_mix_g1', 'L0_mix_be1', 'L0_mix_g2', 'L0_mix_be2', 'L0_ffn_Wr',
        'L0_ffn_br', 'L0_ffn_W1', 'L0_ffn_b1', 'L0_ffn_W2', 'L0_ffn_b2']
_TURNED = ('L0_gnn_self_w', 'L0_gnn_neigh_w')
_COLUMNS = ('L0_mix_g1', 'L0_mix_be1', 'L0_mix_g2', 'L0_mix_be2', 'L0_mix_b1', 'L0_ffn_b1')


def kernel(**inputs):
    import numpy as _np
    import concourse.bacc as _bacc
    from concourse import mybir as _mybir
    from concourse.bass_utils import run_bass_kernel_spmd as _run

    nc = _bacc.Bacc("TRN2", target_bir_lowering=False, num_devices=1)
    arrays, args = {}, []
    for name in _INS:
        a = _np.asarray(inputs[name])
        if name in _COLUMNS:
            a = a.reshape(-1, P).T
        a = _np.ascontiguousarray(a.T if name in _TURNED else a)
        arrays[f"in_{name}_dram"] = a
        args.append(nc.dram_tensor(f"in_{name}_dram", a.shape, _mybir.dt.from_np(a.dtype), kind="ExternalInput").ap())
    args.append(nc.dram_tensor("out_0_dram", arrays["in_x_dram"].shape, F32, kind="ExternalOutput").ap())
    gps_layer_kernel(nc, *args)
    r = _run(nc, [arrays], core_ids=[0])
    return r.results[0]["out_0_dram"]
```

```python
from contextlib import ExitStack

import concourse.bass as bass
from concourse import mybir

F32 = mybir.dt.float32
F32R = mybir.dt.float32r
I32 = mybir.dt.int32
U32 = mybir.dt.uint32
ALU = mybir.AluOpType
ACT = mybir.ActivationFunctionType
AX = mybir.AxisListType

P = 128
EPS_LN = 1e-5
EPS_FLOW = 1e-6


class Flow:

    def __init__(self, sem, n=1):
        self.sem, self.n, self.credit = sem, n, 2 * n

    def after(self, t, k=None):
        return self.n * t + self.credit + (self.n if k is None else k)

    def freed(self, t):
        return self.n * t + self.n


class Transfers:

    def __init__(self, sems, k=1, credit=1):
        self.sems, self.k = sems, k
        self.credit = 16 * k * credit

    def after(self, t, s):
        return 8 * self.k * (t - s) + 16 * self.k + self.credit

    def freed(self, t, s):
        return 8 * self.k * (t - s) + self.credit


def give_credit(eng, flows):
    for f in flows:
        for sem in (f.sems if isinstance(f, Transfers) else [f.sem]):
            if f.credit:
                eng.sem_inc(sem, f.credit)


def stages(eng, tiles, *parts, first=0):
    low, high = min(a for a, _ in parts), max(a for a, _ in parts)

    def turn(t, parity):
        for ahead, step in parts:
            if not isinstance(t, int) or first <= t + ahead < tiles:
                step(t + ahead, (parity + ahead) % 2)

    start = first - low
    looped = max(0, (tiles - 1 - high - start) // 2 * 2)
    for t in range(first - high, start):
        turn(t, t % 2)
    with eng.Fori(start, start + looped - 1, 2) as i:
        turn(i, start % 2)
        turn(i + 1, (start + 1) % 2)
    for t in range(start + looped, tiles - low):
        turn(t, t % 2)


def gps_layer_kernel(nc, x, src, dst, self_wT, self_b, neigh_wT, neigh_b, Wq, bq, Wk, bk, Wv, bv, Wo, bo,
                     W1, b1, W2, b2, g1, be1, g2, be2, Wr, br, E1, e1b, E2, e2b, out):
    N, D = x.shape
    EDGES = src.shape[0]
    TILES = (N + P - 1) // P
    NP = TILES * P
    TAIL = N - (TILES - 1) * P
    C = D // P
    H = 8
    DH = D // H
    HID = W1.shape[1]
    HC = HID // P
    EXPERTS = E1.shape[0]
    EP = 125
    EJ = EDGES // EP
    PAIR = 2 * P
    PAIRS = (EDGES - TILES) // PAIR + TILES + 1
    PAIRS += -PAIRS % 4
    ETILES = 2 * PAIRS
    NOROW = 200
    assert EP * EJ == EDGES and TILES % 2 == 1 and PAIRS % 4 == 0

    def rows_of(t):
        return TAIL if isinstance(t, int) and t == TILES - 1 else P

    def tile_rows(d, t, rows=P):
        return d[bass.ds(t * P, rows), :]

    def dram(name, shape, dt=F32):
        return nc.dram_tensor(name, shape, dt, kind="Internal").ap()

    xn_d = dram("xn_d", [NP, D])
    self_d = dram("self_d", [NP, D])
    y_d = dram("y_d", [NP, D])
    q_d = dram("q_d", [NP, D])
    k_d = dram("k_d", [NP, D])
    v_d = dram("v_d", [NP, D])
    qs_d = dram("qs_d", [NP, D])
    x1_d = dram("x1_d", [NP, D])
    rec_d = dram("rec_d", [ETILES * P, 2], I32)

    top = ExitStack()

    live = []

    def sem(name):
        live.append(nc.alloc_semaphore(name=name))
        return live[-1]

    def clear_semaphores():
        with nc.Block() as block:

            @block.gpsimd
            def _(e):
                nc.clear_and_free_semaphores(live)
        live.clear()

    def flow(name, n=1):
        return Flow(sem(name), n)

    def transfers(name, k=1, credit=1):
        return Transfers([sem(f"{name}{s}") for s in range(2)], k, credit)

    class Scope:
        def __init__(self):
            self.stack = ExitStack()

        def sb(self, name, shape, dt=F32):
            return self.stack.enter_context(nc.sbuf_tensor(name, shape, dt))

        def ps(self, name, shape, dt=F32):
            return self.stack.enter_context(nc.psum_tensor(name, shape, dt))

        def two(self, name, shape, dt=F32):
            return [self.sb(f"{name}{s}", shape, dt) for s in range(2)]

        def close(self):
            self.stack.close()

    def split_products(eng, bank, hi, lo, whi, wlo, n):
        last = None
        for c in range(n):
            for a, b in ((hi, whi), (hi, wlo), (lo, whi)):
                last = eng.matmul(bank, a[:, c, :], b[:, c, :], start=(c == 0 and a is hi and b is whi),
                                  stop=(c == n - 1 and a is lo))
        return last

    STATISTICS_OPS = 7
    CHOSEN, COUNTED = 15, 18

    def row_statistics(e, stats, mean, var, tmp, made):
        m0, m1 = stats[:, :, 1], stats[:, :, 4]
        e.tensor_tensor(mean[:, :], m0, m1, ALU.add).then_inc(made, 1)
        e.tensor_tensor(tmp[:, :], m0, m1, ALU.subtract).then_inc(made, 1)
        e.tensor_tensor(var[:, :], stats[:, :, 2], stats[:, :, 5], ALU.add).then_inc(made, 1)
        e.wait_ge(made, 3)
        e.tensor_scalar(mean[:, :], mean[:, :], 0.5, None, ALU.mult).then_inc(made, 1)
        e.scalar_tensor_tensor(out=tmp[:, :], in0=tmp[:, :], scalar=D / 4.0, in1=tmp[:, :], op0=ALU.mult,
                               op1=ALU.mult).then_inc(made, 1)
        e.wait_ge(made, 5)
        e.tensor_tensor(var[:, :], var[:, :], tmp[:, :], ALU.add).then_inc(made, 1)
        e.wait_ge(made, 6)
        e.tensor_scalar(var[:, :], var[:, :], 1.0 / D, None, ALU.mult).then_inc(made, 1)
        assert STATISTICS_OPS == 7

    def scatter_records(e, dest, places, recs, rows, columns, to, rec, first, turns, scat, f_slot):

        def scatter(t, s):
            if not (isinstance(t, int) and t < 2):
                e.wait_ge(scat.sems[s], scat.freed(t, s))
            column = bass.ds(columns * (t + first), columns)
            e.tensor_copy(to[s][0:rows, :], places[0:rows, column]).then_inc(f_slot.sem, 1)
            e.tensor_copy(rec[s][0:rows, :], recs[0:rows, column, :].rearrange("p j w -> p (j w)"))\
                .then_inc(f_slot.sem, 1)
            e.wait_ge(f_slot.sem, f_slot.after(t))
            e.tensor_tensor(pace[:, 1:2], zeros[:, 0:1], zeros[:, 1:2], ALU.add)
            for j in range(columns):
                e.indirect_dma_start(dest, bass.IndirectOffsetOnAxis(to[s][0:rows, j:j + 1], 0),
                                     rec[s][0:rows, 2 * j:2 * j + 2], None).then_inc(scat.sems[s], 16)

        scatter(0, 0)
        scatter(1, 1)
        stages(e, turns, (0, scatter), first=2)
        for s in range(2):
            e.wait_ge(scat.sems[s], scat.after(turns - 1 - s, (turns - 1 - s) % 2))

    with top:
        G = Scope()
        Held = Scope()
        SCAT = 8
        SCAT_TURNS = EJ // SCAT
        SCAT_FIRST = 76
        ident = G.sb("ident", [P, P])
        ones = G.sb("ones", [P, P])
        zeros = G.sb("zeros", [P, D])
        consts = G.sb("consts", [P, 4])
        eps_c, mhalf = consts[:, 0:1], consts[:, 1:2]
        pace = G.sb("pace", [P, 2])
        block_mask = G.sb("block_mask", [P, P])
        qsum = G.sb("qsum", [P, D])
        ksum = G.sb("ksum", [P, D])
        rs_all = G.sb("rs_all", [P, TILES])
        mean_all = G.sb("mean_all", [P, TILES])
        r2_all = G.sb("r2_all", [P, TILES])
        stats1 = G.sb("stats1", [P, TILES, 6])
        bucket_of_pair = G.sb("bucket_of_pair", [1, PAIRS], I32)

        place_i = Held.sb("place_i", [P, EJ], I32)
        records = Held.sb("records", [P, EJ, 2], I32)
        to8 = Held.two("to8", [P, SCAT], I32)
        rec8 = Held.two("rec8", [P, 2 * SCAT], I32)

        A = Scope()
        names = ("neigh", "self", "q", "k", "v")
        whi = {n: A.sb(f"whi_{n}", [P, C, D], F32R) for n in names}
        wlo = {n: A.sb(f"wlo_{n}", [P, C, D], F32R) for n in names}
        bias_all = A.sb("bias_all", [P, 4, D])
        bucket = A.sb("bucket", [P, EJ])
        bucket_ids = A.sb("bucket_ids", [P, TILES])
        ones_e = A.sb("ones_e", [P, EJ])
        counts = A.sb("counts", [P, TILES])
        base = A.sb("base", [P, TILES])
        S = Scope()
        raw = [S.sb(f"raw{s}", [P, C, D]) for s in range(2)]
        gcol = S.sb("gcol", [P, C])
        bcol = S.sb("bcol", [P, C])
        be_wide = S.sb("be_wide", [P, C, P])
        brow = S.sb("brow", [1, 5, D])
        rec_pad = S.sb("rec_pad", [P, ETILES, 2], I32)
        srcs = S.sb("srcs", [P, EJ], I32)
        dsts = S.sb("dsts", [P, EJ], I32)
        high = S.sb("high", [P, EJ], I32)
        pos = S.sb("pos", [P, EJ])
        rmatch = S.sb("rmatch", [P, EJ])
        rank = S.sb("rank", [P, EJ])
        placed = S.two("placed", [P, EJ])
        XG = 4
        x_turns = TILES // XG
        xs = S.two("xs", [P, XG, D])
        stats = S.sb("stats", [P, TILES, 6])
        st_a = S.sb("st_a", [P, TILES])
        st_b = S.sb("st_b", [P, TILES])
        match = S.sb("match", [P, EJ])
        upper = S.sb("upper", [P, P])
        upper_incl = S.sb("upper_incl", [P, P])
        pair_no = S.sb("pair_no", [P, PAIRS])
        padded = S.sb("padded", [P, TILES])
        padded_i = S.sb("padded_i", [P, TILES], I32)
        ends = S.sb("ends", [P, TILES])
        pad_col = S.sb("pad_col", [P, 1])
        pad_col_i = S.sb("pad_col_i", [P, 1], I32)
        end_col = S.sb("end_col", [P, 1])
        past = S.sb("past", [P, PAIRS])
        ps_bias = S.ps("ps_bias", [P, 4, D])
        ps_e = S.ps("ps_e", [P, D])
        ps_e2 = S.ps("ps_e2", [P, D])

        s_cons = sem("s_cons")
        s_consd = sem("s_consd")
        s_raw = [sem(f"s_raw{s}") for s in range(2)]
        s_small = sem("s_small")
        s_src = sem("s_src")
        s_pad = sem("s_pad")
        s_padout = sem("s_padout")
        s_wide = sem("s_wide")
        s_biasmm = sem("s_biasmm")
        s_hi = sem("s_hi")
        s_lo = sem("s_lo")
        s_biasv = sem("s_biasv")
        s_edge = sem("s_edge")
        s_count = sem("s_count")
        s_emm = sem("s_emm")
        s_stat = sem("s_stat")
        s_pow = sem("s_pow")
        s_rec = sem("s_rec")
        xs_in = transfers("xs_in")
        f_xs = flow("f_xs", XG)
        f_rank = flow("f_rank", 3)
        f_pos = flow("f_pos")
        weights = {"neigh": neigh_wT, "self": self_wT, "q": Wq, "k": Wk, "v": Wv}
        folded = {"neigh": False, "self": False, "q": True, "k": True, "v": True}

        with nc.Block() as block:

            @block.sync
            def _(e):
                give_credit(e, [xs_in, f_xs, f_rank, f_pos])
                e.dma_start(srcs[0:EP, :], src.rearrange("(p j) -> p j", p=EP)).then_inc(s_src, 16)
                e.dma_start(dsts[0:EP, :], dst.rearrange("(p j) -> p j", p=EP)).then_inc(s_src, 16)
                e.dma_start(gcol[:, :], g1).then_inc(s_small, 16)
                e.dma_start(bcol[:, :], be1).then_inc(s_small, 16)
                for i, b in enumerate((self_b, neigh_b, bq, bk, bv)):
                    e.dma_start(brow[:, i, :], b.rearrange("(a n) -> a n", a=1)).then_inc(s_small, 16)

                def load_x(t, s):
                    e.wait_ge(f_xs.sem, f_xs.freed(t))
                    e.dma_start(xs[s][:, :, :], x[bass.ds(XG * P * t, XG * P), :]
                                .rearrange("(g p) d -> p g d", p=P)).then_inc(xs_in.sems[s], 16)

                stages(e, x_turns, (0, load_x))
                e.wait_ge(f_xs.sem, f_xs.freed(x_turns))
                e.dma_start(xs[x_turns % 2][0:TAIL, 0, :], x[(TILES - 1) * P:N, :])\
                    .then_inc(xs_in.sems[x_turns % 2], 16)
                for i, n in enumerate(names):
                    if i >= 2:
                        e.wait_ge(s_hi, C * (i - 1))
                        e.wait_ge(s_lo, C * (i - 1))
                    if i == 4:
                        e.wait_ge(s_biasmm, 2)
                    e.dma_start(raw[i % 2][:, :, :], weights[n].rearrange("(c p) n -> p c n", p=P))\
                        .then_inc(s_raw[i % 2], 16)
                e.wait_ge(s_pad, 2)
                e.dma_start(rec_d.rearrange("(p t) w -> p (t w)", p=P),
                            rec_pad[:, :, :].rearrange("p t w -> p (t w)")).then_inc(s_padout, 16)
                e.wait_ge(s_padout, 16)

            @block.gpsimd
            def _(e):
                e.memset(ones[:, :], 1.0).then_inc(s_cons, 1)
                e.memset(ident[:, :], 0.0).then_inc(s_cons, 1)
                e.memset(zeros[:, :], 0.0).then_inc(s_cons, 1)
                e.memset(eps_c, EPS_LN).then_inc(s_cons, 1)
                e.memset(mhalf, -0.5).then_inc(s_cons, 1)
                e.memset(pace[:, :], 0.0).then_inc(s_cons, 1)
                e.memset(qsum[:, :], 0.0).then_inc(s_cons, 1)
                e.memset(ksum[:, :], 0.0).then_inc(s_cons, 1)
                e.memset(pos[:, :], 0.0).then_inc(s_cons, 1)
                e.memset(stats[:, :, :], 0.0).then_inc(s_cons, 1)
                e.memset(ones_e[:, :], 1.0).then_inc(s_cons, 1)
                e.memset(rec_pad[:, :, 0], 0).then_inc(s_pad, 1)
                e.memset(rec_pad[:, :, 1], NOROW).then_inc(s_pad, 1)
                e.iota(bucket_ids[:, :], pattern=[[1, TILES]], base=0, channel_multiplier=0,
                       allow_small_or_imprecise_dtypes=True).then_inc(s_cons, 1)
                e.iota(pair_no[:, :], pattern=[[1, PAIRS]], base=0, channel_multiplier=0,
                       allow_small_or_imprecise_dtypes=True).then_inc(s_cons, 1)
                e.wait_ge(s_cons, 13)
                e.affine_select(out=ident[:, :], in_=ident[:, :], compare_op=ALU.not_equal, fill=1.0, base=0,
                                pattern=[[-1, P]], channel_multiplier=1).then_inc(s_consd, 1)
                e.affine_select(out=upper[:, :], in_=ones[:, :], compare_op=ALU.is_gt, fill=0.0, base=0,
                                pattern=[[1, P]], channel_multiplier=-1).then_inc(s_consd, 1)
                e.affine_select(out=upper_incl[:, :], in_=ones[:, :], compare_op=ALU.is_ge, fill=0.0, base=0,
                                pattern=[[1, P]], channel_multiplier=-1).then_inc(s_consd, 1)
                ops = ((st_b, st_a, eps_c, ALU.add), (rs_all, st_b, mhalf, ALU.pow),
                       (st_b, st_a, rs_all, ALU.mult), (st_b, st_b, rs_all, ALU.mult),
                       (st_b, st_b, eps_c, ALU.add), (r2_all, st_b, mhalf, ALU.pow))
                e.wait_ge(s_stat, 7)
                for k, (o, a, b, op) in enumerate(ops):
                    b = b.broadcast_to([P, TILES]) if b is eps_c or b is mhalf else b[:, :]
                    e.tensor_tensor(o[:, :], a[:, :], b, op).then_inc(s_pow, 1)
                    e.wait_ge(s_pow, k + 1)

                def add_places(t, s):
                    e.wait_ge(f_pos.sem, f_pos.after(t - 1))
                    e.wait_ge(f_rank.sem, f_rank.after(t, 3))
                    e.tensor_tensor(pos[0:EP, :], pos[0:EP, :], placed[s][0:EP, :], ALU.add)\
                        .then_inc(f_pos.sem, 1)

                stages(e, TILES, (0, add_places))

            @block.tensor
            def _(e):
                e.wait_ge(s_consd, 3)
                e.wait_ge(s_small, 16 * 7)
                e.wait_ge(s_wide, C)
                e.matmul(ps_bias[:, 0, :], ones[0:1, :], brow[:, 0, :], start=True, stop=False)
                e.matmul(ps_bias[:, 0, :], ones[0:1, :], brow[:, 1, :], start=False, stop=True)
                for i in range(2, 5):
                    e.wait_ge(s_raw[i % 2], 16 * (i // 2 + 1))
                    e.matmul(ps_bias[:, i - 1, :], ones[0:1, :], brow[:, i, :], start=True, stop=False)
                    for c in range(C):
                        mm = e.matmul(ps_bias[:, i - 1, :], be_wide[:, c, :], raw[i % 2][:, c, :], start=False,
                                      stop=(c == C - 1))
                    mm.then_inc(s_biasmm, 2)
                e.wait_ge(s_count, TILES + 1)
                e.matmul(ps_e[:, 0:TILES], upper[0:EP, :], counts[0:EP, :], start=True, stop=True)
                e.matmul(ps_e[:, 64:64 + TILES], ones[0:EP, :], counts[0:EP, :], start=True, stop=True)
                e.matmul(ps_e[0:TILES, 128:129], counts[0:EP, :], ones[0:EP, 0:1], start=True, stop=True)\
                    .then_inc(s_emm, 1)
                e.wait_ge(s_edge, 8)
                e.matmul(ps_e2[0:TILES, 0:1], upper_incl[0:TILES, 0:TILES], pad_col[0:TILES, :], start=True,
                         stop=True).then_inc(s_emm, 1)
                e.wait_ge(s_edge, 11)
                e.matmul(ps_e2[0:1, 0:PAIRS], ones[0:TILES, 0:1], past[0:TILES, :], start=True, stop=True)\
                    .then_inc(s_emm, 1)

            @block.scalar
            def _(e):
                e.wait_ge(s_small, 16 * 7)
                for i, n in enumerate(names):
                    e.wait_ge(s_raw[i % 2], 16 * (i // 2 + 1))
                    for c in range(C):
                        e.activation(whi[n][:, c, :], raw[i % 2][:, c, :], ACT.Copy,
                                     scale=gcol[:, c:c + 1] if folded[n] else 1.0).then_inc(s_hi, 1)

            @block.vector
            def _(e):
                for h in range(P // DH):
                    for g in range(P // DH):
                        e.memset(block_mask[h * DH:(h + 1) * DH, g * DH:(g + 1) * DH], float(h == g))
                e.wait_ge(s_small, 16 * 7)
                e.wait_ge(s_cons, 13)
                for c in range(C):
                    e.tensor_scalar(be_wide[:, c, :], ones[:, :], bcol[:, c:c + 1], None, ALU.mult)\
                        .then_inc(s_wide, 1)
                e.wait_ge(s_src, 32)
                e.tensor_scalar(high[0:EP, :], srcs[0:EP, :], 7, None, ALU.logical_shift_right)\
                    .then_inc(s_edge, 1)
                e.wait_ge(s_edge, 1)
                e.tensor_copy(bucket[0:EP, :], high[0:EP, :]).then_inc(s_edge, 1)
                e.wait_ge(s_edge, 2)
                e.memset(match[0:EP, :], 0.0).then_inc(s_count, 1)
                with e.Fori(0, TILES, 1) as b:
                    e.wait_ge(s_count, b + 1)
                    e.tensor_scalar(match[0:EP, :], bucket[0:EP, :], bucket_ids[0:EP, bass.ds(b, 1)], 0.0,
                                    ALU.is_equal, ALU.add, accum_out=counts[0:EP, bass.ds(b, 1)])\
                        .then_inc(s_count, 1)

                def statistics(t, s):
                    e.wait_ge(xs_in.sems[s], xs_in.after(t, s))
                    for g in range(XG):
                        e.bn_stats(stats[:, bass.ds(XG * t + g, 1), :].rearrange("p t k -> p (t k)"),
                                   xs[s][:, g, :]).then_inc(f_xs.sem, 1)

                stages(e, x_turns, (0, statistics))
                e.wait_ge(xs_in.sems[x_turns % 2], xs_in.after(x_turns, x_turns % 2))
                e.bn_stats(stats[0:TAIL, TILES - 1, :], xs[x_turns % 2][0:TAIL, 0, :]).then_inc(f_xs.sem, 1)
                e.wait_ge(f_xs.sem, f_xs.after(x_turns - 1) + 1)
                row_statistics(e, stats, mean_all, st_a, st_b, s_stat)
                for i, n in enumerate(names):
                    for c in range(C):
                        e.wait_ge(s_hi, C * i + c + 1)
                        e.scalar_tensor_tensor(out=wlo[n][:, c, :], in0=raw[i % 2][:, c, :],
                                               scalar=gcol[:, c:c + 1] if folded[n] else 1.0,
                                               in1=whi[n][:, c, :].bitcast(F32), op0=ALU.mult,
                                               op1=ALU.subtract).then_inc(s_lo, 1)
                e.wait_ge(s_emm, 1)
                e.tensor_scalar(padded_i[:, :], ps_e[:, 64:64 + TILES], float(PAIR - 1), None, ALU.add)\
                    .then_inc(s_edge, 1)
                e.tensor_scalar(pad_col_i[0:TILES, :], ps_e[0:TILES, 128:129], float(PAIR - 1), None, ALU.add)\
                    .then_inc(s_edge, 1)
                e.wait_ge(s_edge, 4)
                e.tensor_scalar(padded_i[:, :], padded_i[:, :], 8, 8, ALU.logical_shift_right,
                                ALU.logical_shift_left).then_inc(s_edge, 1)
                e.tensor_scalar(pad_col_i[0:TILES, :], pad_col_i[0:TILES, :], 8, None,
                                ALU.logical_shift_right).then_inc(s_edge, 1)
                e.wait_ge(s_edge, 6)
                e.tensor_copy(padded[:, :], padded_i[:, :]).then_inc(s_edge, 1)
                e.tensor_copy(pad_col[0:TILES, :], pad_col_i[0:TILES, :]).then_inc(s_edge, 1)
                e.wait_ge(s_edge, 8)
                e.tensor_tensor_scan(ends[:, :], ones_e[:, 0:TILES], padded[:, :], 0.0, ALU.mult, ALU.add)\
                    .then_inc(s_edge, 1)
                e.wait_ge(s_emm, 2)
                e.tensor_copy(end_col[0:TILES, :], ps_e2[0:TILES, 0:1]).then_inc(s_edge, 1)
                e.wait_ge(s_edge, 10)
                e.tensor_scalar(past[0:TILES, :], pair_no[0:TILES, :], end_col[0:TILES, :], None, ALU.is_ge)\
                    .then_inc(s_edge, 1)
                e.tensor_tensor(ends[:, :], ends[:, :], padded[:, :], ALU.subtract).then_inc(s_edge, 1)
                e.wait_ge(s_edge, 12)
                e.tensor_tensor(base[:, :], ps_e[:, 0:TILES], ends[:, :], ALU.add).then_inc(s_edge, 1)
                e.wait_ge(s_emm, 3)
                e.tensor_scalar(bucket_of_pair[:, :], ps_e2[0:1, 0:PAIRS], float(TILES - 1), None, ALU.min)\
                    .then_inc(s_edge, 1)

                def rank_bucket(t, s):
                    e.wait_ge(f_rank.sem, f_rank.after(t - 1))
                    e.tensor_scalar(rmatch[0:EP, :], bucket[0:EP, :], bucket_ids[0:EP, bass.ds(t, 1)], None,
                                    ALU.is_equal).then_inc(f_rank.sem, 1)
                    e.wait_ge(f_rank.sem, f_rank.after(t, 1))
                    e.tensor_tensor_scan(rank[0:EP, :], ones_e[0:EP, :], rmatch[0:EP, :],
                                         base[0:EP, bass.ds(t, 1)], ALU.mult, ALU.add).then_inc(f_rank.sem, 1)
                    e.wait_ge(f_rank.sem, f_rank.after(t, 2))
                    e.wait_ge(f_pos.sem, f_pos.freed(t))
                    e.tensor_tensor(placed[s][0:EP, :], rank[0:EP, :], rmatch[0:EP, :], ALU.mult)\
                        .then_inc(f_rank.sem, 1)

                e.wait_ge(s_edge, 14)
                stages(e, TILES, (0, rank_bucket))
                e.wait_ge(f_pos.sem, f_pos.after(TILES - 1))
                e.tensor_scalar(place_i[0:EP, :], pos[0:EP, :], -1.0, None, ALU.add).then_inc(s_rec, 1)
                e.tensor_scalar(records[0:EP, :, 1], srcs[0:EP, :], P - 1, None, ALU.bitwise_and)\
                    .then_inc(s_rec, 1)
                e.tensor_copy(records[0:EP, :, 0], dsts[0:EP, :]).then_inc(s_rec, 1)
                e.wait_ge(s_rec, 3)
                e.tensor_scalar(high[0:EP, :], place_i[0:EP, :], 7, None, ALU.logical_shift_right)\
                    .then_inc(s_rec, 1)
                e.tensor_scalar(place_i[0:EP, :], place_i[0:EP, :], P - 1, None, ALU.bitwise_and)\
                    .then_inc(s_rec, 1)
                e.wait_ge(s_rec, 5)
                e.scalar_tensor_tensor(out=place_i[0:EP, :], in0=place_i[0:EP, :], scalar=float(ETILES),
                                       in1=high[0:EP, :], op0=ALU.mult, op1=ALU.add).then_inc(s_rec, 1)
                e.wait_ge(s_biasmm, 6)
                e.tensor_copy(bias_all[:, :, :], ps_bias[:, :, :]).then_inc(s_biasv, 1)
        S.close()

        B = Scope()
        X = B.two("X", [P, D])
        XN = B.two("XN", [P, D])
        XH = B.two("XH", [P, C, P], F32R)
        XL = B.two("XL", [P, C, P], F32R)
        SO = B.two("SO", [P, D])
        YO = B.two("YO", [P, D])
        QT = B.two("QT", [P, D])
        KT = B.two("KT", [P, D])
        Q = B.two("Q", [P, D])
        K = B.two("K", [P, D])
        V = B.two("V", [P, D])
        PT = [B.ps(f"PT{s}", [P, C, P]) for s in range(2)]
        PB = {n: B.ps(f"PB_{n}", [P, D]) for n in names}

        x_in = transfers("x_in")
        xn_out = transfers("xn_out")
        outs = {n: transfers(f"o_{n}") for n in names}
        f_xn = flow("f_xn")
        f_pt = flow("f_pt")
        f_hi = flow("f_hi")
        f_lo = flow("f_lo")
        f_prod = flow("f_prod", 5)
        f_pre = flow("f_pre", 2)
        f_made = {n: flow(f"f_made_{n}") for n in names}
        f_acc = flow("f_acc", 2)
        f_slot = flow("f_slot", 2)
        scat = transfers("scat", SCAT, credit=0)
        flows = [x_in, xn_out, *outs.values(), f_xn, f_pt, f_hi, f_lo, f_prod, f_pre,
                 *f_made.values(), f_acc, f_slot, scat]
        made_in = {"neigh": YO, "self": SO, "q": Q, "k": K, "v": V}
        stored = {"neigh": y_d, "self": self_d, "q": q_d, "k": k_d, "v": v_d}

        with nc.Block() as block:

            @block.sync
            def _(e):
                give_credit(e, flows)

                def front(t, s):
                    rows = rows_of(t)
                    e.wait_ge(f_xn.sem, f_xn.freed(t))
                    e.dma_start(X[s][0:rows, :], tile_rows(x, t, rows)).then_inc(x_in.sems[s], 16)

                def back(t, s):
                    e.wait_ge(f_xn.sem, f_xn.after(t))
                    e.dma_start(tile_rows(xn_d, t), XN[s][:, :]).then_inc(xn_out.sems[s], 16)
                    for n in names:
                        e.wait_ge(f_made[n].sem, f_made[n].after(t))
                        e.dma_start(tile_rows(stored[n], t), made_in[n][s][:, :]).then_inc(outs[n].sems[s], 16)

                stages(e, TILES, (2, front), (0, back))
                for f in (xn_out, *outs.values()):
                    for s in range(2):
                        e.wait_ge(f.sems[s], f.after(TILES - 1 - s, (TILES - 1 - s) % 2))

            @block.vector
            def _(e):
                def front(t, s):
                    e.wait_ge(x_in.sems[s], x_in.after(t, s))
                    e.wait_ge(xn_out.sems[s], xn_out.freed(t, s))
                    e.tensor_scalar(XN[s][:, :], X[s][:, :], mean_all[:, bass.ds(t, 1)], rs_all[:, bass.ds(t, 1)], ALU.subtract,
                                    ALU.mult).then_inc(f_xn.sem, 1)
                    e.wait_ge(f_pt.sem, f_pt.after(t))
                    e.wait_ge(f_hi.sem, f_hi.after(t))
                    e.tensor_tensor(XL[s][:, :, :], PT[s][:, :, :], XH[s][:, :, :].bitcast(F32), ALU.subtract)\
                        .then_inc(f_lo.sem, 1)

                def back(t, s):
                    e.wait_ge(f_prod.sem, f_prod.after(t, 2))
                    e.wait_ge(outs["self"].sems[s], outs["self"].freed(t, s))
                    e.tensor_tensor(SO[s][:, :], PB["self"][:, :], bias_all[:, 0, :], ALU.add)\
                        .then_inc(f_made["self"].sem, 1)
                    for k, (n, to, fr) in enumerate((("q", QT, f_made["q"]), ("k", KT, f_made["k"]))):
                        e.wait_ge(f_prod.sem, f_prod.after(t, 3 + k))
                        e.wait_ge(fr.sem, fr.freed(t))
                        e.scalar_tensor_tensor(out=to[s][:, :], in0=PB[n][:, :], scalar=r2_all[:, bass.ds(t, 1)],
                                               in1=bias_all[:, 1 + k, :], op0=ALU.mult, op1=ALU.add)\
                            .then_inc(f_pre.sem, 1)
                    e.wait_ge(f_prod.sem, f_prod.after(t, 5))
                    e.wait_ge(outs["v"].sems[s], outs["v"].freed(t, s))
                    e.scalar_tensor_tensor(out=V[s][:, :], in0=PB["v"][:, :], scalar=r2_all[:, bass.ds(t, 1)],
                                           in1=bias_all[:, 3, :], op0=ALU.mult, op1=ALU.add)\
                        .then_inc(f_made["v"].sem, 1)

                def sums(t, s):
                    rows = rows_of(t)
                    e.wait_ge(f_acc.sem, f_acc.after(t - 1))
                    e.wait_ge(f_made["q"].sem, f_made["q"].after(t))
                    e.tensor_tensor(qsum[0:rows, :], qsum[0:rows, :], Q[s][0:rows, :], ALU.add)\
                        .then_inc(f_acc.sem, 1)
                    e.wait_ge(f_made["k"].sem, f_made["k"].after(t))
                    e.tensor_tensor(ksum[0:rows, :], ksum[0:rows, :], K[s][0:rows, :], ALU.add)\
                        .then_inc(f_acc.sem, 1)

                stages(e, TILES, (1, front), (-1, sums), (0, back))

            @block.gpsimd
            def _(e):
                scatter_records(e, rec_d, place_i, records, EP, SCAT, to8, rec8, 0, SCAT_FIRST, scat, f_slot)

            @block.tensor
            def _(e):
                def front(t, s):
                    e.wait_ge(f_xn.sem, f_xn.after(t))
                    e.wait_ge(f_lo.sem, f_lo.freed(t))
                    for c in range(C):
                        mm = e.transpose(PT[s][:, c, :], XN[s][:, c * P:(c + 1) * P], ident[:, :])
                    mm.then_inc(f_pt.sem, 1)

                def back(t, s):
                    e.wait_ge(f_lo.sem, f_lo.after(t))
                    for n in names:
                        ready = {"q": (f_pre, 1), "k": (f_pre, 2)}.get(n, (f_made[n], 1))
                        e.wait_ge(ready[0].sem, ready[0].after(t - 1, ready[1]))
                        split_products(e, PB[n][:, :], XH[s], XL[s], whi[n], wlo[n], C).then_inc(f_prod.sem, 1)

                stages(e, TILES, (1, front), (0, back))

            @block.scalar
            def _(e):
                def front(t, s):
                    e.wait_ge(f_pt.sem, f_pt.after(t))
                    e.wait_ge(f_prod.sem, f_prod.freed(t))
                    e.activation(XH[s][:, :, :], PT[s][:, :, :], ACT.Copy).then_inc(f_hi.sem, 1)

                def back(t, s):
                    e.wait_ge(f_prod.sem, f_prod.after(t, 1))
                    e.wait_ge(outs["neigh"].sems[s], outs["neigh"].freed(t, s))
                    e.activation(YO[s][:, :], PB["neigh"][:, :], ACT.Copy).then_inc(f_made["neigh"].sem, 1)
                    for k, (n, fr, to) in enumerate((("q", QT, Q), ("k", KT, K))):
                        e.wait_ge(f_pre.sem, f_pre.after(t, k + 1))
                        e.wait_ge(outs[n].sems[s], outs[n].freed(t, s))
                        e.wait_ge(f_acc.sem, f_acc.freed(t))
                        e.activation(to[s][:, :], fr[s][:, :], ACT.Sigmoid).then_inc(f_made[n].sem, 1)

                stages(e, TILES, (1, front), (0, back))
        B.close()
        A.close()
        clear_semaphores()

        M = Scope()
        wmix_hi = M.sb("wmix_hi", [P, C, D], F32R)
        wmix_lo = M.sb("wmix_lo", [P, C, D], F32R)
        Cs = Scope()
        Q = Cs.two("Qc", [P, D])
        K = Cs.two("Kc", [P, D])
        V = Cs.two("Vc", [P, D])
        QA = Cs.two("QA", [P, D])
        KA = Cs.two("KA", [P, D])
        QS = Cs.two("QSc", [P, D])
        VE = Cs.two("VE", [P, D])
        q_row = Cs.sb("q_row", [P, D])
        k_row = Cs.sb("k_row", [P, D])
        dots = Cs.two("dots", [P, 2 * H])
        inv = Cs.two("inv", [P, 2 * H])
        si_all = Cs.sb("si_all", [P, TILES * H])
        ex = Cs.two("ex", [P, 2 * H])
        alloc = Cs.two("alloc", [P, H])
        alloc_inv = Cs.two("alloc_inv", [P, H])
        scale8 = Cs.two("scale8", [P, H])
        e_sum = Cs.sb("e_sum", [P, H])
        head_mask = Cs.sb("head_mask", [H, D])
        picked = Cs.sb("picked", [H, 2, D])
        wo_raw = Cs.sb("wo_raw", [P, C, D])
        kv_blocks = Cs.sb("kv_blocks", [P, C, P])
        e_inv = Cs.sb("e_inv", [P, H])
        PQ = Cs.ps("PQ", [P, D])
        PK = Cs.ps("PK", [P, D])
        PSI = Cs.ps("PSI", [P, D])
        PSO = Cs.ps("PSO", [P, D])
        PKV = Cs.ps("PKV", [P, C, P])
        PW = [Cs.ps(f"PW{s}", [P, D]) for s in range(2)]

        s_wo = sem("s_wo")
        s_mask = sem("s_mask")
        s_row = sem("s_row")
        s_rowmm = sem("s_rowmm")
        s_sums = sem("s_sums")
        s_kvn = sem("s_kvn")
        s_wmm = sem("s_wmm")
        s_whi = sem("s_whi")
        s_wlo = sem("s_wlo")
        f_slot = flow("f_slot_b", 2)
        scat = transfers("scat_b", SCAT, credit=0)
        q_in, k_in = transfers("q_in"), transfers("k_in")
        f_sum = flow("f_sum", 6)
        f_use = flow("f_use", 2)
        q_in3, k_in3, v_in3 = transfers("q_in3"), transfers("k_in3"), transfers("v_in3")
        qs_out = transfers("qs_out")
        f_dot = flow("f_dot", 5)
        f_exp = flow("f_exp", 2)
        f_mul = flow("f_mul", 6)
        f_kv = flow("f_kv")
        flows = [f_slot, scat, q_in, k_in, f_sum, f_use, q_in3, k_in3, v_in3, qs_out, f_dot, f_exp, f_mul, f_kv]

        with nc.Block() as block:

            @block.sync
            def _(e):
                give_credit(e, flows)

                def load_sums(t, s):
                    e.wait_ge(f_use.sem, f_use.freed(t))
                    e.dma_start(Q[s][:, :], tile_rows(q_d, t)).then_inc(q_in.sems[s], 16)
                    e.dma_start(K[s][:, :], tile_rows(k_d, t)).then_inc(k_in.sems[s], 16)

                stages(e, TILES, (0, load_sums))
                e.dma_start(wo_raw[:, :, :], Wo.rearrange("(c p) n -> p c n", p=P)).then_inc(s_wo, 16)
                e.wait_ge(f_use.sem, f_use.after(TILES - 1))

                def load_mix(t, s):
                    e.wait_ge(f_kv.sem, f_kv.freed(t))
                    e.wait_ge(f_mul.sem, f_mul.freed(t))
                    e.dma_start(Q[s][:, :], tile_rows(q_d, t)).then_inc(q_in3.sems[s], 16)
                    e.dma_start(K[s][:, :], tile_rows(k_d, t)).then_inc(k_in3.sems[s], 16)
                    e.dma_start(V[s][:, :], tile_rows(v_d, t)).then_inc(v_in3.sems[s], 16)

                def store_qs(t, s):
                    e.wait_ge(f_mul.sem, f_mul.after(t, 4))
                    e.dma_start(tile_rows(qs_d, t), QS[s][:, :]).then_inc(qs_out.sems[s], 16)

                stages(e, TILES, (1, load_mix), (0, store_qs))
                for s in range(2):
                    e.wait_ge(qs_out.sems[s], qs_out.after(TILES - 1 - s, (TILES - 1 - s) % 2))

            @block.gpsimd
            def _(e):
                e.memset(e_sum[:, :], 0.0).then_inc(s_mask, 1)
                e.memset(head_mask[:, :], 1.0).then_inc(s_mask, 1)
                e.wait_ge(s_mask, 2)
                e.affine_select(out=head_mask[:, :], in_=head_mask[:, :], compare_op=ALU.is_ge, fill=0.0, base=0,
                                pattern=[[1, D]], channel_multiplier=-DH).then_inc(s_mask, 1)
                e.wait_ge(s_mask, 3)
                e.affine_select(out=head_mask[:, :], in_=head_mask[:, :], compare_op=ALU.is_ge, fill=0.0,
                                base=DH - 1, pattern=[[-1, D]], channel_multiplier=DH).then_inc(s_mask, 1)
                scatter_records(e, rec_d, place_i, records, EP, SCAT, to8, rec8, SCAT_FIRST, SCAT_TURNS - SCAT_FIRST,
                                scat, f_slot)

            @block.tensor
            def _(e):
                e.matmul(PQ[:, :], ones[:, :], qsum[:, :], start=True, stop=True).then_inc(s_rowmm, 1)
                e.matmul(PK[:, :], ones[:, :], ksum[:, :], start=True, stop=True).then_inc(s_rowmm, 1)
                for bank in (PSI, PSO):
                    e.matmul(bank[0:H, :], zeros[:, 0:H], zeros[:, :], start=True, stop=False)

                def sums(t, s):
                    rows = rows_of(t)
                    last = isinstance(t, int) and t == TILES - 1
                    e.wait_ge(f_sum.sem, f_sum.after(t, 5))
                    e.matmul(PSI[0:H, :], inv[s][0:rows, 0:H], Q[s][0:rows, :], start=False, stop=last)\
                        .then_inc(f_use.sem, 1)
                    e.matmul(PSO[0:H, :], inv[s][0:rows, H:2 * H], K[s][0:rows, :], start=False, stop=last)\
                        .then_inc(f_use.sem, 1)

                stages(e, TILES, (0, sums))
                e.wait_ge(s_sums, 2)
                e.matmul(PQ[:, :], ones[0:H, :], picked[:, 0, :], start=True, stop=True).then_inc(s_rowmm, 1)
                e.matmul(PK[:, :], ones[0:H, :], picked[:, 1, :], start=True, stop=True).then_inc(s_rowmm, 1)
                e.matmul(PKV[:, :, :].rearrange("p c m -> p (c m)"), zeros[:, 0:P], zeros[:, :], start=True,
                         stop=False)

                def kv(t, s):
                    rows = rows_of(t)
                    e.wait_ge(f_mul.sem, f_mul.after(t, 5))
                    for c in range(C):
                        mm = e.matmul(PKV[:, c, :], VE[s][0:rows, c * P:(c + 1) * P],
                                      K[s][0:rows, c * P:(c + 1) * P], start=False, stop=False,
                                      skip_group_check=True)
                    mm.then_inc(f_kv.sem, 1)

                stages(e, TILES, (0, kv))
                e.matmul(PKV[:, :, :].rearrange("p c m -> p (c m)"), zeros[:, 0:P], zeros[:, :], start=False,
                         stop=True)
                e.wait_ge(f_mul.sem, f_mul.after(TILES - 1))
                e.matmul(PSI[:, 0:H], ones[:, :], e_sum[:, :], start=True, stop=True).then_inc(s_rowmm, 1)
                e.wait_ge(s_wo, 16)
                for c in range(C):
                    e.wait_ge(s_kvn, 2 + c + 1)
                    if c >= 2:
                        e.wait_ge(s_wlo, c - 1)
                    e.matmul(PW[c % 2][:, :], kv_blocks[:, c, :], wo_raw[:, c, :], start=True, stop=True)\
                        .then_inc(s_wmm, 1)

            @block.scalar
            def _(e):
                def exps(t, s):
                    e.wait_ge(f_dot.sem, f_dot.after(t))
                    e.activation(ex[s][:, 0:H], dots[s][:, 0:H], ACT.Exp, scale=-1.0).then_inc(f_exp.sem, 1)
                    e.activation(ex[s][:, H:2 * H], dots[s][:, H:2 * H], ACT.Exp).then_inc(f_exp.sem, 1)

                stages(e, TILES, (0, exps))
                for c in range(C):
                    e.wait_ge(s_wmm, c + 1)
                    e.activation(wmix_hi[:, c, :], PW[c % 2][:, :], ACT.Copy).then_inc(s_whi, 1)

            @block.vector
            def _(e):
                e.wait_ge(s_rowmm, 2)
                e.tensor_scalar(q_row[:, :], PQ[:, :], EPS_FLOW, None, ALU.add).then_inc(s_row, 1)
                e.tensor_scalar(k_row[:, :], PK[:, :], EPS_FLOW, None, ALU.add).then_inc(s_row, 1)
                e.wait_ge(s_row, 2)

                def heads(a):
                    return a[:, :].rearrange("p (h d) -> p h d", h=H)

                def dot(t, s, ins, f, k, row_of_q, row_of_k):
                    e.wait_ge(ins[0].sems[s], ins[0].after(t, s))
                    e.wait_ge(ins[1].sems[s], ins[1].after(t, s))
                    for a, b, row in ((QA, Q, row_of_q), (KA, K, row_of_k)):
                        e.scalar_tensor_tensor(out=a[s][:, :], in0=b[s][:, :], scalar=EPS_FLOW, in1=row[:, :],
                                               op0=ALU.add, op1=ALU.mult).then_inc(f.sem, 1)
                    for i, a in enumerate((QA, KA)):
                        e.wait_ge(f.sem, f.after(t, i + 1))
                        e.tensor_reduce(dots[s][:, i * H:(i + 1) * H], heads(a[s]), AX.X, ALU.add)\
                            .then_inc(f.sem, 1)
                    e.wait_ge(f.sem, f.after(t, 4))

                def sums(t, s):
                    dot(t, s, (q_in, k_in), f_sum, 5, k_row, q_row)
                    e.wait_ge(f_use.sem, f_use.freed(t))
                    e.reciprocal(inv[s][:, :], dots[s][:, :]).then_inc(f_sum.sem, 1)
                    e.wait_ge(f_sum.sem, f_sum.after(t, 5))
                    e.tensor_copy(si_all[:, bass.ds(H * t, H)], inv[s][:, 0:H]).then_inc(f_sum.sem, 1)

                stages(e, TILES, (0, sums))
                e.wait_ge(f_use.sem, f_use.after(TILES - 1))
                e.wait_ge(s_mask, 4)
                e.tensor_tensor(picked[:, 0, :], PSI[0:H, :], head_mask[:, :], ALU.mult).then_inc(s_sums, 1)
                e.tensor_tensor(picked[:, 1, :], PSO[0:H, :], head_mask[:, :], ALU.mult).then_inc(s_sums, 1)
                e.wait_ge(s_rowmm, 4)
                e.tensor_scalar(q_row[:, :], PQ[:, :], EPS_FLOW, None, ALU.add).then_inc(s_row, 1)
                e.tensor_scalar(k_row[:, :], PK[:, :], EPS_FLOW, None, ALU.add).then_inc(s_row, 1)
                e.wait_ge(s_row, 4)

                def dots3(t, s):
                    e.wait_ge(f_exp.sem, f_exp.freed(t))
                    dot(t, s, (q_in3, k_in3), f_dot, 5, k_row, q_row)
                    e.tensor_scalar(dots[s][:, H:2 * H], dots[s][:, H:2 * H], -1.0, 1.0, ALU.max, ALU.min)\
                        .then_inc(f_dot.sem, 1)

                def wide(a):
                    return a.unsqueeze(2).broadcast_to([P, H, DH])

                def mix(t, s):
                    rows = rows_of(t)
                    e.wait_ge(f_exp.sem, f_exp.after(t))
                    e.tensor_scalar(alloc[s][:, :], ex[s][:, 0:H], 1.0, None, ALU.add).then_inc(f_mul.sem, 1)
                    e.wait_ge(f_mul.sem, f_mul.after(t, 1))
                    e.reciprocal(alloc_inv[s][:, :], alloc[s][:, :]).then_inc(f_mul.sem, 1)
                    e.wait_ge(f_mul.sem, f_mul.after(t, 2))
                    e.tensor_tensor(scale8[s][:, :], si_all[:, bass.ds(H * t, H)], alloc_inv[s][:, :], ALU.mult)\
                        .then_inc(f_mul.sem, 1)
                    e.wait_ge(f_mul.sem, f_mul.after(t, 3))
                    e.wait_ge(qs_out.sems[s], qs_out.freed(t, s))
                    e.tensor_tensor(heads(QS[s]), heads(Q[s]), wide(scale8[s][:, :]), ALU.mult)\
                        .then_inc(f_mul.sem, 1)
                    e.wait_ge(v_in3.sems[s], v_in3.after(t, s))
                    e.wait_ge(f_kv.sem, f_kv.freed(t))
                    e.tensor_tensor(heads(VE[s]), heads(V[s]), wide(ex[s][:, H:2 * H]), ALU.mult)\
                        .then_inc(f_mul.sem, 1)
                    e.tensor_tensor(e_sum[0:rows, :], e_sum[0:rows, :], ex[s][0:rows, H:2 * H], ALU.add)\
                        .then_inc(f_mul.sem, 1)

                stages(e, TILES, (1, dots3), (0, mix))
                e.wait_ge(s_rowmm, 5)
                e.reciprocal(e_inv[:, :], PSI[:, 0:H]).then_inc(s_kvn, 1)
                e.wait_ge(s_kvn, 1)
                e.tensor_scalar(e_inv[:, :], e_inv[:, :], float(N), None, ALU.mult).then_inc(s_kvn, 1)
                e.wait_ge(s_kvn, 2)
                e.wait_ge(f_kv.sem, f_kv.after(TILES - 1))
                for c in range(C):
                    for h in range(P // DH):
                        r = slice(h * DH, (h + 1) * DH)
                        ins = e.scalar_tensor_tensor(out=kv_blocks[r, c, :], in0=PKV[r, c, :],
                                                     scalar=e_inv[r, c * (P // DH) + h:c * (P // DH) + h + 1],
                                                     in1=block_mask[r, :], op0=ALU.mult, op1=ALU.mult)
                    ins.then_inc(s_kvn, 1)
                for c in range(C):
                    e.wait_ge(s_whi, c + 1)
                    e.tensor_tensor(wmix_lo[:, c, :], PW[c % 2][:, :], wmix_hi[:, c, :].bitcast(F32),
                                    ALU.subtract).then_inc(s_wlo, 1)
        Cs.close()

        R = Scope()
        agg = R.sb("agg", [P, TILES * D])
        Ds = Scope()
        GRP = 8
        turns = ETILES // GRP
        table = Ds.sb("table", [P, ETILES, 2], I32)
        row_f = Ds.sb("row_f", [P, ETILES])
        columns = Ds.sb("columns", [P, P])
        from8 = Ds.two("from8", [P, GRP], I32)
        gathered = [[Ds.sb(f"gathered{s}_{j}", [P, D]) for j in range(GRP)] for s in range(2)]
        onehot = Ds.two("onehot", [P, GRP, P])
        PA = [[Ds.ps(f"PA{s}_{p}", [P, D]) for p in range(GRP // 2)] for s in range(2)]
        s_table = sem("s_table")
        s_agg = sem("s_agg")
        s_cols = sem("s_cols")
        s_rowf = sem("s_rowf")
        f_from = flow("f_from")
        g_in = [transfers(f"g_in{j}_", credit=0) for j in range(GRP)]
        f_hot = flow("f_hot")
        f_emm = flow("f_emm", GRP // 2)
        f_add = flow("f_add", GRP // 2)
        flows = [f_from, *g_in, f_hot, f_emm, f_add]

        with nc.Block() as block:

            @block.sync
            def _(e):
                give_credit(e, flows)
                e.dma_start(table[:, :, :].rearrange("p t w -> p (t w)"),
                            rec_d.rearrange("(p t) w -> p (t w)", p=P)).then_inc(s_table, 16)
                e.dma_start(agg[:, :].rearrange("p (t d) -> p t d", d=D),
                            self_d.rearrange("(t p) d -> p t d", p=P)).then_inc(s_agg, 16)

            @block.gpsimd
            def _(e):
                e.iota(columns[:, :], pattern=[[1, P]], base=0, channel_multiplier=0,
                       allow_small_or_imprecise_dtypes=True).then_inc(s_cols, 1)
                e.wait_ge(s_table, 16)

                def gather(t, s):
                    e.wait_ge(f_emm.sem, f_emm.freed(t))
                    e.tensor_copy(from8[s][:, :], table[:, bass.ds(GRP * t, GRP), 0]).then_inc(f_from.sem, 1)
                    e.wait_ge(f_from.sem, f_from.after(t))
                    e.tensor_tensor(pace[:, 1:2], zeros[:, 0:1], zeros[:, 1:2], ALU.add)
                    for j in range(GRP):
                        e.indirect_dma_start(gathered[s][j][:, :], None, y_d,
                                             bass.IndirectOffsetOnAxis(from8[s][:, j:j + 1], 0))\
                            .then_inc(g_in[j].sems[s], 16)

                stages(e, turns, (0, gather))

            @block.tensor
            def _(e):
                def spread(t, s):
                    e.wait_ge(f_hot.sem, f_hot.after(t))
                    e.wait_ge(f_add.sem, f_add.freed(t))
                    for j in range(GRP):
                        e.wait_ge(g_in[j].sems[s], g_in[j].after(t, s))
                        mm = e.matmul(PA[s][j // 2][:, :], onehot[s][:, j, :], gathered[s][j][:, :],
                                      start=(j % 2 == 0), stop=(j % 2 == 1))
                        if j % 2:
                            mm.then_inc(f_emm.sem, 1)

                stages(e, turns, (0, spread))

            @block.vector
            def _(e):
                e.wait_ge(s_table, 16)
                e.tensor_copy(row_f[:, :], table[:, :, 1]).then_inc(s_rowf, 1)
                e.wait_ge(s_rowf, 1)
                e.wait_ge(s_cols, 1)
                e.wait_ge(s_agg, 16)

                def hot(t, s):
                    e.wait_ge(f_emm.sem, f_emm.freed(t))
                    e.tensor_tensor(onehot[s][:, :, :], columns[:, :].unsqueeze(1).broadcast_to([P, GRP, P]),
                                    row_f[:, bass.ds(GRP * t, GRP)].unsqueeze(2).broadcast_to([P, GRP, P]),
                                    ALU.is_equal).then_inc(f_hot.sem, 1)

                def add(t, s):
                    for p in range(GRP // 2):
                        b = e.value_load(bucket_of_pair[0:1, bass.ds(GRP // 2 * t + p, 1)], min_val=0,
                                         max_val=TILES - 1)
                        rows = agg[:, bass.ds(b * D, D)]
                        e.wait_ge(f_add.sem, f_add.after(t, p) if p else f_add.after(t - 1))
                        e.wait_ge(f_emm.sem, f_emm.after(t, p + 1))
                        e.tensor_tensor(rows, rows, PA[s][p][:, :], ALU.add).then_inc(f_add.sem, 1)

                stages(e, turns, (1, hot), (0, add))
        Ds.close()
        clear_semaphores()

        Es = Scope()
        w1_hi = Es.sb("w1_hi", [P, C, HID], F32R)
        w1_lo = Es.sb("w1_lo", [P, C, HID], F32R)
        w2_hi = Es.sb("w2_hi", [P, HC, D], F32R)
        w2_lo = Es.sb("w2_lo", [P, HC, D], F32R)
        b1_col = Es.sb("b1_col", [P, HC])
        rows2 = Es.sb("rows2", [P, 2, D])
        Es1 = Scope()
        raw1 = Es1.sb("w1_raw", [P, C, HID])
        raw2 = Es1.sb("w2_raw", [P, HC, D])
        g2col = Es1.sb("g2col", [P, C])
        be2col = Es1.sb("be2col", [P, C])
        b1raw = Es1.sb("b1raw", [P, HC])
        brow2 = Es1.sb("brow2", [1, 2, D])
        PR = Es1.ps("PR", [P, 2, D])
        PR2 = Es1.ps("PR2", [P, D])
        s_in4 = sem("s_in4")
        s_mm4 = sem("s_mm4")
        s_hi4 = sem("s_hi4")
        s_v4 = sem("s_v4")

        with nc.Block() as block:

            @block.sync
            def _(e):
                e.dma_start(raw1[:, :, :], W1.rearrange("(c p) n -> p c n", p=P)).then_inc(s_in4, 16)
                e.dma_start(raw2[:, :, :], W2.rearrange("(c p) n -> p c n", p=P)).then_inc(s_in4, 16)
                e.dma_start(g2col[:, :], g2).then_inc(s_in4, 16)
                e.dma_start(be2col[:, :], be2).then_inc(s_in4, 16)
                e.dma_start(b1raw[:, :], b1).then_inc(s_in4, 16)
                e.dma_start(brow2[:, 0, :], bo.rearrange("(a n) -> a n", a=1)).then_inc(s_in4, 16)
                e.dma_start(brow2[:, 1, :], b2.rearrange("(a n) -> a n", a=1)).then_inc(s_in4, 16)

            @block.tensor
            def _(e):
                e.wait_ge(s_in4, 16 * 7)
                for i in range(2):
                    e.matmul(PR[:, i, :], ones[0:1, :], brow2[:, i, :], start=True, stop=True)
                for m in range(HC):
                    for c in range(C):
                        mm = e.matmul(PR2[:, m:m + 1], raw1[:, c, m * P:(m + 1) * P], be2col[:, c:c + 1],
                                      start=(c == 0), stop=(c == C - 1))
                mm.then_inc(s_mm4, 1)

            @block.scalar
            def _(e):
                e.wait_ge(s_in4, 16 * 7)
                for c in range(C):
                    e.activation(w1_hi[:, c, :], raw1[:, c, :], ACT.Copy, scale=g2col[:, c:c + 1])\
                        .then_inc(s_hi4, 1)
                for c in range(HC):
                    e.activation(w2_hi[:, c, :], raw2[:, c, :], ACT.Copy).then_inc(s_hi4, 1)

            @block.vector
            def _(e):
                e.wait_ge(s_in4, 16 * 7)
                e.wait_ge(s_hi4, C + HC)
                for c in range(C):
                    e.scalar_tensor_tensor(out=w1_lo[:, c, :], in0=raw1[:, c, :], scalar=g2col[:, c:c + 1],
                                           in1=w1_hi[:, c, :].bitcast(F32), op0=ALU.mult, op1=ALU.subtract)
                e.tensor_tensor(w2_lo[:, :, :], raw2[:, :, :], w2_hi[:, :, :].bitcast(F32), ALU.subtract)
                e.wait_ge(s_mm4, 1)
                e.tensor_tensor(b1_col[:, :], b1raw[:, :], PR2[:, 0:HC], ALU.add)
                e.tensor_copy(rows2[:, :, :], PR[:, :, :]).then_inc(s_v4, 1)
        Es1.close()

        X = Es.two("Xe", [P, D])
        Y = Es.two("Ye", [P, D])
        QS = Es.two("QSe", [P, D])
        U = Es.two("Ue", [P, D])
        QH = Es.two("QH", [P, C, P], F32R)
        QL = Es.two("QL", [P, C, P], F32R)
        UH = Es.two("UH", [P, C, P], F32R)
        UL = Es.two("UL", [P, C, P], F32R)
        HG = Es.two("HG", [P, HC, P])
        HH = Es.two("HH", [P, HC, P], F32R)
        HL = Es.two("HL", [P, HC, P], F32R)
        stats = Es.two("stats_e", [P, 6])
        mv = Es.two("mv_e", [P, 2])
        rs = Es.two("rs_e", [P, 1])
        sc = Es.sb("sc_e", [P, 1])
        PTQ = [Es.ps(f"PTQ{s}", [P, C, P]) for s in range(2)]
        PTU = [Es.ps(f"PTU{s}", [P, C, P]) for s in range(2)]
        PO = Es.ps("PO", [P, D])
        PH = Es.ps("PH", [P, HC, P])
        PF = Es.ps("PF", [P, D])
        x_in, xn_in, qs_in, x1_out = transfers("x_in4"), transfers("xn_in4"), transfers("qs_in4"), transfers("x1_out")
        f_tq = flow("f_tq")
        f_qh = flow("f_qh")
        f_ql = flow("f_ql")
        f_po = flow("f_po")
        f_xnb = flow("f_xnb")
        f_y = flow("f_y")
        f_st = flow("f_st")
        f_mv = flow("f_mv4")
        f_rs = flow("f_rs4", 2)
        f_u = flow("f_u")
        f_tu = flow("f_tu")
        f_uh = flow("f_uh")
        f_ul = flow("f_ul")
        f_ph = flow("f_ph")
        f_hg = flow("f_hg", HC)
        f_hh = flow("f_hh")
        f_hl = flow("f_hl")
        f_pf = flow("f_pf")
        f_relu = flow("f_relu")
        f_sum = flow("f_sum4", 2)
        f_x1 = flow("f_x1")
        f_st1 = flow("f_st1")
        flows = [x_in, xn_in, qs_in, x1_out, f_tq, f_qh, f_ql, f_po, f_xnb, f_y, f_st, f_mv, f_rs, f_u, f_tu, f_uh,
                 f_ul, f_ph, f_hg, f_hh, f_hl, f_pf, f_relu, f_sum, f_x1, f_st1]

        with nc.Block() as block:

            @block.sync
            def _(e):
                give_credit(e, flows)

                def load(t, s):
                    rows = rows_of(t)
                    e.wait_ge(f_tq.sem, f_tq.freed(t))
                    e.dma_start(QS[s][:, :], tile_rows(qs_d, t)).then_inc(qs_in.sems[s], 16)
                    e.wait_ge(f_u.sem, f_u.freed(t))
                    e.wait_ge(f_sum.sem, f_sum.freed(t))
                    e.dma_start(Y[s][:, :], tile_rows(xn_d, t)).then_inc(xn_in.sems[s], 16)
                    e.wait_ge(x1_out.sems[s], x1_out.freed(t, s))
                    e.wait_ge(f_st1.sem, f_st1.freed(t))
                    e.dma_start(X[s][0:rows, :], tile_rows(x, t, rows)).then_inc(x_in.sems[s], 16)

                def store(t, s):
                    e.wait_ge(f_x1.sem, f_x1.after(t))
                    e.dma_start(tile_rows(x1_d, t), X[s][:, :]).then_inc(x1_out.sems[s], 16)

                stages(e, TILES, (1, load), (0, store))
                for s in range(2):
                    e.wait_ge(x1_out.sems[s], x1_out.after(TILES - 1 - s, (TILES - 1 - s) % 2))

            @block.gpsimd
            def _(e):
                def front(t, s):
                    e.wait_ge(xn_in.sems[s], xn_in.after(t, s))
                    e.tensor_tensor(Y[s][:, :], Y[s][:, :], rows2[:, 0, :], ALU.add).then_inc(f_xnb.sem, 1)
                    e.wait_ge(f_mv.sem, f_mv.after(t))
                    e.tensor_tensor(sc[:, :], mv[s][:, 1:2], eps_c, ALU.add).then_inc(f_rs.sem, 1)
                    e.wait_ge(f_rs.sem, f_rs.after(t, 1))
                    e.tensor_tensor(rs[s][:, :], sc[:, :], mhalf, ALU.pow).then_inc(f_rs.sem, 1)

                def back(t, s):
                    e.wait_ge(f_relu.sem, f_relu.after(t))
                    e.tensor_tensor(X[s][:, :], X[s][:, :], Y[s][:, :], ALU.add).then_inc(f_sum.sem, 1)
                    e.wait_ge(f_sum.sem, f_sum.after(t, 1))
                    e.tensor_tensor(X[s][:, :], X[s][:, :], rows2[:, 1, :], ALU.add).then_inc(f_sum.sem, 1)

                stages(e, TILES, (1, front), (0, back))

            @block.tensor
            def _(e):
                def front(t, s):
                    e.wait_ge(qs_in.sems[s], qs_in.after(t, s))
                    e.wait_ge(f_ql.sem, f_ql.freed(t))
                    for c in range(C):
                        mm = e.transpose(PTQ[s][:, c, :], QS[s][:, c * P:(c + 1) * P], ident[:, :])
                    mm.then_inc(f_tq.sem, 1)
                    e.wait_ge(f_ql.sem, f_ql.after(t))
                    e.wait_ge(f_y.sem, f_y.after(t - 1))
                    split_products(e, PO[:, :], QH[s], QL[s], wmix_hi, wmix_lo, C).then_inc(f_po.sem, 1)

                def back(t, s):
                    e.wait_ge(f_u.sem, f_u.after(t))
                    e.wait_ge(f_ul.sem, f_ul.freed(t))
                    for c in range(C):
                        mm = e.transpose(PTU[s][:, c, :], U[s][:, c * P:(c + 1) * P], ident[:, :])
                    mm.then_inc(f_tu.sem, 1)
                    e.wait_ge(f_ul.sem, f_ul.after(t))
                    e.wait_ge(f_hg.sem, f_hg.after(t - 1))
                    for m in range(HC):
                        mm = split_products(e, PH[:, m, :], w1_hi[:, :, m * P:(m + 1) * P],
                                            w1_lo[:, :, m * P:(m + 1) * P], UH[s], UL[s], C)
                    mm.then_inc(f_ph.sem, 1)
                    e.wait_ge(f_hl.sem, f_hl.after(t))
                    e.wait_ge(f_x1.sem, f_x1.after(t - 1))
                    split_products(e, PF[:, :], HH[s], HL[s], w2_hi, w2_lo, HC).then_inc(f_pf.sem, 1)

                stages(e, TILES, (1, front), (0, back))

            @block.scalar
            def _(e):
                def front(t, s):
                    e.wait_ge(f_tq.sem, f_tq.after(t))
                    e.wait_ge(f_po.sem, f_po.freed(t))
                    e.activation(QH[s][:, :, :], PTQ[s][:, :, :], ACT.Copy).then_inc(f_qh.sem, 1)

                def back(t, s):
                    e.wait_ge(f_tu.sem, f_tu.after(t))
                    e.wait_ge(f_ph.sem, f_ph.freed(t))
                    e.activation(UH[s][:, :, :], PTU[s][:, :, :], ACT.Copy).then_inc(f_uh.sem, 1)
                    e.wait_ge(f_ph.sem, f_ph.after(t))
                    e.wait_ge(f_hl.sem, f_hl.freed(t))
                    for m in range(HC):
                        e.activation(HG[s][:, m, :], PH[:, m, :], ACT.Gelu, bias=b1_col[:, m:m + 1])\
                            .then_inc(f_hg.sem, 1)
                    e.wait_ge(f_hg.sem, f_hg.after(t))
                    e.wait_ge(f_pf.sem, f_pf.freed(t))
                    e.activation(HH[s][:, :, :], HG[s][:, :, :], ACT.Copy).then_inc(f_hh.sem, 1)

                stages(e, TILES, (1, front), (0, back))

            @block.vector
            def _(e):
                def front(t, s):
                    e.wait_ge(f_qh.sem, f_qh.after(t))
                    e.tensor_tensor(QL[s][:, :, :], PTQ[s][:, :, :], QH[s][:, :, :].bitcast(F32), ALU.subtract)\
                        .then_inc(f_ql.sem, 1)
                    e.wait_ge(x_in.sems[s], x_in.after(t, s))
                    e.scalar_tensor_tensor(out=X[s][:, :], in0=agg[:, bass.ds(t * D, D)], scalar=0.0,
                                           in1=X[s][:, :], op0=ALU.max, op1=ALU.add).then_inc(f_relu.sem, 1)
                    e.wait_ge(f_po.sem, f_po.after(t))
                    e.wait_ge(f_xnb.sem, f_xnb.after(t))
                    e.tensor_tensor(Y[s][:, :], PO[:, :], Y[s][:, :], ALU.add).then_inc(f_y.sem, 1)
                    e.wait_ge(f_y.sem, f_y.after(t))
                    e.bn_stats(stats[s][:, :], Y[s][:, :]).then_inc(f_st.sem, 1)
                    e.wait_ge(f_st.sem, f_st.after(t))
                    e.memset(pace[:, 0:1], 0.0)
                    e.bn_aggr(mv[s][:, :], stats[s][:, :]).then_inc(f_mv.sem, 1)
                    e.wait_ge(f_rs.sem, f_rs.after(t))
                    e.wait_ge(f_tu.sem, f_tu.freed(t))
                    e.tensor_scalar(U[s][:, :], Y[s][:, :], mv[s][:, 0:1], rs[s][:, :], ALU.subtract, ALU.mult)\
                        .then_inc(f_u.sem, 1)

                def back(t, s):
                    e.wait_ge(f_uh.sem, f_uh.after(t))
                    e.tensor_tensor(UL[s][:, :, :], PTU[s][:, :, :], UH[s][:, :, :].bitcast(F32), ALU.subtract)\
                        .then_inc(f_ul.sem, 1)
                    e.wait_ge(f_hh.sem, f_hh.after(t))
                    e.tensor_tensor(HL[s][:, :, :], HG[s][:, :, :], HH[s][:, :, :].bitcast(F32), ALU.subtract)\
                        .then_inc(f_hl.sem, 1)
                    e.wait_ge(f_pf.sem, f_pf.after(t))
                    e.wait_ge(f_sum.sem, f_sum.after(t))
                    e.tensor_tensor(X[s][:, :], PF[:, :], X[s][:, :], ALU.add).then_inc(f_x1.sem, 1)
                    e.wait_ge(f_x1.sem, f_x1.after(t))
                    e.bn_stats(stats1[:, bass.ds(t, 1), :].rearrange("p t k -> p (t k)"), X[s][:, :])\
                        .then_inc(f_st1.sem, 1)

                stages(e, TILES, (1, front), (0, back))
        Es.close()
        R.close()
        M.close()
        Held.close()

        clear_semaphores()

        GROUPS = EXPERTS + 1
        J = 2 * TILES
        ST = (2 * NP + EXPERTS * (P - 1) + P - 1) // P
        ST += ST % 2
        list_d = dram("list_d", [P * ST, 2], I32)
        ysl_d = dram("ysl_d", [ST * P, D])
        z_d = dram("z_d", [NP, D])

        Fs = Scope()
        logits = Fs.sb("logits", [P, TILES, EXPERTS])
        slot_i = Fs.sb("slot_i", [P, J], I32)
        expert_of_tile = Fs.sb("expert_of_tile", [1, ST], I32)

        F1 = Scope()
        wr_raw = F1.sb("wr_raw", [P, C, EXPERTS])
        wr_hi = F1.sb("wr_hi", [P, C, EXPERTS], F32R)
        wr_lo = F1.sb("wr_lo", [P, C, EXPERTS], F32R)
        br_raw = F1.sb("br_raw", [1, EXPERTS])
        br_rows = F1.sb("br_rows", [P, EXPERTS])
        mean1 = F1.sb("mean1", [P, TILES])
        var1 = F1.sb("var1", [P, TILES])
        tmp1 = F1.sb("tmp1", [P, TILES])
        rs1 = F1.sb("rs1", [P, TILES])
        X = F1.two("Xr", [P, D])
        Z = F1.two("Zr", [P, D])
        ZH = F1.two("ZHr", [P, C, P], F32R)
        ZL = F1.two("ZLr", [P, C, P], F32R)
        PTZ = [F1.ps(f"PTZr{s}", [P, C, P]) for s in range(2)]
        PLG = [F1.ps(f"PLG{s}", [P, D]) for s in range(2)]
        PBR = F1.ps("PBR", [P, D])
        s_wr = sem("s_wr")
        s_wrs = sem("s_wrs")
        s_brmm = sem("s_brmm")
        s_st1 = sem("s_st1")
        s_pow1 = sem("s_pow1")
        x_in, z_out = transfers("x_in5"), transfers("z_out")
        f_z = flow("f_z")
        f_tz = flow("f_tz")
        f_zh = flow("f_zh")
        f_zl = flow("f_zl")
        f_lg = flow("f_lg")
        f_la = flow("f_la")
        flows = [x_in, z_out, f_z, f_tz, f_zh, f_zl, f_lg, f_la]

        with nc.Block() as block:

            @block.sync
            def _(e):
                give_credit(e, flows)
                e.dma_start(wr_raw[:, :, :], Wr.rearrange("(c p) n -> p c n", p=P)).then_inc(s_wr, 16)
                e.dma_start(br_raw[:, :], br.rearrange("(a n) -> a n", a=1)).then_inc(s_wr, 16)

                def load(t, s):
                    e.wait_ge(f_z.sem, f_z.freed(t))
                    e.dma_start(X[s][:, :], tile_rows(x1_d, t)).then_inc(x_in.sems[s], 16)

                def store(t, s):
                    e.wait_ge(f_z.sem, f_z.after(t))
                    e.dma_start(tile_rows(z_d, t), Z[s][:, :]).then_inc(z_out.sems[s], 16)

                stages(e, TILES, (4, load), (2, store))
                for s in range(2):
                    e.wait_ge(z_out.sems[s], z_out.after(TILES - 1 - s, (TILES - 1 - s) % 2))

            @block.gpsimd
            def _(e):
                e.wait_ge(s_st1, STATISTICS_OPS)
                e.tensor_tensor(tmp1[:, :], var1[:, :], eps_c.broadcast_to([P, TILES]), ALU.add)\
                    .then_inc(s_pow1, 1)
                e.wait_ge(s_pow1, 1)
                e.tensor_tensor(rs1[:, :], tmp1[:, :], mhalf.broadcast_to([P, TILES]), ALU.pow)\
                    .then_inc(s_pow1, 1)

            @block.tensor
            def _(e):
                e.wait_ge(s_wr, 32)
                e.matmul(PBR[:, 0:EXPERTS], ones[0:1, :], br_raw[:, :], start=True, stop=True).then_inc(s_brmm, 1)
                e.wait_ge(s_wrs, 2)

                def turned(t, s):
                    e.wait_ge(f_z.sem, f_z.after(t))
                    e.wait_ge(f_zl.sem, f_zl.freed(t))
                    for c in range(C):
                        mm = e.transpose(PTZ[s][:, c, :], Z[s][:, c * P:(c + 1) * P], ident[:, :])
                    mm.then_inc(f_tz.sem, 1)

                def products(t, s):
                    e.wait_ge(f_zl.sem, f_zl.after(t))
                    e.wait_ge(f_la.sem, f_la.freed(t))
                    split_products(e, PLG[s][:, 0:EXPERTS], ZH[s], ZL[s], wr_hi, wr_lo, C).then_inc(f_lg.sem, 1)

                stages(e, TILES, (1, turned), (0, products))

            @block.scalar
            def _(e):
                e.wait_ge(s_wr, 32)
                e.activation(wr_hi[:, :, :], wr_raw[:, :, :], ACT.Copy).then_inc(s_wrs, 1)

                def high_part(t, s):
                    e.wait_ge(f_tz.sem, f_tz.after(t))
                    e.wait_ge(f_lg.sem, f_lg.freed(t))
                    e.activation(ZH[s][:, :, :], PTZ[s][:, :, :], ACT.Copy).then_inc(f_zh.sem, 1)

                stages(e, TILES, (1, high_part))

            @block.vector
            def _(e):
                row_statistics(e, stats1, mean1, var1, tmp1, s_st1)
                e.wait_ge(s_wrs, 1)
                e.tensor_tensor(wr_lo[:, :, :], wr_raw[:, :, :], wr_hi[:, :, :].bitcast(F32), ALU.subtract)\
                    .then_inc(s_wrs, 1)
                e.wait_ge(s_brmm, 1)
                e.tensor_copy(br_rows[:, :], PBR[:, 0:EXPERTS]).then_inc(s_brmm, 1)
                e.wait_ge(s_brmm, 2)
                e.wait_ge(s_pow1, 2)

                def normal(t, s):
                    e.wait_ge(x_in.sems[s], x_in.after(t, s))
                    e.wait_ge(f_tz.sem, f_tz.freed(t))
                    e.wait_ge(z_out.sems[s], z_out.freed(t, s))
                    e.tensor_scalar(Z[s][:, :], X[s][:, :], mean1[:, bass.ds(t, 1)], rs1[:, bass.ds(t, 1)],
                                    ALU.subtract, ALU.mult).then_inc(f_z.sem, 1)

                def low_part(t, s):
                    e.wait_ge(f_zh.sem, f_zh.after(t))
                    e.tensor_tensor(ZL[s][:, :, :], PTZ[s][:, :, :], ZH[s][:, :, :].bitcast(F32), ALU.subtract)\
                        .then_inc(f_zl.sem, 1)

                def with_bias(t, s):
                    e.wait_ge(f_lg.sem, f_lg.after(t))
                    e.tensor_tensor(logits[:, bass.ds(t, 1), :].rearrange("p t n -> p (t n)"),
                                    PLG[s][:, 0:EXPERTS], br_rows[:, :], ALU.add).then_inc(f_la.sem, 1)

                stages(e, TILES, (2, normal), (1, low_part), (0, with_bias))
        F1.close()
        clear_semaphores()

        W = Scope()
        e1_hi = W.sb("e1_hi", [P, EXPERTS, C, HID], F32R)
        e1_lo = W.sb("e1_lo", [P, EXPERTS, C, HID], F32R)
        e2_hi = W.sb("e2_hi", [P, EXPERTS, HC, D], F32R)
        e2_lo = W.sb("e2_lo", [P, EXPERTS, HC, D], F32R)
        e1b_rows = W.sb("e1b_rows", [P, EXPERTS, HID])
        e2b_rows = W.sb("e2b_rows", [P, EXPERTS, D])
        F2 = Scope()
        rawm = F2.two("rawm", [P, C * HID])
        e1b_sb = F2.sb("e1b_sb", [EXPERTS, HID])
        e2b_sb = F2.sb("e2b_sb", [EXPERTS, D])
        row_of = F2.sb("row_of", [EXPERTS, EXPERTS, P])
        number = F2.sb("number", [P, GROUPS])
        number_past = F2.sb("number_past", [P, EXPERTS])
        tile_start = F2.sb("tile_start", [1, ST])
        prob = F2.sb("prob", [P, TILES, EXPERTS])
        same = F2.sb("same", [P, TILES, EXPERTS])
        place_no = F2.sb("place_no", [P, TILES, EXPERTS])
        most = F2.sb("most", [P, TILES])
        weight = F2.sb("weight", [P, TILES, 2])
        choice = F2.sb("choice", [P, TILES, 2])
        member = F2.sb("member", [P, GROUPS, J])
        running = F2.sb("running", [P, GROUPS, J])
        going_on = F2.sb("going_on", [P, GROUPS, J])
        totals = F2.sb("totals", [P, GROUPS])
        totals_i = F2.sb("totals_i", [P, GROUPS], I32)
        ends9 = F2.sb("ends9", [P, GROUPS])
        base9 = F2.sb("base9", [P, GROUPS])
        slot_f = F2.sb("slot_f", [P, J])
        place9 = F2.sb("place9", [P, J], I32)
        high9 = F2.sb("high9", [P, J], I32)
        tile_past = F2.sb("tile_past", [1, ST, EXPERTS])
        tile_expert = F2.sb("tile_expert", [1, ST])
        tokens = F2.sb("tokens", [P, J, 2], I32)
        upper2 = F2.sb("upper2", [P, P])
        nothing = F2.sb("nothing", [P, ST * 2], I32)
        ONCE = 7
        to_m = F2.two("to_m", [P, ONCE], I32)
        rec_m = F2.two("rec_m", [P, 2 * ONCE], I32)
        PBB = [F2.ps(f"PBB{s}", [P, D]) for s in range(4)]
        PCT = F2.ps("PCT", [P, D])
        s_in6 = [sem(f"s_in6{s}") for s in range(2)]
        s_small6 = sem("s_small6")
        s_hi6 = sem("s_hi6")
        s_lo6 = sem("s_lo6")
        s_c6 = sem("s_c6")
        s_rows6 = sem("s_rows6")
        s_rows6c = sem("s_rows6c")
        s_fill = sem("s_fill")
        s_exp = sem("s_exp")
        s_tail = sem("s_tail")
        s_cnt = sem("s_cnt")
        s_rt = sem("s_rt")
        s_place = sem("s_place")
        f_slotm = flow("f_slotm", 2)
        scat_m = transfers("scat_m", ONCE, credit=0)
        loads = [(e1_hi, e1_lo, E1, n) for n in range(EXPERTS)] + [(e2_hi, e2_lo, E2, n) for n in range(EXPERTS)]

        with nc.Block() as block:

            @block.sync
            def _(e):
                give_credit(e, [f_slotm])
                e.wait_ge(s_c6, 1)
                e.dma_start(list_d.rearrange("(p t) w -> p (t w)", p=P), nothing[:, :]).then_inc(s_fill, 16)
                e.dma_start(e1b_sb[:, :], e1b).then_inc(s_small6, 16)
                e.dma_start(e2b_sb[:, :], e2b).then_inc(s_small6, 16)
                for i, (_, _, w, n) in enumerate(loads):
                    if i >= 2:
                        e.wait_ge(s_lo6, i - 1)
                    e.dma_start(rawm[i % 2][:, :].rearrange("p (c n) -> p c n", n=w.shape[2]),
                                w[n].rearrange("(c p) n -> p c n", p=P)).then_inc(s_in6[i % 2], 16)

            @block.gpsimd
            def _(e):
                e.memset(nothing[:, :], 0).then_inc(s_c6, 1)
                e.memset(going_on[:, :, :], 1.0).then_inc(s_c6, 1)
                e.memset(row_of[:, :, :], 0.0).then_inc(s_c6, 1)
                e.iota(number[:, :], pattern=[[1, GROUPS]], base=0, channel_multiplier=0,
                       allow_small_or_imprecise_dtypes=True).then_inc(s_c6, 1)
                e.iota(number_past[:, :], pattern=[[1, EXPERTS]], base=EXPERTS, channel_multiplier=0,
                       allow_small_or_imprecise_dtypes=True).then_inc(s_c6, 1)
                e.iota(tile_start[:, :], pattern=[[P, ST]], base=0, channel_multiplier=0,
                       allow_small_or_imprecise_dtypes=True).then_inc(s_c6, 1)
                e.iota(tokens[:, :, 0].rearrange("p (t k) -> p t k", k=2), pattern=[[P, TILES], [0, 2]], base=0,
                       channel_multiplier=1).then_inc(s_c6, 1)
                e.affine_select(out=upper2[:, :], in_=ones[:, :], compare_op=ALU.is_gt, fill=0.0, base=0,
                                pattern=[[1, P]], channel_multiplier=-1).then_inc(s_c6, 1)
                e.wait_ge(s_c6, 8)
                e.memset(going_on[:, :, 0:1], 0.0).then_inc(s_c6, 1)
                e.affine_select(out=row_of[:, :, :], in_=row_of[:, :, :], compare_op=ALU.not_equal, fill=1.0,
                                base=0, pattern=[[-1, EXPERTS], [0, P]], channel_multiplier=1).then_inc(s_c6, 1)
                e.wait_ge(s_rt, CHOSEN)
                e.affine_select(out=choice[:, TILES - 1, :], in_=choice[:, TILES - 1, :], compare_op=ALU.is_ge,
                                fill=float(EXPERTS), base=TAIL - 1, pattern=[[0, 2]], channel_multiplier=-1)\
                    .then_inc(s_tail, 1)
                e.wait_ge(s_place, 1)
                e.wait_ge(s_fill, 16)
                scatter_records(e, list_d, place9, tokens, P, ONCE, to_m, rec_m, 0, J // ONCE, scat_m, f_slotm)

            @block.tensor
            def _(e):
                e.wait_ge(s_small6, 32)
                e.wait_ge(s_c6, 10)
                for i in range(EXPERTS // 2 + EXPERTS):
                    if i >= 4:
                        e.wait_ge(s_rows6c, i - 3)
                    if i < EXPERTS // 2:
                        e.matmul(PBB[i % 4][:, 0:HID], row_of[:, 2 * i, :], e1b_sb[:, :], start=True, stop=True)
                        e.matmul(PBB[i % 4][:, HID:2 * HID], row_of[:, 2 * i + 1, :], e1b_sb[:, :], start=True,
                                 stop=True).then_inc(s_rows6, 1)
                    else:
                        e.matmul(PBB[i % 4][:, :], row_of[:, i - EXPERTS // 2, :], e2b_sb[:, :], start=True,
                                 stop=True).then_inc(s_rows6, 1)
                e.wait_ge(s_rt, COUNTED)
                e.matmul(PCT[:, 0:GROUPS], upper2[:, :], totals[:, :], start=True, stop=True)
                e.matmul(PCT[:, 64:64 + GROUPS], ones[:, :], totals[:, :], start=True, stop=True).then_inc(s_cnt, 1)

            @block.scalar
            def _(e):
                e.wait_ge(s_rt, 2)
                e.activation(prob[:, :, :], prob[:, :, :], ACT.Exp).then_inc(s_exp, 1)
                for i in range(EXPERTS // 2 + EXPERTS):
                    e.wait_ge(s_rows6, i + 1)
                    to = (e1b_rows[:, 2 * i:2 * i + 2, :].rearrange("p e n -> p (e n)") if i < EXPERTS // 2
                          else e2b_rows[:, i - EXPERTS // 2, :])
                    e.activation(to, PBB[i % 4][:, :], ACT.Copy).then_inc(s_rows6c, 1)
                for i, (hi, _, w, n) in enumerate(loads):
                    e.wait_ge(s_in6[i % 2], 16 * (i // 2 + 1))
                    e.activation(hi[:, n, :, :].rearrange("p c n -> p (c n)"), rawm[i % 2][:, :], ACT.Copy)\
                        .then_inc(s_hi6, 1)

            @block.vector
            def _(e):
                done = [0]

                def then(ins):
                    done[0] += 1
                    ins.then_inc(s_rt, 1)
                    e.wait_ge(s_rt, done[0])

                def per_tile(a):
                    return a.unsqueeze(2).broadcast_to([P, TILES, EXPERTS])

                def per_expert(a):
                    return a.unsqueeze(1).broadcast_to([P, TILES, EXPERTS])

                then(e.tensor_reduce(most[:, :], logits[:, :, :], AX.X, ALU.max))
                then(e.tensor_tensor(prob[:, :, :], logits[:, :, :], per_tile(most[:, :]), ALU.subtract))
                e.wait_ge(s_exp, 1)
                then(e.tensor_reduce(most[:, :], prob[:, :, :], AX.X, ALU.add))
                then(e.reciprocal(most[:, :], most[:, :]))
                then(e.tensor_tensor(prob[:, :, :], prob[:, :, :], per_tile(most[:, :]), ALU.mult))
                e.wait_ge(s_c6, 10)
                for k in range(2):
                    then(e.tensor_reduce(weight[:, :, k], prob[:, :, :], AX.X, ALU.max))
                    then(e.tensor_tensor(same[:, :, :], prob[:, :, :], per_tile(weight[:, :, k]), ALU.is_equal))
                    then(e.scalar_tensor_tensor(out=place_no[:, :, :], in0=same[:, :, :], scalar=-float(EXPERTS),
                                                in1=per_expert(number_past[:, :]), op0=ALU.mult, op1=ALU.add))
                    then(e.tensor_reduce(choice[:, :, k], place_no[:, :, :], AX.X, ALU.min))
                    if k == 0:
                        then(e.tensor_tensor(same[:, :, :], per_tile(choice[:, :, 0]),
                                             per_expert(number[:, 0:EXPERTS]), ALU.is_equal))
                        then(e.scalar_tensor_tensor(out=prob[:, :, :], in0=same[:, :, :], scalar=-2.0,
                                                    in1=prob[:, :, :], op0=ALU.mult, op1=ALU.add))
                assert done[0] == CHOSEN
                e.wait_ge(s_tail, 1)
                then(e.tensor_tensor(member[:, :, :], choice[:, :, :].rearrange("p t k -> p (t k)").unsqueeze(1)
                                     .broadcast_to([P, GROUPS, J]),
                                     number[:, :].unsqueeze(2).broadcast_to([P, GROUPS, J]), ALU.is_equal))
                then(e.tensor_tensor_scan(running[:, :, :].rearrange("p g j -> p (g j)"),
                                          going_on[:, :, :].rearrange("p g j -> p (g j)"),
                                          member[:, :, :].rearrange("p g j -> p (g j)"), 0.0, ALU.mult, ALU.add))
                then(e.tensor_copy(totals[:, :], running[:, :, J - 1]))
                assert done[0] == COUNTED
                e.wait_ge(s_cnt, 1)
                then(e.tensor_scalar(totals_i[:, :], PCT[:, 64:64 + GROUPS], float(P - 1), None, ALU.add))
                then(e.tensor_scalar(totals_i[:, :], totals_i[:, :], 7, 7, ALU.logical_shift_right,
                                     ALU.logical_shift_left))
                then(e.tensor_copy(totals[:, :], totals_i[:, :]))
                then(e.tensor_tensor_scan(ends9[:, :], going_on[:, 0, 1:1 + GROUPS], totals[:, :], 0.0, ALU.mult,
                                          ALU.add))
                then(e.tensor_tensor(base9[:, :], ends9[:, :], totals[:, :], ALU.subtract))
                then(e.tensor_tensor(base9[:, :], base9[:, :], PCT[:, 0:GROUPS], ALU.add))
                then(e.tensor_tensor(running[:, :, :], running[:, :, :],
                                     base9[:, :].unsqueeze(2).broadcast_to([P, GROUPS, J]), ALU.add))
                then(e.tensor_tensor(running[:, :, :], running[:, :, :], member[:, :, :], ALU.mult))
                then(e.tensor_reduce(slot_f[:, :], running[:, :, :].rearrange("p g j -> p j g"), AX.X, ALU.add))
                then(e.tensor_scalar(slot_i[:, :], slot_f[:, :], -1.0, None, ALU.add))
                then(e.tensor_scalar(high9[:, :], slot_i[:, :], 7, None, ALU.logical_shift_right))
                then(e.tensor_scalar(place9[:, :], slot_i[:, :], P - 1, None, ALU.bitwise_and))
                then(e.scalar_tensor_tensor(out=place9[:, :], in0=place9[:, :], scalar=float(ST),
                                            in1=high9[:, :], op0=ALU.mult, op1=ALU.add))
                e.tensor_copy(tokens[:, :, :].bitcast(F32)[:, :, 1], weight[:, :, :].rearrange("p t k -> p (t k)"))\
                    .then_inc(s_place, 1)
                then(e.tensor_tensor(tile_past[:, :, :],
                                     tile_start[:, :].unsqueeze(2).broadcast_to([1, ST, EXPERTS]),
                                     ends9[0:1, 0:EXPERTS].unsqueeze(1).broadcast_to([1, ST, EXPERTS]), ALU.is_ge))
                then(e.tensor_reduce(tile_expert[:, :], tile_past[:, :, :], AX.X, ALU.add))
                then(e.tensor_scalar(expert_of_tile[:, :], tile_expert[:, :], float(EXPERTS - 1), None, ALU.min))
                for i, (hi, lo, w, n) in enumerate(loads):
                    e.wait_ge(s_hi6, i + 1)
                    e.tensor_tensor(lo[:, n, :, :].rearrange("p c n -> p (c n)"), rawm[i % 2][:, :],
                                    hi[:, n, :, :].rearrange("p c n -> p (c n)").bitcast(F32), ALU.subtract)\
                        .then_inc(s_lo6, 1)
        F2.close()
        clear_semaphores()

        F3 = Scope()
        slots = F3.sb("slots", [P, ST, 2], I32)
        from_m = F3.two("from_m", [P, 2], I32)
        w_m = F3.two("w_m", [P, 2])
        ZG = F3.two("ZG", [P, 2, D])
        ZH = F3.two("ZHm", [P, 2, C, P], F32R)
        ZL = F3.two("ZLm", [P, 2, C, P], F32R)
        HB = F3.sb("HBm", [P, 2, HID])
        HR = F3.sb("HRm", [P, 2, HID])
        HH = F3.sb("HHm", [P, 2, HC, P], F32R)
        HL = F3.sb("HLm", [P, 2, HC, P], F32R)
        YO = F3.two("YOm", [P, 2, D])
        PTZ = F3.ps("PTZm", [P, 2, C, P])
        PH = F3.ps("PHm", [P, 2, HID])
        PHT = F3.ps("PHTm", [P, 2, HC, P])
        PY = [F3.ps(f"PYm{s}", [P, 2, D]) for s in range(2)]
        s_slots = sem("s_slots")
        y_out = transfers("y_out")
        z_in = transfers("z_in", 2, credit=0)
        f_from = flow("f_fromm", 2)
        f_tz = flow("f_tzm")
        f_zh = flow("f_zhm")
        f_zl = flow("f_zlm")
        f_h = flow("f_hm")
        f_hb = flow("f_hbm", 2)
        f_hr = flow("f_hrm", 2)
        f_th = flow("f_thm")
        f_hh = flow("f_hhm")
        f_hl = flow("f_hlm")
        f_y = flow("f_ym")
        f_yo = flow("f_yom", 2)
        flows = [y_out, z_in, f_from, f_tz, f_zh, f_zl, f_h, f_hb, f_hr, f_th, f_hh, f_hl, f_y, f_yo]
        pairs_of_tiles = ST // 2

        def expert(e, t, k):
            return e.value_load(expert_of_tile[0:1, bass.ds(2 * t + k, 1)], min_val=0, max_val=EXPERTS - 1)

        with nc.Block() as block:

            @block.sync
            def _(e):
                give_credit(e, flows)
                e.dma_start(slots[:, :, :].rearrange("p t w -> p (t w)"), list_d.rearrange("(p t) w -> p (t w)", p=P))\
                    .then_inc(s_slots, 16)

                def store(t, s):
                    e.wait_ge(f_yo.sem, f_yo.after(t))
                    e.dma_start(ysl_d[bass.ds(2 * P * t, 2 * P), :].rearrange("(k p) d -> p k d", p=P),
                                YO[s][:, :, :]).then_inc(y_out.sems[s], 16)

                stages(e, pairs_of_tiles, (0, store))
                for s in range(2):
                    last = pairs_of_tiles - 1 - s
                    e.wait_ge(y_out.sems[s], y_out.after(last, last % 2))

            @block.gpsimd
            def _(e):
                e.wait_ge(s_slots, 16)

                def gather(t, s):
                    e.wait_ge(f_tz.sem, f_tz.freed(t))
                    e.wait_ge(f_hr.sem, f_hr.freed(t))
                    e.tensor_copy(from_m[s][:, :], slots[:, bass.ds(2 * t, 2), 0]).then_inc(f_from.sem, 1)
                    e.tensor_copy(w_m[s][:, :], slots[:, :, :].bitcast(F32)[:, bass.ds(2 * t, 2), 1])\
                        .then_inc(f_from.sem, 1)
                    e.wait_ge(f_from.sem, f_from.after(t))
                    e.tensor_tensor(pace[:, 1:2], zeros[:, 0:1], zeros[:, 1:2], ALU.add)
                    for k in range(2):
                        e.indirect_dma_start(ZG[s][:, k, :], None, z_d,
                                             bass.IndirectOffsetOnAxis(from_m[s][:, k:k + 1], 0))\
                            .then_inc(z_in.sems[s], 16)

                stages(e, pairs_of_tiles, (0, gather))

            @block.tensor
            def _(e):
                def first_products(t, s):
                    experts = [expert(e, t, k) for k in range(2)]
                    e.wait_ge(f_zl.sem, f_zl.after(t))
                    e.wait_ge(f_hb.sem, f_hb.after(t - 1))
                    for k in range(2):
                        n = experts[k]
                        for c in range(C):
                            for i, (a, b) in enumerate(((ZH, e1_hi), (ZH, e1_lo), (ZL, e1_hi))):
                                mm = e.matmul(PH[:, k, :], a[s][:, k, c, :],
                                              b[:, bass.ds(n, 1), c, :].rearrange("p e n -> p (e n)"),
                                              start=(c == 0 and i == 0), stop=(c == C - 1 and i == 2))
                    mm.then_inc(f_h.sem, 1)

                def turn_rows(t, s):
                    e.wait_ge(z_in.sems[s], z_in.after(t, s))
                    e.wait_ge(f_zl.sem, f_zl.after(t - 1))
                    for k in range(2):
                        for c in range(C):
                            mm = e.transpose(PTZ[:, k, c, :], ZG[s][:, k, c * P:(c + 1) * P], ident[:, :])
                    mm.then_inc(f_tz.sem, 1)

                def second_products(t, s):
                    experts = [expert(e, t, k) for k in range(2)]
                    e.wait_ge(f_hl.sem, f_hl.after(t))
                    e.wait_ge(f_yo.sem, f_yo.freed(t))
                    for k in range(2):
                        n = experts[k]
                        for m in range(HC):
                            for i, (a, b) in enumerate(((HH, e2_hi), (HH, e2_lo), (HL, e2_hi))):
                                mm = e.matmul(PY[s][:, k, :], a[:, k, m, :],
                                              b[:, bass.ds(n, 1), m, :].rearrange("p e n -> p (e n)"),
                                              start=(m == 0 and i == 0), stop=(m == HC - 1 and i == 2))
                    mm.then_inc(f_y.sem, 1)

                def turn_hidden(t, s):
                    e.wait_ge(f_hr.sem, f_hr.after(t))
                    e.wait_ge(f_hl.sem, f_hl.after(t - 1))
                    for k in range(2):
                        for m in range(HC):
                            mm = e.transpose(PHT[:, k, m, :], HR[:, k, m * P:(m + 1) * P], ident[:, :])
                    mm.then_inc(f_th.sem, 1)

                stages(e, pairs_of_tiles, (0, first_products), (1, turn_rows), (-1, second_products),
                       (0, turn_hidden))

            @block.scalar
            def _(e):
                def relu(t, s):
                    e.wait_ge(f_from.sem, f_from.after(t))
                    e.wait_ge(f_hb.sem, f_hb.after(t))
                    e.wait_ge(f_th.sem, f_th.after(t - 1))
                    for k in range(2):
                        e.activation(HR[:, k, :], HB[:, k, :], ACT.Relu, scale=w_m[s][:, k:k + 1])\
                            .then_inc(f_hr.sem, 1)

                def high_rows(t, s):
                    e.wait_ge(f_tz.sem, f_tz.after(t))
                    e.wait_ge(f_h.sem, f_h.freed(t))
                    e.activation(ZH[s][:, :, :, :], PTZ[:, :, :, :], ACT.Copy).then_inc(f_zh.sem, 1)

                def high_hidden(t, s):
                    e.wait_ge(f_th.sem, f_th.after(t))
                    e.wait_ge(f_y.sem, f_y.after(t - 1))
                    e.activation(HH[:, :, :, :], PHT[:, :, :, :], ACT.Copy).then_inc(f_hh.sem, 1)

                stages(e, pairs_of_tiles, (0, relu), (1, high_rows), (0, high_hidden))

            @block.vector
            def _(e):
                e.wait_ge(s_slots, 16)

                def bias(t, s):
                    for k in range(2):
                        n = expert(e, t, k)
                        e.wait_ge(f_h.sem, f_h.after(t))
                        e.wait_ge(f_hr.sem, f_hr.after(t - 1))
                        e.tensor_tensor(HB[:, k, :], PH[:, k, :],
                                        e1b_rows[:, bass.ds(n, 1), :].rearrange("p e n -> p (e n)"), ALU.add)\
                            .then_inc(f_hb.sem, 1)

                def low_rows(t, s):
                    e.wait_ge(f_zh.sem, f_zh.after(t))
                    e.tensor_tensor(ZL[s][:, :, :, :], PTZ[:, :, :, :], ZH[s][:, :, :, :].bitcast(F32),
                                    ALU.subtract).then_inc(f_zl.sem, 1)

                def outputs(t, s):
                    for k in range(2):
                        n = expert(e, t, k)
                        e.wait_ge(f_y.sem, f_y.after(t))
                        e.wait_ge(y_out.sems[s], y_out.freed(t, s))
                        e.scalar_tensor_tensor(out=YO[s][:, k, :],
                                               in0=e2b_rows[:, bass.ds(n, 1), :].rearrange("p e n -> p (e n)"),
                                               scalar=slots[:, :, :].bitcast(F32)[:, bass.ds(2 * t + k, 1), 1],
                                               in1=PY[s][:, k, :], op0=ALU.mult,
                                               op1=ALU.add).then_inc(f_yo.sem, 1)

                def low_hidden(t, s):
                    e.wait_ge(f_hh.sem, f_hh.after(t))
                    e.tensor_tensor(HL[:, :, :, :], PHT[:, :, :, :], HH[:, :, :, :].bitcast(F32), ALU.subtract)\
                        .then_inc(f_hl.sem, 1)

                stages(e, pairs_of_tiles, (0, bias), (1, low_rows), (-1, outputs), (0, low_hidden))
        F3.close()
        W.close()
        clear_semaphores()

        F4 = Scope()
        SUM = 7
        sum_turns = TILES // SUM
        from_y = F4.two("from_y", [P, 2 * SUM], I32)
        XS = F4.two("XS", [P, SUM, D])
        YG = F4.two("YG", [P, 2 * SUM, D])
        x_in7 = transfers("x_in7")
        out_out = transfers("out_out")
        y_in7 = transfers("y_in7", 2 * SUM, credit=0)
        f_from7 = flow("f_from7")
        f_sum7 = flow("f_sum7", 2)
        flows = [x_in7, out_out, y_in7, f_from7, f_sum7]
        assert sum_turns * SUM == TILES

        with nc.Block() as block:

            @block.sync
            def _(e):
                give_credit(e, flows)

                def load(t, s):
                    e.wait_ge(out_out.sems[s], out_out.freed(t, s))
                    e.dma_start(XS[s][:, :, :], x1_d[bass.ds(SUM * P * t, SUM * P), :]
                                .rearrange("(g p) d -> p g d", p=P)).then_inc(x_in7.sems[s], 16)

                def store(t, s):
                    e.wait_ge(f_sum7.sem, f_sum7.after(t))
                    if isinstance(t, int) and t == sum_turns - 1:
                        whole = N - TAIL - SUM * P * t
                        e.dma_start(out[SUM * P * t:N - TAIL, :].rearrange("(g p) d -> p g d", p=P),
                                    XS[s][:, 0:whole // P, :]).then_inc(out_out.sems[s], 16)
                        e.dma_start(out[N - TAIL:N, :], XS[s][0:TAIL, SUM - 1, :]).then_inc(out_out.sems[s], 16)
                        return
                    e.dma_start(out[bass.ds(SUM * P * t, SUM * P), :].rearrange("(g p) d -> p g d", p=P),
                                XS[s][:, :, :]).then_inc(out_out.sems[s], 16)

                stages(e, sum_turns, (1, load), (0, store))
                last = sum_turns - 1
                e.wait_ge(out_out.sems[last % 2], out_out.after(last, last % 2) + 16)
                e.wait_ge(out_out.sems[(last - 1) % 2], out_out.after(last - 1, (last - 1) % 2))

            @block.gpsimd
            def _(e):
                def gather(t, s):
                    e.wait_ge(f_sum7.sem, f_sum7.freed(t))
                    e.tensor_copy(from_y[s][:, :], slot_i[:, bass.ds(2 * SUM * t, 2 * SUM)])\
                        .then_inc(f_from7.sem, 1)
                    e.wait_ge(f_from7.sem, f_from7.after(t))
                    e.tensor_tensor(pace[:, 1:2], zeros[:, 0:1], zeros[:, 1:2], ALU.add)
                    for j in range(2 * SUM):
                        e.indirect_dma_start(YG[s][:, j, :], None, ysl_d,
                                             bass.IndirectOffsetOnAxis(from_y[s][:, j:j + 1], 0))\
                            .then_inc(y_in7.sems[s], 16)

                stages(e, sum_turns, (0, gather))

            @block.vector
            def _(e):
                def add(t, s):
                    e.wait_ge(x_in7.sems[s], x_in7.after(t, s))
                    e.wait_ge(y_in7.sems[s], y_in7.after(t, s))
                    for k in range(2):
                        if k:
                            e.wait_ge(f_sum7.sem, f_sum7.after(t, 1))
                        e.tensor_tensor(XS[s][:, :, :], XS[s][:, :, :],
                                        YG[s][:, :, :].rearrange("p (g k) d -> p g k d", k=2)[:, :, k, :], ALU.add)\
                            .then_inc(f_sum7.sem, 1)

                stages(e, sum_turns, (0, add))
        F4.close()
        Fs.close()
        G.close()


_INS = ['x', 'src', 'dst', 'L0_gnn_self_w', 'L0_gnn_self_b', 'L0_gnn_neigh_w', 'L0_gnn_neigh_b', 'L0_mix_Wq',
        'L0_mix_bq', 'L0_mix_Wk', 'L0_mix_bk', 'L0_mix_Wv', 'L0_mix_bv', 'L0_mix_Wo', 'L0_mix_bo', 'L0_mix_W1',
        'L0_mix_b1', 'L0_mix_W2', 'L0_mix_b2', 'L0_mix_g1', 'L0_mix_be1', 'L0_mix_g2', 'L0_mix_be2', 'L0_ffn_Wr',
        'L0_ffn_br', 'L0_ffn_W1', 'L0_ffn_b1', 'L0_ffn_W2', 'L0_ffn_b2']
_TURNED = ('L0_gnn_self_w', 'L0_gnn_neigh_w')
_COLUMNS = ('L0_mix_g1', 'L0_mix_be1', 'L0_mix_g2', 'L0_mix_be2', 'L0_mix_b1')


def kernel(**inputs):
    import numpy as _np
    import concourse.bacc as _bacc
    from concourse import mybir as _mybir
    from concourse.bass_utils import run_bass_kernel_spmd as _run

    nc = _bacc.Bacc("TRN2", target_bir_lowering=False, num_devices=1)
    arrays, args = {}, []
    for name in _INS:
        a = _np.asarray(inputs[name])
        if name in _COLUMNS:
            a = a.reshape(-1, P).T
        a = _np.ascontiguousarray(a.T if name in _TURNED else a)
        arrays[f"in_{name}_dram"] = a
        args.append(nc.dram_tensor(f"in_{name}_dram", a.shape, _mybir.dt.from_np(a.dtype), kind="ExternalInput").ap())
    args.append(nc.dram_tensor("out_0_dram", arrays["in_x_dram"].shape, F32, kind="ExternalOutput").ap())
    gps_layer_kernel(nc, *args)
    r = _run(nc, [arrays], core_ids=[0])
    return r.results[0]["out_0_dram"]
```

```python
from contextlib import ExitStack

import concourse.bass as bass
from concourse import mybir

F32 = mybir.dt.float32
F32R = mybir.dt.float32r
I32 = mybir.dt.int32
U32 = mybir.dt.uint32
ALU = mybir.AluOpType
ACT = mybir.ActivationFunctionType
AX = mybir.AxisListType

P = 128
EPS_LN = 1e-5
EPS_FLOW = 1e-6


class Flow:

    def __init__(self, sem, n=1):
        self.sem, self.n, self.credit = sem, n, 2 * n

    def after(self, t, k=None):
        return self.n * t + self.credit + (self.n if k is None else k)

    def freed(self, t):
        return self.n * t + self.n


class Transfers:

    def __init__(self, sems, k=1, credit=1):
        self.sems, self.k = sems, k
        self.credit = 16 * k * credit

    def after(self, t, s):
        return 8 * self.k * (t - s) + 16 * self.k + self.credit

    def freed(self, t, s):
        return 8 * self.k * (t - s) + self.credit


def give_credit(eng, flows):
    for f in flows:
        for sem in (f.sems if isinstance(f, Transfers) else [f.sem]):
            if f.credit:
                eng.sem_inc(sem, f.credit)


def stages(eng, tiles, *parts, first=0, beside=None):
    low, high = min(a for a, _ in parts), max(a for a, _ in parts)
    before, extra, more, end = beside or (None, 0, None, None)

    def turn(t, parity, k=None):
        for n, (ahead, step) in enumerate(parts):
            if n == before and k is not None:
                more(k, (parity - start) % 2)
            if not isinstance(t, int) or first <= t + ahead < tiles:
                step(t + ahead, (parity + ahead) % 2)

    start = first - low
    looped = max(0, (tiles - 1 - high - start) // 2 * 2)
    for t in range(first - high, start):
        turn(t, t % 2)
    if extra:
        with eng.Fori(start, start + extra - 1, 2) as i:
            turn(i, start % 2, i - start)
            turn(i + 1, (start + 1) % 2, i + 1 - start)
        end()
    with eng.Fori(start + extra, start + looped - 1, 2) as i:
        turn(i, start % 2)
        turn(i + 1, (start + 1) % 2)
    for t in range(start + looped, tiles - low):
        turn(t, t % 2)


def gps_layer_kernel(nc, x, src, dst, self_wT, self_b, neigh_wT, neigh_b, Wq, bq, Wk, bk, Wv, bv, Wo, bo,
                     W1, b1, W2, b2, g1, be1, g2, be2, Wr, br, E1, e1b, E2, e2b, out):
    N, D = x.shape
    EDGES = src.shape[0]
    TILES = (N + P - 1) // P
    NP = TILES * P
    TAIL = N - (TILES - 1) * P
    C = D // P
    H = 8
    DH = D // H
    HID = W1.shape[1]
    HC = HID // P
    EXPERTS = E1.shape[0]
    EP = 125
    EJ = EDGES // EP
    GRP = 8
    ETILES = (EDGES - TILES) // P + TILES + 1
    ETILES += -ETILES % GRP
    GROUPS = EXPERTS + 1
    ST = (2 * NP + EXPERTS * (P - 1) + P - 1) // P
    ST += ST % 2
    NOROW = 200
    assert EP * EJ == EDGES and TILES % 2 == 1

    def rows_of(t):
        return TAIL if isinstance(t, int) and t == TILES - 1 else P

    def tile_rows(d, t, rows=P):
        return d[bass.ds(t * P, rows), :]

    def dram(name, shape, dt=F32):
        return nc.dram_tensor(name, shape, dt, kind="Internal").ap()

    xn_d = dram("xn_d", [NP, D])
    self_d = dram("self_d", [NP, D])
    y_d = dram("y_d", [NP, D])
    q_d = dram("q_d", [NP, D])
    k_d = dram("k_d", [NP, D])
    v_d = dram("v_d", [NP, D])
    qs_d = dram("qs_d", [NP, D])
    x1_d = dram("x1_d", [NP, D])
    rec_d = dram("rec_d", [ETILES * P, 2], I32)

    top = ExitStack()

    live = []

    def sem(name):
        live.append(nc.alloc_semaphore(name=name))
        return live[-1]

    def clear_semaphores():
        with nc.Block() as block:

            @block.gpsimd
            def _(e):
                nc.clear_and_free_semaphores(live)
        live.clear()

    def flow(name, n=1):
        return Flow(sem(name), n)

    def transfers(name, k=1, credit=1):
        return Transfers([sem(f"{name}{s}") for s in range(2)], k, credit)

    class Scope:
        def __init__(self):
            self.stack = ExitStack()

        def sb(self, name, shape, dt=F32):
            return self.stack.enter_context(nc.sbuf_tensor(name, shape, dt))

        def ps(self, name, shape, dt=F32):
            return self.stack.enter_context(nc.psum_tensor(name, shape, dt))

        def two(self, name, shape, dt=F32):
            return [self.sb(f"{name}{s}", shape, dt) for s in range(2)]

        def close(self):
            self.stack.close()

    def split_products(eng, bank, hi, lo, whi, wlo, n):
        last = None
        for c in range(n):
            for a, b in ((hi, whi), (hi, wlo), (lo, whi)):
                last = eng.matmul(bank, a[:, c, :], b[:, c, :], start=(c == 0 and a is hi and b is whi),
                                  stop=(c == n - 1 and a is lo))
        return last

    STATISTICS_OPS = 7
    CHOSEN, COUNTED = 17, 20

    def row_statistics(e, stats, mean, var, tmp, made):
        m0, m1 = stats[:, :, 1], stats[:, :, 4]
        e.tensor_tensor(mean[:, :], m0, m1, ALU.add).then_inc(made, 1)
        e.tensor_tensor(tmp[:, :], m0, m1, ALU.subtract).then_inc(made, 1)
        e.tensor_tensor(var[:, :], stats[:, :, 2], stats[:, :, 5], ALU.add).then_inc(made, 1)
        e.wait_ge(made, 3)
        e.tensor_scalar(mean[:, :], mean[:, :], 0.5, None, ALU.mult).then_inc(made, 1)
        e.scalar_tensor_tensor(out=tmp[:, :], in0=tmp[:, :], scalar=D / 4.0, in1=tmp[:, :], op0=ALU.mult,
                               op1=ALU.mult).then_inc(made, 1)
        e.wait_ge(made, 5)
        e.tensor_tensor(var[:, :], var[:, :], tmp[:, :], ALU.add).then_inc(made, 1)
        e.wait_ge(made, 6)
        e.tensor_scalar(var[:, :], var[:, :], 1.0 / D, None, ALU.mult).then_inc(made, 1)
        assert STATISTICS_OPS == 7

    def scatter_records(e, dest, places, recs, rows, columns, to, rec, first, turns, scat, f_slot):

        def scatter(t, s):
            if not (isinstance(t, int) and t < 2):
                e.wait_ge(scat.sems[s], scat.freed(t, s))
            column = bass.ds(columns * (t + first), columns)
            e.tensor_copy(to[s][0:rows, :], places[0:rows, column]).then_inc(f_slot.sem, 1)
            e.tensor_copy(rec[s][0:rows, :], recs[0:rows, column, :].rearrange("p j w -> p (j w)"))\
                .then_inc(f_slot.sem, 1)
            e.wait_ge(f_slot.sem, f_slot.after(t))
            e.tensor_tensor(pace[:, 1:2], zeros[:, 0:1], zeros[:, 1:2], ALU.add)
            for j in range(columns):
                e.indirect_dma_start(dest, bass.IndirectOffsetOnAxis(to[s][0:rows, j:j + 1], 0),
                                     rec[s][0:rows, 2 * j:2 * j + 2], None).then_inc(scat.sems[s], 16)

        scatter(0, 0)
        scatter(1, 1)
        stages(e, turns, (0, scatter), first=2)
        for s in range(2):
            e.wait_ge(scat.sems[s], scat.after(turns - 1 - s, (turns - 1 - s) % 2))

    with top:
        G = Scope()
        Held = Scope()
        SCAT = 16
        SCAT_TURNS = EJ // SCAT
        RANK_PAIRS = (TILES + 1) // 2
        RANKED = 4
        SCAT_FIRST = 28
        ident = G.sb("ident", [P, P])
        ones = G.sb("ones", [P, P])
        zeros = G.sb("zeros", [P, D])
        consts = G.sb("consts", [P, 4])
        eps_c, mhalf = consts[:, 0:1], consts[:, 1:2]
        pace = G.sb("pace", [P, 2])
        bucket_of_tile = G.sb("bucket_of_tile", [1, ETILES], I32)
        both = G.sb("both", [P, TILES, 2 * EXPERTS])
        br_rows = G.sb("br_rows", [P, EXPERTS])
        slot_i = G.sb("slot_i", [P, 2 * TILES], I32)
        expert_of_tile = G.sb("expert_of_tile", [1, ST], I32)

        qsum = Held.sb("qsum", [P, D])
        ksum = Held.sb("ksum", [P, D])
        block_mask = Held.sb("block_mask", [P, P])
        rs_all = Held.sb("rs_all", [P, TILES])
        mean_all = Held.sb("mean_all", [P, TILES])
        r2_all = Held.sb("r2_all", [P, TILES])
        place_i = Held.sb("place_i", [P, EJ], I32)
        records = Held.sb("records", [P, EJ, 2], I32)
        to8 = Held.two("to8", [P, SCAT], I32)
        rec8 = Held.two("rec8", [P, 2 * SCAT], I32)

        A = Scope()
        names = ("neigh", "self", "q", "k", "v")
        whi = {n: A.sb(f"whi_{n}", [P, C, D], F32R) for n in names}
        wlo = {n: A.sb(f"wlo_{n}", [P, C, D], F32R) for n in names}
        bias_all = A.sb("bias_all", [P, 4, D])
        bucket = A.sb("bucket", [P, EJ])
        bucket_ids = A.sb("bucket_ids", [P, TILES + 1])
        ones_e = A.sb("ones_e", [P, EJ])
        counts = A.sb("counts", [P, TILES + 1])
        base = A.sb("base", [P, TILES + 1])
        srcs = A.sb("srcs", [P, EJ], I32)
        dsts = A.sb("dsts", [P, EJ], I32)
        high = A.sb("high", [P, EJ], I32)
        rmatch = A.two("rmatch", [P, EJ])
        rank = A.two("rank", [P, EJ])
        placed = A.two("placed", [P, EJ])
        pos = A.sb("pos", [P, EJ])
        S = Scope()
        raw = [S.sb(f"raw{s}", [P, C, D]) for s in range(2)]
        gcol = S.sb("gcol", [P, C])
        bcol = S.sb("bcol", [P, C])
        be_wide = S.sb("be_wide", [P, C, P])
        brow = S.sb("brow", [1, 5, D])
        rec_pad = S.sb("rec_pad", [P, ETILES, 2], I32)
        XG = 3
        x_turns = TILES // XG
        xs = S.two("xs", [P, XG, D])
        stats = S.sb("stats", [P, TILES, 6])
        st_a = S.sb("st_a", [P, TILES])
        st_b = S.sb("st_b", [P, TILES])
        upper = S.sb("upper", [P, P])
        upper_incl = S.sb("upper_incl", [P, P])
        tile_no = S.sb("tile_no", [P, ETILES])
        padded = S.sb("padded", [P, TILES])
        padded_i = S.sb("padded_i", [P, TILES], I32)
        ends = S.sb("ends", [P, TILES])
        pad_col = S.sb("pad_col", [P, 1])
        pad_col_i = S.sb("pad_col_i", [P, 1], I32)
        end_col = S.sb("end_col", [P, 1])
        ps_bias = S.ps("ps_bias", [P, 4, D])
        ps_e = S.ps("ps_e", [P, D])
        ps_e2 = S.ps("ps_e2", [P, 2, D])

        s_cons = sem("s_cons")
        s_consd = sem("s_consd")
        s_raw = [sem(f"s_raw{s}") for s in range(2)]
        s_small = sem("s_small")
        s_src = sem("s_src")
        s_pad = sem("s_pad")
        s_padout = sem("s_padout")
        s_wide = sem("s_wide")
        s_biasmm = sem("s_biasmm")
        s_hi = sem("s_hi")
        s_lo = sem("s_lo")
        s_biasv = sem("s_biasv")
        s_edge = sem("s_edge")
        s_count = sem("s_count")
        s_emm = sem("s_emm")
        s_stat = sem("s_stat")
        s_pow = sem("s_pow")
        xs_in = transfers("xs_in")
        f_xs = flow("f_xs", XG)
        weights = {"neigh": neigh_wT, "self": self_wT, "q": Wq, "k": Wk, "v": Wv}
        folded = {"neigh": False, "self": False, "q": True, "k": True, "v": True}

        with nc.Block() as block:

            @block.sync
            def _(e):
                give_credit(e, [xs_in, f_xs])
                e.dma_start(srcs[0:EP, :], src.rearrange("(p j) -> p j", p=EP)).then_inc(s_src, 16)
                e.dma_start(dsts[0:EP, :], dst.rearrange("(p j) -> p j", p=EP)).then_inc(s_src, 16)
                e.dma_start(gcol[:, :], g1).then_inc(s_small, 16)
                e.dma_start(bcol[:, :], be1).then_inc(s_small, 16)
                for i, b in enumerate((self_b, neigh_b, bq, bk, bv)):
                    e.dma_start(brow[:, i, :], b.rearrange("(a n) -> a n", a=1)).then_inc(s_small, 16)

                def load_weight(i):
                    if i >= 2:
                        e.wait_ge(s_hi, C * (i - 1))
                        e.wait_ge(s_lo, C * (i - 1))
                    if i == 4:
                        e.wait_ge(s_biasmm, 2)
                    e.dma_start(raw[i % 2][:, :, :], weights[names[i]].rearrange("(c p) n -> p c n", p=P))\
                        .then_inc(s_raw[i % 2], 16)

                load_weight(0)
                load_weight(1)

                def load_x(t, s):
                    e.wait_ge(f_xs.sem, f_xs.freed(t))
                    e.dma_start(xs[s][:, :, :], x[bass.ds(XG * P * t, XG * P), :]
                                .rearrange("(g p) d -> p g d", p=P)).then_inc(xs_in.sems[s], 16)

                stages(e, x_turns, (0, load_x))
                e.wait_ge(f_xs.sem, f_xs.freed(x_turns))
                e.dma_start(xs[x_turns % 2][0:TAIL, 0, :], x[(TILES - 1) * P:N, :])\
                    .then_inc(xs_in.sems[x_turns % 2], 16)
                for i in range(2, len(names)):
                    load_weight(i)
                e.wait_ge(s_pad, 2)
                e.dma_start(rec_d.rearrange("(p t) w -> p (t w)", p=P),
                            rec_pad[:, :, :].rearrange("p t w -> p (t w)")).then_inc(s_padout, 16)
                e.wait_ge(s_padout, 16)

            @block.gpsimd
            def _(e):
                e.memset(ones[:, :], 1.0).then_inc(s_cons, 1)
                e.memset(ident[:, :], 0.0).then_inc(s_cons, 1)
                e.memset(zeros[:, :], 0.0).then_inc(s_cons, 1)
                e.memset(eps_c, EPS_LN).then_inc(s_cons, 1)
                e.memset(mhalf, -0.5).then_inc(s_cons, 1)
                e.memset(pace[:, :], 0.0).then_inc(s_cons, 1)
                e.memset(qsum[:, :], 0.0).then_inc(s_cons, 1)
                e.memset(ksum[:, :], 0.0).then_inc(s_cons, 1)
                e.memset(pos[:, :], 0.0).then_inc(s_cons, 1)
                e.memset(stats[:, :, :], 0.0).then_inc(s_cons, 1)
                e.memset(ones_e[:, :], 1.0).then_inc(s_cons, 1)
                e.memset(rec_pad[:, :, 0], 0).then_inc(s_pad, 1)
                e.memset(rec_pad[:, :, 1], NOROW).then_inc(s_pad, 1)
                e.iota(bucket_ids[:, :], pattern=[[1, TILES + 1]], base=0, channel_multiplier=0,
                       allow_small_or_imprecise_dtypes=True).then_inc(s_cons, 1)
                e.iota(tile_no[:, :], pattern=[[1, ETILES]], base=0, channel_multiplier=0,
                       allow_small_or_imprecise_dtypes=True).then_inc(s_cons, 1)
                e.wait_ge(s_cons, 13)
                e.affine_select(out=ident[:, :], in_=ident[:, :], compare_op=ALU.not_equal, fill=1.0, base=0,
                                pattern=[[-1, P]], channel_multiplier=1).then_inc(s_consd, 1)
                e.affine_select(out=upper[:, :], in_=ones[:, :], compare_op=ALU.is_gt, fill=0.0, base=0,
                                pattern=[[1, P]], channel_multiplier=-1).then_inc(s_consd, 1)
                e.affine_select(out=upper_incl[:, :], in_=ones[:, :], compare_op=ALU.is_ge, fill=0.0, base=0,
                                pattern=[[1, P]], channel_multiplier=-1).then_inc(s_consd, 1)
                ops = ((st_b, st_a, eps_c, ALU.add), (rs_all, st_b, mhalf, ALU.pow),
                       (st_b, st_a, rs_all, ALU.mult), (st_b, st_b, rs_all, ALU.mult),
                       (st_b, st_b, eps_c, ALU.add), (r2_all, st_b, mhalf, ALU.pow))
                e.wait_ge(s_stat, 7)
                for k, (o, a, b, op) in enumerate(ops):
                    b = b.broadcast_to([P, TILES]) if b is eps_c or b is mhalf else b[:, :]
                    e.tensor_tensor(o[:, :], a[:, :], b, op).then_inc(s_pow, 1)
                    e.wait_ge(s_pow, k + 1)

            @block.tensor
            def _(e):
                e.wait_ge(s_consd, 3)
                e.wait_ge(s_small, 16 * 7)
                e.wait_ge(s_wide, C)
                e.matmul(ps_bias[:, 0, :], ones[0:1, :], brow[:, 0, :], start=True, stop=False)
                e.matmul(ps_bias[:, 0, :], ones[0:1, :], brow[:, 1, :], start=False, stop=True)
                for i in range(2, 5):
                    e.wait_ge(s_raw[i % 2], 16 * (i // 2 + 1))
                    e.matmul(ps_bias[:, i - 1, :], ones[0:1, :], brow[:, i, :], start=True, stop=False)
                    for c in range(C):
                        mm = e.matmul(ps_bias[:, i - 1, :], be_wide[:, c, :], raw[i % 2][:, c, :], start=False,
                                      stop=(c == C - 1))
                    mm.then_inc(s_biasmm, 2)
                e.wait_ge(s_count, TILES + 3)
                e.matmul(ps_e[:, 0:TILES], upper[0:EP, :], counts[0:EP, 0:TILES], start=True, stop=True)
                e.matmul(ps_e[:, 64:64 + TILES], ones[0:EP, :], counts[0:EP, 0:TILES], start=True, stop=True)
                e.matmul(ps_e[0:TILES, 128:129], counts[0:EP, 0:TILES], ones[0:EP, 0:1], start=True, stop=True)\
                    .then_inc(s_emm, 1)
                e.wait_ge(s_edge, 8)
                e.matmul(ps_e2[0:TILES, 0, 0:1], upper_incl[0:TILES, 0:TILES], pad_col[0:TILES, :], start=True,
                         stop=True).then_inc(s_emm, 1)
                e.wait_ge(s_edge, 11)
                for h in range(2):
                    mm = e.matmul(ps_e2[0:1, h, 0:ETILES // 2], ones[0:TILES, 0:1],
                                  tile_no[0:TILES, h * (ETILES // 2):(h + 1) * (ETILES // 2)], start=True, stop=True)
                mm.then_inc(s_emm, 1)

            @block.scalar
            def _(e):
                e.wait_ge(s_small, 16 * 7)
                for i, n in enumerate(names):
                    e.wait_ge(s_raw[i % 2], 16 * (i // 2 + 1))
                    for c in range(C):
                        e.activation(whi[n][:, c, :], raw[i % 2][:, c, :], ACT.Copy,
                                     scale=gcol[:, c:c + 1] if folded[n] else 1.0).then_inc(s_hi, 1)

            @block.vector
            def _(e):
                for h in range(P // DH):
                    for g in range(P // DH):
                        e.memset(block_mask[h * DH:(h + 1) * DH, g * DH:(g + 1) * DH], float(h == g))
                e.wait_ge(s_small, 16 * 7)
                e.wait_ge(s_cons, 13)
                for c in range(C):
                    e.tensor_scalar(be_wide[:, c, :], ones[:, :], bcol[:, c:c + 1], None, ALU.mult)\
                        .then_inc(s_wide, 1)
                e.wait_ge(s_src, 32)
                e.tensor_scalar(high[0:EP, :], srcs[0:EP, :], 7, None, ALU.logical_shift_right)\
                    .then_inc(s_edge, 1)
                e.wait_ge(s_edge, 1)
                e.tensor_copy(bucket[0:EP, :], high[0:EP, :]).then_inc(s_edge, 1)
                e.wait_ge(s_edge, 2)
                for k in range(2):
                    e.memset(rmatch[k][0:EP, :], 0.0).then_inc(s_count, 1)
                e.memset(base[:, TILES:TILES + 1], 0.0)

                def low_parts(i0, i1):
                    for i in range(i0, i1):
                        n = names[i]
                        for c in range(C):
                            e.wait_ge(s_hi, C * i + c + 1)
                            e.scalar_tensor_tensor(out=wlo[n][:, c, :], in0=raw[i % 2][:, c, :],
                                                   scalar=gcol[:, c:c + 1] if folded[n] else 1.0,
                                                   in1=whi[n][:, c, :].bitcast(F32), op0=ALU.mult,
                                                   op1=ALU.subtract).then_inc(s_lo, 1)

                def count(b, k):
                    e.wait_ge(s_count, b + 1)
                    e.tensor_scalar(rmatch[k][0:EP, :], bucket[0:EP, :], bucket_ids[0:EP, bass.ds(b, 1)],
                                    0.0, ALU.is_equal, ALU.add, accum_out=counts[0:EP, bass.ds(b, 1)])\
                        .then_inc(s_count, 1)

                def statistics(t, s):
                    e.wait_ge(xs_in.sems[s], xs_in.after(t, s))
                    for g in range(XG):
                        e.bn_stats(stats[:, bass.ds(XG * t + g, 1), :].rearrange("p t k -> p (t k)"),
                                   xs[s][:, g, :]).then_inc(f_xs.sem, 1)
                    for g in range(XG):
                        count(XG * t + g, (XG * s + g) % 2)

                low_parts(0, 2)
                stages(e, x_turns, (0, statistics))
                for b in range(XG * x_turns, TILES + 1):
                    count(b, b % 2)
                e.wait_ge(xs_in.sems[x_turns % 2], xs_in.after(x_turns, x_turns % 2))
                e.bn_stats(stats[0:TAIL, TILES - 1, :], xs[x_turns % 2][0:TAIL, 0, :]).then_inc(f_xs.sem, 1)
                e.wait_ge(f_xs.sem, f_xs.after(x_turns - 1) + 1)
                row_statistics(e, stats, mean_all, st_a, st_b, s_stat)
                low_parts(2, len(names))
                e.wait_ge(s_emm, 1)
                e.tensor_scalar(padded_i[:, :], ps_e[:, 64:64 + TILES], float(P - 1), None, ALU.add)\
                    .then_inc(s_edge, 1)
                e.tensor_scalar(pad_col_i[0:TILES, :], ps_e[0:TILES, 128:129], float(P - 1), None, ALU.add)\
                    .then_inc(s_edge, 1)
                e.wait_ge(s_edge, 4)
                e.tensor_scalar(padded_i[:, :], padded_i[:, :], 7, 7, ALU.logical_shift_right,
                                ALU.logical_shift_left).then_inc(s_edge, 1)
                e.tensor_scalar(pad_col_i[0:TILES, :], pad_col_i[0:TILES, :], 7, None,
                                ALU.logical_shift_right).then_inc(s_edge, 1)
                e.wait_ge(s_edge, 6)
                e.tensor_copy(padded[:, :], padded_i[:, :]).then_inc(s_edge, 1)
                e.tensor_copy(pad_col[0:TILES, :], pad_col_i[0:TILES, :]).then_inc(s_edge, 1)
                e.wait_ge(s_edge, 8)
                e.tensor_tensor_scan(ends[:, :], ones_e[:, 0:TILES], padded[:, :], 0.0, ALU.mult, ALU.add)\
                    .then_inc(s_edge, 1)
                e.wait_ge(s_emm, 2)
                e.tensor_copy(end_col[0:TILES, :], ps_e2[0:TILES, 0, 0:1]).then_inc(s_edge, 1)
                e.wait_ge(s_edge, 10)
                e.tensor_scalar(tile_no[0:TILES, :], tile_no[0:TILES, :], end_col[0:TILES, :], None, ALU.is_ge)\
                    .then_inc(s_edge, 1)
                e.tensor_tensor(ends[:, :], ends[:, :], padded[:, :], ALU.subtract).then_inc(s_edge, 1)
                e.wait_ge(s_edge, 12)
                e.tensor_tensor(base[:, 0:TILES], ps_e[:, 0:TILES], ends[:, :], ALU.add).then_inc(s_edge, 1)
                e.wait_ge(s_emm, 3)
                e.tensor_scalar(bucket_of_tile[:, :].rearrange("a (h t) -> a h t", h=2), ps_e2[0:1, :, 0:ETILES // 2],
                                float(TILES - 1), None, ALU.min)\
                    .then_inc(s_edge, 1)

                e.wait_ge(s_biasmm, 6)
                e.tensor_copy(bias_all[:, :, :], ps_bias[:, :, :]).then_inc(s_biasv, 1)
        S.close()

        B = Scope()
        X = B.two("X", [P, D])
        XN = B.two("XN", [P, D])
        XH = B.two("XH", [P, C, P], F32R)
        XL = B.two("XL", [P, C, P], F32R)
        SO = B.two("SO", [P, D])
        YO = B.two("YO", [P, D])
        QT = B.two("QT", [P, D])
        KT = B.two("KT", [P, D])
        Q = B.two("Q", [P, D])
        K = B.two("K", [P, D])
        V = B.two("V", [P, D])
        PT = [B.ps(f"PT{s}", [P, C, P]) for s in range(2)]
        PB = {n: B.ps(f"PB_{n}", [P, D]) for n in names}

        x_in = transfers("x_in")
        xn_out = transfers("xn_out")
        outs = {n: transfers(f"o_{n}") for n in names}
        f_xn = flow("f_xn")
        f_pt = flow("f_pt")
        f_hi = flow("f_hi")
        f_lo = flow("f_lo")
        f_prod = flow("f_prod", 5)
        f_pre = flow("f_pre", 2)
        f_made = {n: flow(f"f_made_{n}") for n in names}
        f_acc = flow("f_acc", 2)
        f_rank = flow("f_rank", 6)
        f_pos = flow("f_pos", 2)
        s_rec = sem("s_rec")
        f_slot = flow("f_slot", 2)
        scat = transfers("scat", SCAT, credit=0)
        flows = [x_in, xn_out, *outs.values(), f_xn, f_pt, f_hi, f_lo, f_prod, f_pre,
                 *f_made.values(), f_acc, f_rank, f_pos, f_slot, scat]
        made_in = {"neigh": YO, "self": SO, "q": Q, "k": K, "v": V}
        stored = {"neigh": y_d, "self": self_d, "q": q_d, "k": k_d, "v": v_d}

        with nc.Block() as block:

            @block.sync
            def _(e):
                give_credit(e, flows)

                def front(t, s):
                    rows = rows_of(t)
                    e.wait_ge(f_xn.sem, f_xn.freed(t))
                    e.dma_start(X[s][0:rows, :], tile_rows(x, t, rows)).then_inc(x_in.sems[s], 16)

                def store_xn(t, s):
                    e.wait_ge(f_xn.sem, f_xn.after(t))
                    e.dma_start(tile_rows(xn_d, t), XN[s][:, :]).then_inc(xn_out.sems[s], 16)

                def back(t, s):
                    for n in names:
                        e.wait_ge(f_made[n].sem, f_made[n].after(t))
                        e.dma_start(tile_rows(stored[n], t), made_in[n][s][:, :]).then_inc(outs[n].sems[s], 16)

                stages(e, TILES, (4, front), (2, store_xn), (0, back))
                for f in (xn_out, *outs.values()):
                    for s in range(2):
                        e.wait_ge(f.sems[s], f.after(TILES - 1 - s, (TILES - 1 - s) % 2))

            @block.vector
            def _(e):
                def front(t, s):
                    e.wait_ge(x_in.sems[s], x_in.after(t, s))
                    e.wait_ge(xn_out.sems[s], xn_out.freed(t, s))
                    e.wait_ge(f_pt.sem, f_pt.freed(t))
                    e.tensor_scalar(XN[s][:, :], X[s][:, :], mean_all[:, bass.ds(t, 1)],
                                    rs_all[:, bass.ds(t, 1)], ALU.subtract, ALU.mult).then_inc(f_xn.sem, 1)

                def low_part(t, s):
                    e.wait_ge(f_pt.sem, f_pt.after(t))
                    e.wait_ge(f_hi.sem, f_hi.after(t))
                    e.tensor_tensor(XL[s][:, :, :], PT[s][:, :, :], XH[s][:, :, :].bitcast(F32), ALU.subtract)\
                        .then_inc(f_lo.sem, 1)

                def back(t, s):
                    e.wait_ge(f_prod.sem, f_prod.after(t, 2))
                    e.wait_ge(outs["self"].sems[s], outs["self"].freed(t, s))
                    e.tensor_tensor(SO[s][:, :], PB["self"][:, :], bias_all[:, 0, :], ALU.add)\
                        .then_inc(f_made["self"].sem, 1)
                    for k, (n, to, fr) in enumerate((("q", QT, f_made["q"]), ("k", KT, f_made["k"]))):
                        e.wait_ge(f_prod.sem, f_prod.after(t, 3 + k))
                        e.wait_ge(fr.sem, fr.freed(t))
                        e.scalar_tensor_tensor(out=to[s][:, :], in0=PB[n][:, :], scalar=r2_all[:, bass.ds(t, 1)],
                                               in1=bias_all[:, 1 + k, :], op0=ALU.mult, op1=ALU.add)\
                            .then_inc(f_pre.sem, 1)
                    e.wait_ge(f_prod.sem, f_prod.after(t, 5))
                    e.wait_ge(outs["v"].sems[s], outs["v"].freed(t, s))
                    e.scalar_tensor_tensor(out=V[s][:, :], in0=PB["v"][:, :], scalar=r2_all[:, bass.ds(t, 1)],
                                           in1=bias_all[:, 3, :], op0=ALU.mult, op1=ALU.add)\
                        .then_inc(f_made["v"].sem, 1)

                def sums(t, s):
                    rows = rows_of(t)
                    e.wait_ge(f_acc.sem, f_acc.after(t - 1))
                    e.wait_ge(f_made["q"].sem, f_made["q"].after(t))
                    e.tensor_tensor(qsum[0:rows, :], qsum[0:rows, :], Q[s][0:rows, :], ALU.add)\
                        .then_inc(f_acc.sem, 1)
                    e.wait_ge(f_made["k"].sem, f_made["k"].after(t))
                    e.tensor_tensor(ksum[0:rows, :], ksum[0:rows, :], K[s][0:rows, :], ALU.add)\
                        .then_inc(f_acc.sem, 1)

                def rank_pair(t):
                    e.wait_ge(f_rank.sem, f_rank.after(t - 1))
                    for k in range(2):
                        e.tensor_scalar(rmatch[k][0:EP, :], bucket[0:EP, :], bucket_ids[0:EP, bass.ds(2 * t + k, 1)],
                                        None, ALU.is_equal).then_inc(f_rank.sem, 1)
                    for k in range(2):
                        e.wait_ge(f_rank.sem, f_rank.after(t, 1 + k))
                        e.tensor_tensor_scan(rank[k][0:EP, :], ones_e[0:EP, :], rmatch[k][0:EP, :],
                                             base[0:EP, bass.ds(2 * t + k, 1)], ALU.mult, ALU.add)\
                            .then_inc(f_rank.sem, 1)
                    for k in range(2):
                        e.wait_ge(f_rank.sem, f_rank.after(t, 3 + k))
                        e.wait_ge(f_pos.sem, f_pos.after(t - 1, 1 + k))
                        e.tensor_tensor(placed[k][0:EP, :], rank[k][0:EP, :], rmatch[k][0:EP, :], ALU.mult)\
                            .then_inc(f_rank.sem, 1)

                def rank_some(k, parity):
                    for j in range(RANKED // 2):
                        rank_pair(RANKED // 2 * k + j)

                def place_edges():
                    for t in range(TILES // RANKED * RANKED // 2, RANK_PAIRS):
                        rank_pair(t)
                    e.wait_ge(f_pos.sem, f_pos.after(RANK_PAIRS - 1))
                    e.tensor_scalar(place_i[0:EP, :], pos[0:EP, :], -1.0, None, ALU.add).then_inc(s_rec, 1)
                    e.tensor_scalar(records[0:EP, :, 1], srcs[0:EP, :], P - 1, None, ALU.bitwise_and)\
                        .then_inc(s_rec, 1)
                    e.tensor_copy(records[0:EP, :, 0], dsts[0:EP, :]).then_inc(s_rec, 1)
                    e.wait_ge(s_rec, 3)
                    e.tensor_scalar(high[0:EP, :], place_i[0:EP, :], 7, None, ALU.logical_shift_right)\
                        .then_inc(s_rec, 1)
                    e.tensor_scalar(place_i[0:EP, :], place_i[0:EP, :], P - 1, None, ALU.bitwise_and)\
                        .then_inc(s_rec, 1)
                    e.wait_ge(s_rec, 5)
                    e.scalar_tensor_tensor(out=place_i[0:EP, :], in0=place_i[0:EP, :], scalar=float(ETILES),
                                           in1=high[0:EP, :], op0=ALU.mult, op1=ALU.add).then_inc(s_rec, 1)

                stages(e, TILES, (2, front), (-1, sums), (1, low_part), (0, back),
                       beside=(3, TILES // RANKED, rank_some, place_edges))

            @block.gpsimd
            def _(e):
                def add_places(t, s):
                    for k in range(2):
                        e.wait_ge(f_pos.sem, f_pos.after(t, k) if k else f_pos.after(t - 1))
                        e.wait_ge(f_rank.sem, f_rank.after(t, 5 + k))
                        e.tensor_tensor(pos[0:EP, :], pos[0:EP, :], placed[k][0:EP, :], ALU.add)\
                            .then_inc(f_pos.sem, 1)

                stages(e, RANK_PAIRS, (0, add_places))
                e.wait_ge(s_rec, 6)
                scatter_records(e, rec_d, place_i, records, EP, SCAT, to8, rec8, 0, SCAT_FIRST, scat, f_slot)

            @block.tensor
            def _(e):
                def front(t, s):
                    e.wait_ge(f_xn.sem, f_xn.after(t))
                    e.wait_ge(f_lo.sem, f_lo.freed(t))
                    for c in range(C):
                        mm = e.transpose(PT[s][:, c, :], XN[s][:, c * P:(c + 1) * P], ident[:, :])
                    mm.then_inc(f_pt.sem, 1)

                def back(t, s):
                    e.wait_ge(f_lo.sem, f_lo.after(t))
                    for n in names:
                        ready = {"q": (f_pre, 1), "k": (f_pre, 2)}.get(n, (f_made[n], 1))
                        e.wait_ge(ready[0].sem, ready[0].after(t - 1, ready[1]))
                        split_products(e, PB[n][:, :], XH[s], XL[s], whi[n], wlo[n], C).then_inc(f_prod.sem, 1)

                stages(e, TILES, (1, front), (0, back))

            @block.scalar
            def _(e):
                def front(t, s):
                    e.wait_ge(f_pt.sem, f_pt.after(t))
                    e.wait_ge(f_prod.sem, f_prod.freed(t))
                    e.activation(XH[s][:, :, :], PT[s][:, :, :], ACT.Copy).then_inc(f_hi.sem, 1)

                def back(t, s):
                    e.wait_ge(f_prod.sem, f_prod.after(t, 1))
                    e.wait_ge(outs["neigh"].sems[s], outs["neigh"].freed(t, s))
                    e.activation(YO[s][:, :], PB["neigh"][:, :], ACT.Copy).then_inc(f_made["neigh"].sem, 1)
                    for k, (n, fr, to) in enumerate((("q", QT, Q), ("k", KT, K))):
                        e.wait_ge(f_pre.sem, f_pre.after(t, k + 1))
                        e.wait_ge(outs[n].sems[s], outs[n].freed(t, s))
                        e.wait_ge(f_acc.sem, f_acc.freed(t))
                        e.activation(to[s][:, :], fr[s][:, :], ACT.Sigmoid).then_inc(f_made[n].sem, 1)

                stages(e, TILES, (1, front), (0, back))
        B.close()
        A.close()
        clear_semaphores()

        M = Scope()
        wmix_hi = M.sb("wmix_hi", [P, C, D], F32R)
        wmix_lo = M.sb("wmix_lo", [P, C, D], F32R)
        Cs = Scope()
        G7 = 7
        turns7 = TILES // G7
        assert turns7 * G7 == TILES
        Q = Cs.two("Qc", [P, G7, D])
        K = Cs.two("Kc", [P, G7, D])
        V = Cs.two("Vc", [P, G7, D])
        QA = Cs.sb("QA", [P, G7, D])
        KA = Cs.sb("KA", [P, G7, D])
        q_row = Cs.sb("q_row", [P, D])
        k_row = Cs.sb("k_row", [P, D])
        dots = Cs.two("dots", [P, G7, 2 * H])
        inv = Cs.two("inv", [P, G7, 2 * H])
        si_all = Cs.sb("si_all", [P, TILES, H])
        ex = Cs.two("ex", [P, G7, 2 * H])
        alloc = Cs.sb("alloc", [P, G7, H])
        alloc_inv = Cs.sb("alloc_inv", [P, G7, H])
        scale8 = Cs.sb("scale8", [P, G7, H])
        e_acc = Cs.sb("e_acc", [P, G7, H])
        e_sum = Cs.sb("e_sum", [P, H])
        head_mask = Cs.sb("head_mask", [H, D])
        picked = Cs.sb("picked", [H, 2, D])
        wo_raw = Cs.sb("wo_raw", [P, C, D])
        kv_blocks = Cs.sb("kv_blocks", [P, C, P])
        e_inv = Cs.sb("e_inv", [P, H])
        PQ = Cs.ps("PQ", [P, D])
        PK = Cs.ps("PK", [P, D])
        PSI = Cs.ps("PSI", [P, D])
        PSO = Cs.ps("PSO", [P, D])
        PKV = Cs.ps("PKV", [P, C, P])
        PW = [Cs.ps(f"PW{s}", [P, D]) for s in range(2)]

        s_wo = sem("s_wo")
        s_mask = sem("s_mask")
        s_row = sem("s_row")
        s_rowmm = sem("s_rowmm")
        s_sums = sem("s_sums")
        s_kvn = sem("s_kvn")
        s_esum = sem("s_esum")
        s_wmm = sem("s_wmm")
        s_whi = sem("s_whi")
        s_wlo = sem("s_wlo")
        f_slot = flow("f_slot_b", 2)
        scat = transfers("scat_b", SCAT, credit=0)
        q_in, k_in = transfers("q_in"), transfers("k_in")
        f_sum = flow("f_sum", 6)
        f_use = flow("f_use")
        q_in3, k_in3, v_in3 = transfers("q_in3"), transfers("k_in3"), transfers("v_in3")
        qs_out = transfers("qs_out")
        f_dot = flow("f_dot", 5)
        f_exp = flow("f_exp", 2)
        f_mul = flow("f_mul", 6)
        f_kv = flow("f_kv")
        flows = [f_slot, scat, q_in, k_in, f_sum, f_use, q_in3, k_in3, v_in3, qs_out, f_dot, f_exp, f_mul, f_kv]

        with nc.Block() as block:

            @block.sync
            def _(e):
                give_credit(e, flows)

                def turn_rows_of(d, t):
                    return d[bass.ds(G7 * P * t, G7 * P), :].rearrange("(g p) d -> p g d", p=P)

                def load_sums(t, s):
                    e.wait_ge(f_use.sem, f_use.freed(t))
                    e.dma_start(Q[s][:, :, :], turn_rows_of(q_d, t)).then_inc(q_in.sems[s], 16)
                    e.dma_start(K[s][:, :, :], turn_rows_of(k_d, t)).then_inc(k_in.sems[s], 16)

                stages(e, turns7, (0, load_sums))
                e.dma_start(wo_raw[:, :, :], Wo.rearrange("(c p) n -> p c n", p=P)).then_inc(s_wo, 16)

                def load_mix(t, s):
                    e.wait_ge(f_kv.sem, f_kv.freed(t))
                    e.dma_start(K[s][:, :, :], turn_rows_of(k_d, t)).then_inc(k_in3.sems[s], 16)
                    e.wait_ge(qs_out.sems[s], qs_out.freed(t, s))
                    e.dma_start(Q[s][:, :, :], turn_rows_of(q_d, t)).then_inc(q_in3.sems[s], 16)
                    e.dma_start(V[s][:, :, :], turn_rows_of(v_d, t)).then_inc(v_in3.sems[s], 16)

                def store_qs(t, s):
                    e.wait_ge(f_mul.sem, f_mul.after(t, 5))
                    e.dma_start(turn_rows_of(qs_d, t), Q[s][:, :, :]).then_inc(qs_out.sems[s], 16)

                def load_later(t, s):
                    if not (isinstance(t, int) and t < 2):
                        load_mix(t, s)

                e.wait_ge(f_use.sem, f_use.after(turns7 - 2))
                load_mix(1, 1)
                e.wait_ge(f_use.sem, f_use.after(turns7 - 1))
                load_mix(0, 0)
                stages(e, turns7, (0, store_qs), (2, load_later))
                for s in range(2):
                    e.wait_ge(qs_out.sems[s], qs_out.after(turns7 - 1 - s, (turns7 - 1 - s) % 2))

            @block.gpsimd
            def _(e):
                e.memset(e_acc[:, :, :], 0.0).then_inc(s_mask, 1)
                e.memset(head_mask[:, :], 1.0).then_inc(s_mask, 1)
                e.wait_ge(s_mask, 2)
                e.affine_select(out=head_mask[:, :], in_=head_mask[:, :], compare_op=ALU.is_ge, fill=0.0, base=0,
                                pattern=[[1, D]], channel_multiplier=-DH).then_inc(s_mask, 1)
                e.wait_ge(s_mask, 3)
                e.affine_select(out=head_mask[:, :], in_=head_mask[:, :], compare_op=ALU.is_ge, fill=0.0,
                                base=DH - 1, pattern=[[-1, D]], channel_multiplier=DH).then_inc(s_mask, 1)
                scatter_records(e, rec_d, place_i, records, EP, SCAT, to8, rec8, SCAT_FIRST, SCAT_TURNS - SCAT_FIRST,
                                scat, f_slot)

            @block.tensor
            def _(e):
                e.matmul(PQ[:, :], ones[:, :], qsum[:, :], start=True, stop=True).then_inc(s_rowmm, 1)
                e.matmul(PK[:, :], ones[:, :], ksum[:, :], start=True, stop=True).then_inc(s_rowmm, 1)
                for bank in (PSI, PSO):
                    e.matmul(bank[0:H, :], zeros[:, 0:H], zeros[:, :], start=True, stop=False)

                def rows_in(t, g):
                    return TAIL if isinstance(t, int) and G7 * t + g == TILES - 1 else P

                def sums(t, s):
                    e.wait_ge(f_sum.sem, f_sum.after(t, 5))
                    for g in range(G7):
                        rows = rows_in(t, g)
                        last = isinstance(t, int) and t == turns7 - 1 and g == G7 - 1
                        e.matmul(PSI[0:H, :], inv[s][0:rows, g, 0:H], Q[s][0:rows, g, :], start=False, stop=last)
                        mm = e.matmul(PSO[0:H, :], inv[s][0:rows, g, H:2 * H], K[s][0:rows, g, :], start=False,
                                      stop=last)
                    mm.then_inc(f_use.sem, 1)

                stages(e, turns7, (0, sums))
                e.wait_ge(s_sums, 2)
                e.matmul(PQ[:, :], ones[0:H, :], picked[:, 0, :], start=True, stop=True).then_inc(s_rowmm, 1)
                e.matmul(PK[:, :], ones[0:H, :], picked[:, 1, :], start=True, stop=True).then_inc(s_rowmm, 1)
                e.matmul(PKV[:, :, :].rearrange("p c m -> p (c m)"), zeros[:, 0:P], zeros[:, :], start=True,
                         stop=False)

                def kv(t, s):
                    e.wait_ge(f_mul.sem, f_mul.after(t, 4))
                    for g in range(G7):
                        rows = rows_in(t, g)
                        for c in range(C):
                            mm = e.matmul(PKV[:, c, :], V[s][0:rows, g, c * P:(c + 1) * P],
                                          K[s][0:rows, g, c * P:(c + 1) * P], start=False, stop=False,
                                          skip_group_check=True)
                    mm.then_inc(f_kv.sem, 1)

                stages(e, turns7, (0, kv))
                e.matmul(PKV[:, :, :].rearrange("p c m -> p (c m)"), zeros[:, 0:P], zeros[:, :], start=False,
                         stop=True)
                e.wait_ge(s_esum, 1)
                e.matmul(PSI[:, 0:H], ones[:, :], e_sum[:, :], start=True, stop=True).then_inc(s_rowmm, 1)
                e.wait_ge(s_wo, 16)
                for c in range(C):
                    e.wait_ge(s_kvn, 2 + c + 1)
                    if c >= 2:
                        e.wait_ge(s_wlo, c - 1)
                    e.matmul(PW[c % 2][:, :], kv_blocks[:, c, :], wo_raw[:, c, :], start=True, stop=True)\
                        .then_inc(s_wmm, 1)

            @block.scalar
            def _(e):
                def exps(t, s):
                    e.wait_ge(f_dot.sem, f_dot.after(t))
                    e.activation(ex[s][:, :, 0:H], dots[s][:, :, 0:H], ACT.Exp, scale=-1.0).then_inc(f_exp.sem, 1)
                    e.activation(ex[s][:, :, H:2 * H], dots[s][:, :, H:2 * H], ACT.Exp).then_inc(f_exp.sem, 1)

                stages(e, turns7, (0, exps))
                for c in range(C):
                    e.wait_ge(s_wmm, c + 1)
                    e.activation(wmix_hi[:, c, :], PW[c % 2][:, :], ACT.Copy).then_inc(s_whi, 1)

            @block.vector
            def _(e):
                e.wait_ge(s_rowmm, 2)
                e.tensor_scalar(q_row[:, :], PQ[:, :], EPS_FLOW, None, ALU.add).then_inc(s_row, 1)
                e.tensor_scalar(k_row[:, :], PK[:, :], EPS_FLOW, None, ALU.add).then_inc(s_row, 1)
                e.wait_ge(s_row, 2)

                def heads(a):
                    return a[:, :, :].rearrange("p g (h d) -> p g h d", h=H)

                def dot(t, s, ins, f, row_of_q, row_of_k):
                    e.wait_ge(ins[0].sems[s], ins[0].after(t, s))
                    e.wait_ge(ins[1].sems[s], ins[1].after(t, s))
                    e.wait_ge(f.sem, f.after(t - 1))
                    for a, b, row in ((QA, Q, row_of_q), (KA, K, row_of_k)):
                        e.scalar_tensor_tensor(out=a[:, :, :], in0=b[s][:, :, :], scalar=EPS_FLOW,
                                               in1=row[:, :].unsqueeze(1).broadcast_to([P, G7, D]),
                                               op0=ALU.add, op1=ALU.mult).then_inc(f.sem, 1)
                    for i, a in enumerate((QA, KA)):
                        e.wait_ge(f.sem, f.after(t, i + 1))
                        e.tensor_reduce(dots[s][:, :, i * H:(i + 1) * H], heads(a), AX.X, ALU.add)\
                            .then_inc(f.sem, 1)
                    e.wait_ge(f.sem, f.after(t, 4))

                def sums(t, s):
                    dot(t, s, (q_in, k_in), f_sum, k_row, q_row)
                    e.wait_ge(f_use.sem, f_use.freed(t))
                    e.reciprocal(inv[s][:, :, :], dots[s][:, :, :]).then_inc(f_sum.sem, 1)
                    e.wait_ge(f_sum.sem, f_sum.after(t, 5))
                    e.tensor_copy(si_all[:, bass.ds(G7 * t, G7), :], inv[s][:, :, 0:H]).then_inc(f_sum.sem, 1)

                stages(e, turns7, (0, sums))
                e.wait_ge(f_use.sem, f_use.after(turns7 - 1))
                e.wait_ge(s_mask, 4)
                e.tensor_tensor(picked[:, 0, :], PSI[0:H, :], head_mask[:, :], ALU.mult).then_inc(s_sums, 1)
                e.tensor_tensor(picked[:, 1, :], PSO[0:H, :], head_mask[:, :], ALU.mult).then_inc(s_sums, 1)
                e.wait_ge(s_rowmm, 4)
                e.tensor_scalar(q_row[:, :], PQ[:, :], EPS_FLOW, None, ALU.add).then_inc(s_row, 1)
                e.tensor_scalar(k_row[:, :], PK[:, :], EPS_FLOW, None, ALU.add).then_inc(s_row, 1)
                e.wait_ge(s_row, 4)

                def dots3(t, s):
                    e.wait_ge(f_exp.sem, f_exp.freed(t))
                    dot(t, s, (q_in3, k_in3), f_dot, k_row, q_row)
                    e.tensor_scalar(dots[s][:, :, H:2 * H], dots[s][:, :, H:2 * H], -1.0, 1.0, ALU.max, ALU.min)\
                        .then_inc(f_dot.sem, 1)

                def wide(a):
                    return a.unsqueeze(3).broadcast_to([P, G7, H, DH])

                def mix(t, s):
                    e.wait_ge(f_exp.sem, f_exp.after(t))
                    e.tensor_scalar(alloc[:, :, :], ex[s][:, :, 0:H], 1.0, None, ALU.add).then_inc(f_mul.sem, 1)
                    e.wait_ge(f_mul.sem, f_mul.after(t, 1))
                    e.reciprocal(alloc_inv[:, :, :], alloc[:, :, :]).then_inc(f_mul.sem, 1)
                    e.wait_ge(f_mul.sem, f_mul.after(t, 2))
                    e.tensor_tensor(scale8[:, :, :], si_all[:, bass.ds(G7 * t, G7), :], alloc_inv[:, :, :],
                                    ALU.mult).then_inc(f_mul.sem, 1)
                    e.wait_ge(v_in3.sems[s], v_in3.after(t, s))
                    e.tensor_tensor(heads(V[s]), heads(V[s]), wide(ex[s][:, :, H:2 * H]), ALU.mult)\
                        .then_inc(f_mul.sem, 1)
                    e.wait_ge(f_mul.sem, f_mul.after(t, 3))
                    e.tensor_tensor(heads(Q[s]), heads(Q[s]), wide(scale8[:, :, :]), ALU.mult)\
                        .then_inc(f_mul.sem, 1)
                    if isinstance(t, int) and t == turns7 - 1:
                        e.tensor_tensor(e_acc[:, 0:G7 - 1, :], e_acc[:, 0:G7 - 1, :], ex[s][:, 0:G7 - 1, H:2 * H],
                                        ALU.add)
                        e.tensor_tensor(e_acc[0:TAIL, G7 - 1, :], e_acc[0:TAIL, G7 - 1, :],
                                        ex[s][0:TAIL, G7 - 1, H:2 * H], ALU.add).then_inc(f_mul.sem, 1)
                    else:
                        e.tensor_tensor(e_acc[:, :, :], e_acc[:, :, :], ex[s][:, :, H:2 * H], ALU.add)\
                            .then_inc(f_mul.sem, 1)

                stages(e, turns7, (0, dots3), (0, mix))
                e.wait_ge(f_mul.sem, f_mul.after(turns7 - 1))
                e.tensor_reduce(e_sum[:, :], e_acc[:, :, :].rearrange("p g h -> p h g"), AX.X, ALU.add)\
                    .then_inc(s_esum, 1)
                e.wait_ge(s_rowmm, 5)
                e.reciprocal(e_inv[:, :], PSI[:, 0:H]).then_inc(s_kvn, 1)
                e.wait_ge(s_kvn, 1)
                e.tensor_scalar(e_inv[:, :], e_inv[:, :], float(N), None, ALU.mult).then_inc(s_kvn, 1)
                e.wait_ge(s_kvn, 2)
                e.wait_ge(f_kv.sem, f_kv.after(turns7 - 1))
                for c in range(C):
                    for h in range(P // DH):
                        r = slice(h * DH, (h + 1) * DH)
                        ins = e.scalar_tensor_tensor(out=kv_blocks[r, c, :], in0=PKV[r, c, :],
                                                     scalar=e_inv[r, c * (P // DH) + h:c * (P // DH) + h + 1],
                                                     in1=block_mask[r, :], op0=ALU.mult, op1=ALU.mult)
                    ins.then_inc(s_kvn, 1)
                for c in range(C):
                    e.wait_ge(s_whi, c + 1)
                    e.tensor_tensor(wmix_lo[:, c, :], PW[c % 2][:, :], wmix_hi[:, c, :].bitcast(F32),
                                    ALU.subtract).then_inc(s_wlo, 1)
        Cs.close()

        R = Scope()
        agg = R.sb("agg", [P, TILES * D])
        Ds = Scope()
        turns = ETILES // GRP
        table = Ds.sb("table", [P, ETILES, 2], I32)
        row_f = Ds.sb("row_f", [P, ETILES])
        columns = Ds.sb("columns", [P, P])
        from8 = Ds.two("from8", [P, GRP], I32)
        gathered = [[Ds.sb(f"gathered{s}_{j}", [P, D]) for j in range(GRP)] for s in range(2)]
        onehot = Ds.two("onehot", [P, GRP, P])
        PA = [Ds.ps(f"PA{j}", [P, D]) for j in range(GRP)]
        s_table = sem("s_table")
        s_agg = sem("s_agg")
        s_cols = sem("s_cols")
        s_rowf = sem("s_rowf")
        f_from = flow("f_from")
        f_pace = flow("f_pace")
        g_in = [transfers(f"g_in{j}_", credit=0) for j in range(GRP)]
        f_hot = flow("f_hot")
        f_emm = flow("f_emm", GRP)
        f_add = flow("f_add", GRP)
        flows = [f_from, f_pace, *g_in, f_hot, f_emm, f_add]

        with nc.Block() as block:

            @block.sync
            def _(e):
                give_credit(e, flows)
                e.dma_start(table[:, :, :].rearrange("p t w -> p (t w)"),
                            rec_d.rearrange("(p t) w -> p (t w)", p=P)).then_inc(s_table, 16)
                e.dma_start(agg[:, :].rearrange("p (t d) -> p t d", d=D),
                            self_d.rearrange("(t p) d -> p t d", p=P)).then_inc(s_agg, 16)

            @block.gpsimd
            def _(e):
                e.iota(columns[:, :], pattern=[[1, P]], base=0, channel_multiplier=0,
                       allow_small_or_imprecise_dtypes=True).then_inc(s_cols, 1)
                e.wait_ge(s_table, 16)

                def gather(t, s):
                    e.wait_ge(f_emm.sem, f_emm.freed(t))
                    e.wait_ge(f_from.sem, f_from.after(t))
                    e.wait_ge(f_pace.sem, f_pace.after(t - 1))
                    e.tensor_tensor(pace[:, 1:2], zeros[:, 0:1], zeros[:, 1:2], ALU.add).then_inc(f_pace.sem, 1)
                    for j in range(GRP):
                        e.indirect_dma_start(gathered[s][j][:, :], None, y_d,
                                             bass.IndirectOffsetOnAxis(from8[s][:, j:j + 1], 0))\
                            .then_inc(g_in[j].sems[s], 16)

                stages(e, turns, (0, gather))

            @block.tensor
            def _(e):
                def spread(t, s):
                    e.wait_ge(f_hot.sem, f_hot.after(t))
                    for j in range(GRP):
                        e.wait_ge(g_in[j].sems[s], g_in[j].after(t, s))
                        e.wait_ge(f_add.sem, f_add.after(t - 1, j + 1))
                        e.matmul(PA[j][:, :], onehot[s][:, j, :], gathered[s][j][:, :], start=True, stop=True)\
                            .then_inc(f_emm.sem, 1)

                stages(e, turns, (0, spread))

            @block.vector
            def _(e):
                e.wait_ge(s_table, 16)
                e.tensor_copy(row_f[:, :], table[:, :, 1]).then_inc(s_rowf, 1)
                e.wait_ge(s_rowf, 1)
                e.wait_ge(s_cols, 1)

                def hot(t, s):
                    e.wait_ge(f_emm.sem, f_emm.freed(t))
                    e.tensor_tensor(onehot[s][:, :, :], columns[:, :].unsqueeze(1).broadcast_to([P, GRP, P]),
                                    row_f[:, bass.ds(GRP * t, GRP)].unsqueeze(2).broadcast_to([P, GRP, P]),
                                    ALU.is_equal).then_inc(f_hot.sem, 1)

                def indices(t, s):
                    e.wait_ge(f_emm.sem, f_emm.freed(t))
                    e.tensor_copy(from8[s][:, :], table[:, bass.ds(GRP * t, GRP), 0]).then_inc(f_from.sem, 1)

                def add(t, s):
                    e.wait_ge(s_agg, 16)
                    for j in range(GRP):
                        b = e.value_load(bucket_of_tile[0:1, bass.ds(GRP * t + j, 1)], min_val=0,
                                         max_val=TILES - 1)
                        rows = agg[:, bass.ds(b * D, D)]
                        e.wait_ge(f_add.sem, f_add.after(t, j) if j else f_add.after(t - 1))
                        e.wait_ge(f_emm.sem, f_emm.after(t, j + 1))
                        e.tensor_tensor(rows, rows, PA[j][:, :], ALU.add).then_inc(f_add.sem, 1)

                stages(e, turns, (1, hot), (0, add), (2, indices))
        Ds.close()
        clear_semaphores()

        Es = Scope()
        w1_hi = Es.sb("w1_hi", [P, C, HID], F32R)
        w1_lo = Es.sb("w1_lo", [P, C, HID], F32R)
        w2_hi = Es.sb("w2_hi", [P, HC, D], F32R)
        w2_lo = Es.sb("w2_lo", [P, HC, D], F32R)
        b1_rows = Es.sb("b1_rows", [P, HID])
        rows2 = Es.sb("rows2", [P, 2, D])
        wr_pair = Es.sb("wr_pair", [P, C, 2, EXPERTS], F32R)
        J = 2 * TILES
        list_d = dram("list_d", [P * ST, 2], I32)
        ysl_d = dram("ysl_d", [ST * P, D])
        z_d = dram("z_d", [NP, D])
        Es1 = Scope()
        raw1 = Es1.sb("w1_raw", [P, C, HID])
        raw2 = Es1.sb("w2_raw", [P, HC, D])
        g2col = Es1.sb("g2col", [P, C])
        be2col = Es1.sb("be2col", [P, C])
        be2_wide = Es1.sb("be2_wide", [P, C, P])
        wr_raw = Es1.sb("wr_raw", [P, C, EXPERTS])
        br_raw = Es1.sb("br_raw", [1, EXPERTS])
        b1raw = Es1.sb("b1raw", [1, HID])
        brow2 = Es1.sb("brow2", [1, 2, D])
        PR = Es1.ps("PR", [P, 2, D])
        PR2 = Es1.ps("PR2", [P, D])
        PR3 = Es1.ps("PR3", [P, D])
        s_in4 = sem("s_in4")
        s_wide4 = sem("s_wide4")
        s_mm4 = sem("s_mm4")
        s_hi4 = sem("s_hi4")
        s_v4 = sem("s_v4")

        with nc.Block() as block:

            @block.sync
            def _(e):
                e.dma_start(raw1[:, :, :], W1.rearrange("(c p) n -> p c n", p=P)).then_inc(s_in4, 16)
                e.dma_start(raw2[:, :, :], W2.rearrange("(c p) n -> p c n", p=P)).then_inc(s_in4, 16)
                e.dma_start(wr_raw[:, :, :], Wr.rearrange("(c p) n -> p c n", p=P)).then_inc(s_in4, 16)
                e.dma_start(br_raw[:, :], br.rearrange("(a n) -> a n", a=1)).then_inc(s_in4, 16)
                e.dma_start(g2col[:, :], g2).then_inc(s_in4, 16)
                e.dma_start(be2col[:, :], be2).then_inc(s_in4, 16)
                e.dma_start(b1raw[:, :], b1.rearrange("(a n) -> a n", a=1)).then_inc(s_in4, 16)
                e.dma_start(brow2[:, 0, :], bo.rearrange("(a n) -> a n", a=1)).then_inc(s_in4, 16)
                e.dma_start(brow2[:, 1, :], b2.rearrange("(a n) -> a n", a=1)).then_inc(s_in4, 16)

            @block.tensor
            def _(e):
                e.wait_ge(s_in4, 16 * 9)
                for i in range(2):
                    e.matmul(PR[:, i, :], ones[0:1, :], brow2[:, i, :], start=True, stop=True)
                e.matmul(PR3[:, 0:EXPERTS], ones[0:1, :], br_raw[:, :], start=True, stop=True)
                e.wait_ge(s_wide4, C)
                e.matmul(PR2[:, 0:HID], ones[0:1, :], b1raw[:, :], start=True, stop=False)
                for c in range(C):
                    mm = e.matmul(PR2[:, 0:HID], be2_wide[:, c, :], raw1[:, c, :], start=False, stop=(c == C - 1))
                mm.then_inc(s_mm4, 1)

            @block.scalar
            def _(e):
                e.wait_ge(s_in4, 16 * 9)
                for c in range(C):
                    e.activation(w1_hi[:, c, :], raw1[:, c, :], ACT.Copy, scale=g2col[:, c:c + 1])\
                        .then_inc(s_hi4, 1)
                e.activation(wr_pair[:, :, 0, :], wr_raw[:, :, :], ACT.Copy).then_inc(s_hi4, 1)
                for c in range(HC):
                    e.activation(w2_hi[:, c, :], raw2[:, c, :], ACT.Copy).then_inc(s_hi4, 1)

            @block.vector
            def _(e):
                e.wait_ge(s_in4, 16 * 9)
                for c in range(C):
                    e.tensor_scalar(be2_wide[:, c, :], ones[:, :], be2col[:, c:c + 1], None, ALU.mult)\
                        .then_inc(s_wide4, 1)
                e.wait_ge(s_hi4, C + 1 + HC)
                for c in range(C):
                    e.scalar_tensor_tensor(out=w1_lo[:, c, :], in0=raw1[:, c, :], scalar=g2col[:, c:c + 1],
                                           in1=w1_hi[:, c, :].bitcast(F32), op0=ALU.mult, op1=ALU.subtract)
                e.tensor_tensor(w2_lo[:, :, :], raw2[:, :, :], w2_hi[:, :, :].bitcast(F32), ALU.subtract)
                e.wait_ge(s_mm4, 1)
                e.tensor_tensor(wr_pair[:, :, 1, :], wr_raw[:, :, :], wr_pair[:, :, 0, :].bitcast(F32), ALU.subtract)
                e.tensor_copy(b1_rows[:, :], PR2[:, 0:HID])
                e.tensor_copy(br_rows[:, :], PR3[:, 0:EXPERTS])
                e.tensor_copy(rows2[:, :, :], PR[:, :, :]).then_inc(s_v4, 1)
        Es1.close()

        X = Es.two("Xe", [P, D])
        Y = Es.two("Ye", [P, D])
        QS = Es.two("QSe", [P, D])
        U = Es.sb("Ue", [P, D])
        QH = Es.two("QH", [P, C, P], F32R)
        QL = Es.two("QL", [P, C, P], F32R)
        UH = Es.two("UH", [P, C, P], F32R)
        UL = Es.two("UL", [P, C, P], F32R)
        HB = Es.sb("HB", [P, HID])
        HG = Es.two("HG", [P, HID])
        Z = Es.two("Ze", [P, D])
        ZH = Es.two("ZHe", [P, C, P], F32R)
        ZL = Es.two("ZLe", [P, C, P], F32R)
        stats1 = Es.two("stats1", [P, 6])
        mv1 = Es.two("mv1", [P, 2])
        rs1 = Es.two("rs1", [P, 1])
        sc1 = Es.sb("sc1", [P, 1])
        HH = Es.sb("HH", [P, HC, P], F32R)
        HL = Es.sb("HL", [P, HC, P], F32R)
        stats = Es.two("stats_e", [P, 6])
        mv = Es.two("mv_e", [P, 2])
        rs = Es.two("rs_e", [P, 1])
        sc = Es.sb("sc_e", [P, 1])
        PTQ = Es.ps("PTQ", [P, C, P])
        PTU = Es.ps("PTU", [P, C, P])
        PO = Es.ps("PO", [P, D])
        PH = Es.ps("PH", [P, D])
        PHT = Es.ps("PHT", [P, C, P])
        PF = Es.ps("PF", [P, D])
        PTZ = Es.ps("PTZ", [P, C, P])
        PLG = Es.ps("PLG", [P, D])
        x_in, xn_in, qs_in, x1_out = transfers("x_in4"), transfers("xn_in4"), transfers("qs_in4"), transfers("x1_out")
        f_tq = flow("f_tq")
        f_qh = flow("f_qh")
        f_ql = flow("f_ql")
        f_po = flow("f_po")
        f_xnb = flow("f_xnb")
        f_y = flow("f_y")
        f_st = flow("f_st")
        f_mv = flow("f_mv4")
        f_rs = flow("f_rs4", 2)
        f_u = flow("f_u")
        f_tu = flow("f_tu")
        f_uh = flow("f_uh")
        f_ul = flow("f_ul")
        f_ph = flow("f_ph")
        f_hb = flow("f_hb")
        f_hg = flow("f_hg")
        f_th = flow("f_th")
        f_hh = flow("f_hh")
        f_hl = flow("f_hl")
        f_pf = flow("f_pf")
        f_relu = flow("f_relu")
        f_sum = flow("f_sum4", 2)
        f_x1 = flow("f_x1")
        f_st1 = flow("f_st1")
        f_mv1 = flow("f_mv1")
        f_rs1 = flow("f_rs1", 2)
        f_z = flow("f_z")
        f_tz = flow("f_tz")
        f_zh = flow("f_zh")
        f_zl = flow("f_zl")
        f_lg = flow("f_lg")
        f_la = flow("f_la")
        z_out = transfers("z_out")
        flows = [x_in, xn_in, qs_in, x1_out, f_tq, f_qh, f_ql, f_po, f_xnb, f_y, f_st, f_mv, f_rs, f_u, f_tu, f_uh,
                 f_ul, f_ph, f_hb, f_hg, f_th, f_hh, f_hl, f_pf, f_relu, f_sum, f_x1, f_st1,
                 f_mv1, f_rs1, f_z, f_tz, f_zh, f_zl, f_lg, f_la, z_out]

        with nc.Block() as block:

            @block.sync
            def _(e):
                give_credit(e, flows)

                def load_qs(t, s):
                    e.wait_ge(f_tq.sem, f_tq.freed(t))
                    e.dma_start(QS[s][:, :], tile_rows(qs_d, t)).then_inc(qs_in.sems[s], 16)

                def load_x(t, s):
                    rows = rows_of(t)
                    e.wait_ge(f_relu.sem, f_relu.freed(t))
                    e.dma_start(X[s][0:rows, :], tile_rows(x, t, rows)).then_inc(x_in.sems[s], 16)

                def load_xn(t, s):
                    e.wait_ge(f_u.sem, f_u.freed(t))
                    e.wait_ge(f_sum.sem, f_sum.freed(t))
                    e.dma_start(Y[s][:, :], tile_rows(xn_d, t)).then_inc(xn_in.sems[s], 16)

                def store(t, s):
                    e.wait_ge(f_x1.sem, f_x1.after(t))
                    e.dma_start(tile_rows(x1_d, t), agg[:, bass.ds(t * D, D)]).then_inc(x1_out.sems[s], 16)

                def store_z(t, s):
                    e.wait_ge(f_z.sem, f_z.after(t))
                    e.dma_start(tile_rows(z_d, t), Z[s][:, :]).then_inc(z_out.sems[s], 16)

                stages(e, TILES, (4, load_qs), (4, load_x), (-1, store_z), (0, store), (4, load_xn))
                for s in range(2):
                    e.wait_ge(z_out.sems[s], z_out.after(TILES - 1 - s, (TILES - 1 - s) % 2))
                    e.wait_ge(x1_out.sems[s], x1_out.after(TILES - 1 - s, (TILES - 1 - s) % 2))

            @block.gpsimd
            def _(e):
                def root(t, s):
                    e.wait_ge(f_mv.sem, f_mv.after(t))
                    e.tensor_tensor(sc[:, :], mv[s][:, 1:2], eps_c, ALU.add).then_inc(f_rs.sem, 1)
                    e.wait_ge(f_rs.sem, f_rs.after(t, 1))
                    e.tensor_tensor(rs[s][:, :], sc[:, :], mhalf, ALU.pow).then_inc(f_rs.sem, 1)

                def xn_with_bias(t, s):
                    e.wait_ge(xn_in.sems[s], xn_in.after(t, s))
                    e.tensor_tensor(Y[s][:, :], Y[s][:, :], rows2[:, 0, :], ALU.add).then_inc(f_xnb.sem, 1)

                def sum_up(t, s):
                    rows = agg[:, bass.ds(t * D, D)]
                    e.wait_ge(f_relu.sem, f_relu.after(t))
                    e.wait_ge(f_y.sem, f_y.after(t))
                    e.tensor_tensor(pace[:, 1:2], zeros[:, 0:1], zeros[:, 1:2], ALU.add)
                    e.tensor_tensor(rows, rows, Y[s][:, :], ALU.add).then_inc(f_sum.sem, 1)
                    e.wait_ge(f_sum.sem, f_sum.after(t, 1))
                    e.tensor_tensor(pace[:, 1:2], zeros[:, 0:1], zeros[:, 1:2], ALU.add)
                    e.tensor_tensor(rows, rows, rows2[:, 1, :], ALU.add).then_inc(f_sum.sem, 1)

                def root1(t, s):
                    e.wait_ge(f_mv1.sem, f_mv1.after(t))
                    e.tensor_tensor(sc1[:, :], mv1[s][:, 1:2], eps_c, ALU.add).then_inc(f_rs1.sem, 1)
                    e.wait_ge(f_rs1.sem, f_rs1.after(t, 1))
                    e.tensor_tensor(rs1[s][:, :], sc1[:, :], mhalf, ALU.pow).then_inc(f_rs1.sem, 1)

                stages(e, TILES, (-1, root1), (2, root), (3, xn_with_bias), (2, sum_up))

            @block.tensor
            def _(e):
                def turn_u(t, s):
                    e.wait_ge(f_u.sem, f_u.after(t))
                    e.wait_ge(f_ul.sem, f_ul.after(t - 1))
                    for c in range(C):
                        mm = e.transpose(PTU[:, c, :], U[:, c * P:(c + 1) * P], ident[:, :])
                    mm.then_inc(f_tu.sem, 1)

                def attention(t, s):
                    e.wait_ge(f_ql.sem, f_ql.after(t))
                    e.wait_ge(f_y.sem, f_y.after(t - 1))
                    split_products(e, PO[:, :], QH[s], QL[s], wmix_hi, wmix_lo, C).then_inc(f_po.sem, 1)

                def first_products(t, s):
                    e.wait_ge(f_ul.sem, f_ul.after(t))
                    e.wait_ge(f_hb.sem, f_hb.after(t - 1))
                    split_products(e, PH[:, 0:HID], UH[s], UL[s], w1_hi, w1_lo, C).then_inc(f_ph.sem, 1)

                def turn_q(t, s):
                    e.wait_ge(qs_in.sems[s], qs_in.after(t, s))
                    e.wait_ge(f_ql.sem, f_ql.after(t - 1))
                    for c in range(C):
                        mm = e.transpose(PTQ[:, c, :], QS[s][:, c * P:(c + 1) * P], ident[:, :])
                    mm.then_inc(f_tq.sem, 1)

                def second_products(t, s):
                    e.wait_ge(f_hl.sem, f_hl.after(t))
                    e.wait_ge(f_x1.sem, f_x1.after(t - 1))
                    split_products(e, PF[:, :], HH, HL, w2_hi, w2_lo, HC).then_inc(f_pf.sem, 1)

                def turn_hidden(t, s):
                    e.wait_ge(f_hg.sem, f_hg.after(t))
                    e.wait_ge(f_hl.sem, f_hl.after(t - 1))
                    for m in range(HC):
                        mm = e.transpose(PHT[:, m, :], HG[s][:, m * P:(m + 1) * P], ident[:, :])
                    mm.then_inc(f_th.sem, 1)

                def turn_z(t, s):
                    e.wait_ge(f_z.sem, f_z.after(t))
                    e.wait_ge(f_zl.sem, f_zl.after(t - 1))
                    for c in range(C):
                        mm = e.transpose(PTZ[:, c, :], Z[s][:, c * P:(c + 1) * P], ident[:, :])
                    mm.then_inc(f_tz.sem, 1)

                def router(t, s):
                    e.wait_ge(f_zl.sem, f_zl.after(t))
                    e.wait_ge(f_la.sem, f_la.after(t - 1))
                    for c in range(C):
                        for a in (ZH, ZL):
                            mm = e.matmul(PLG[:, 0:2 * EXPERTS], a[s][:, c, :],
                                          wr_pair[:, c, :, :].rearrange("p h n -> p (h n)"),
                                          start=(c == 0 and a is ZH), stop=(c == C - 1 and a is ZL))
                    mm.then_inc(f_lg.sem, 1)

                stages(e, TILES, (1, turn_u), (2, attention), (1, first_products), (-1, turn_z), (3, turn_q),
                       (-2, router), (0, second_products), (1, turn_hidden))

            @block.scalar
            def _(e):
                def high_u(t, s):
                    e.wait_ge(f_tu.sem, f_tu.after(t))
                    e.wait_ge(f_ph.sem, f_ph.freed(t))
                    e.activation(UH[s][:, :, :], PTU[:, :, :], ACT.Copy).then_inc(f_uh.sem, 1)

                def gelu(t, s):
                    e.wait_ge(f_hb.sem, f_hb.after(t))
                    e.wait_ge(f_th.sem, f_th.freed(t))
                    e.activation(HG[s][:, :], HB[:, :], ACT.Gelu).then_inc(f_hg.sem, 1)

                def high_q(t, s):
                    e.wait_ge(f_tq.sem, f_tq.after(t))
                    e.wait_ge(f_po.sem, f_po.freed(t))
                    e.activation(QH[s][:, :, :], PTQ[:, :, :], ACT.Copy).then_inc(f_qh.sem, 1)

                def high_hidden(t, s):
                    e.wait_ge(f_th.sem, f_th.after(t))
                    e.wait_ge(f_pf.sem, f_pf.after(t - 1))
                    e.activation(HH[:, :, :], PHT[:, 0:HC, :], ACT.Copy).then_inc(f_hh.sem, 1)

                def high_z(t, s):
                    e.wait_ge(f_tz.sem, f_tz.after(t))
                    e.wait_ge(f_lg.sem, f_lg.freed(t))
                    e.activation(ZH[s][:, :, :], PTZ[:, :, :], ACT.Copy).then_inc(f_zh.sem, 1)

                stages(e, TILES, (1, high_u), (1, gelu), (-1, high_z), (3, high_q), (1, high_hidden))

            @block.vector
            def _(e):
                def low(to, bank, hi, f_high, f_low, t):
                    e.wait_ge(f_high.sem, f_high.after(t))
                    e.tensor_tensor(to[:, :, :], bank, hi[:, :, :].bitcast(F32), ALU.subtract)\
                        .then_inc(f_low.sem, 1)

                def low_u(t, s):
                    low(UL[s], PTU[:, :, :], UH[s], f_uh, f_ul, t)

                def low_q(t, s):
                    low(QL[s], PTQ[:, :, :], QH[s], f_qh, f_ql, t)

                def low_hidden(t, s):
                    low(HL, PHT[:, 0:HC, :], HH, f_hh, f_hl, t)

                def relu_x(t, s):
                    rows = agg[:, bass.ds(t * D, D)]
                    e.wait_ge(x_in.sems[s], x_in.after(t, s))
                    e.scalar_tensor_tensor(out=rows, in0=rows, scalar=0.0, in1=X[s][:, :], op0=ALU.max,
                                           op1=ALU.add).then_inc(f_relu.sem, 1)

                def y_statistics(t, s):
                    e.wait_ge(f_po.sem, f_po.after(t))
                    e.wait_ge(f_xnb.sem, f_xnb.after(t))
                    e.tensor_tensor(Y[s][:, :], PO[:, :], Y[s][:, :], ALU.add).then_inc(f_y.sem, 1)
                    e.wait_ge(f_y.sem, f_y.after(t))
                    e.bn_stats(stats[s][:, :], Y[s][:, :]).then_inc(f_st.sem, 1)
                    e.wait_ge(f_st.sem, f_st.after(t))
                    e.memset(pace[:, 0:1], 0.0)
                    e.bn_aggr(mv[s][:, :], stats[s][:, :]).then_inc(f_mv.sem, 1)

                def bias(t, s):
                    e.wait_ge(f_ph.sem, f_ph.after(t))
                    e.wait_ge(f_hg.sem, f_hg.after(t - 1))
                    e.tensor_tensor(HB[:, :], PH[:, 0:HID], b1_rows[:, :], ALU.add).then_inc(f_hb.sem, 1)

                def normal(t, s):
                    e.wait_ge(f_rs.sem, f_rs.after(t))
                    e.wait_ge(f_tu.sem, f_tu.after(t - 1))
                    e.tensor_scalar(U[:, :], Y[s][:, :], mv[s][:, 0:1], rs[s][:, :], ALU.subtract, ALU.mult)\
                        .then_inc(f_u.sem, 1)

                def x1_statistics(t, s):
                    e.wait_ge(f_pf.sem, f_pf.after(t))
                    e.wait_ge(f_sum.sem, f_sum.after(t))
                    rows = agg[:, bass.ds(t * D, D)]
                    e.tensor_tensor(rows, PF[:, :], rows, ALU.add).then_inc(f_x1.sem, 1)
                    e.wait_ge(f_x1.sem, f_x1.after(t))
                    e.memset(pace[:, 0:1], 0.0)
                    e.bn_stats(stats1[s][:, :], rows).then_inc(f_st1.sem, 1)
                    e.wait_ge(f_st1.sem, f_st1.after(t))
                    e.memset(pace[:, 0:1], 0.0)
                    e.bn_aggr(mv1[s][:, :], stats1[s][:, :]).then_inc(f_mv1.sem, 1)

                def normal_z(t, s):
                    e.wait_ge(f_rs1.sem, f_rs1.after(t))
                    e.wait_ge(f_tz.sem, f_tz.freed(t))
                    e.wait_ge(z_out.sems[s], z_out.freed(t, s))
                    e.tensor_scalar(Z[s][:, :], agg[:, bass.ds(t * D, D)], mv1[s][:, 0:1], rs1[s][:, :],
                                    ALU.subtract, ALU.mult).then_inc(f_z.sem, 1)

                def low_z(t, s):
                    low(ZL[s], PTZ[:, :, :], ZH[s], f_zh, f_zl, t)

                def logits_of(t, s):
                    e.wait_ge(f_lg.sem, f_lg.after(t))
                    e.tensor_tensor(both[:, bass.ds(t, 1), :].rearrange("p t n -> p (t n)"), PLG[:, 0:2 * EXPERTS],
                                    zeros[:, 0:2 * EXPERTS], ALU.add).then_inc(f_la.sem, 1)

                stages(e, TILES, (1, low_u), (2, relu_x), (-1, normal_z), (2, y_statistics), (1, bias),
                       (2, normal), (-1, low_z), (3, low_q), (-2, logits_of), (0, x1_statistics), (1, low_hidden))
        Es.close()
        R.close()
        M.close()
        Held.close()
        clear_semaphores()

        W = Scope()
        e1_hi = W.sb("e1_hi", [P, EXPERTS, C, HID], F32R)
        e1_lo = W.sb("e1_lo", [P, EXPERTS, C, HID], F32R)
        e2_hi = W.sb("e2_hi", [P, EXPERTS, HC, D], F32R)
        e2_lo = W.sb("e2_lo", [P, EXPERTS, HC, D], F32R)
        e1b_rows = W.sb("e1b_rows", [P, EXPERTS, HID])
        e2b_rows = W.sb("e2b_rows", [P, EXPERTS, D])
        F2 = Scope()
        rawm = F2.two("rawm", [P, C * HID])
        e1b_sb = F2.sb("e1b_sb", [EXPERTS, HID])
        e2b_sb = F2.sb("e2b_sb", [EXPERTS, D])
        row_of = F2.sb("row_of", [EXPERTS, EXPERTS, P])
        number = F2.sb("number", [P, GROUPS])
        number_past = F2.sb("number_past", [P, EXPERTS])
        tile_start = F2.sb("tile_start", [1, ST])
        logits = F2.sb("logits", [P, TILES, EXPERTS])
        prob = F2.sb("prob", [P, TILES, EXPERTS])
        same = F2.sb("same", [P, TILES, EXPERTS])
        place_no = F2.sb("place_no", [P, TILES, EXPERTS])
        most = F2.sb("most", [P, TILES])
        weight = F2.sb("weight", [P, TILES, 2])
        choice = F2.sb("choice", [P, TILES, 2])
        member = F2.sb("member", [P, GROUPS, J])
        running = F2.sb("running", [P, GROUPS, J])
        going_on = F2.sb("going_on", [P, GROUPS, J])
        totals = F2.sb("totals", [P, GROUPS])
        totals_i = F2.sb("totals_i", [P, GROUPS], I32)
        ends9 = F2.sb("ends9", [P, GROUPS])
        base9 = F2.sb("base9", [P, GROUPS])
        slot_f = F2.sb("slot_f", [P, J])
        place9 = F2.sb("place9", [P, J], I32)
        high9 = F2.sb("high9", [P, J], I32)
        tile_past = F2.sb("tile_past", [1, ST, EXPERTS])
        tile_expert = F2.sb("tile_expert", [1, ST])
        tokens = F2.sb("tokens", [P, J, 2], I32)
        upper2 = F2.sb("upper2", [P, P])
        nothing = F2.sb("nothing", [P, ST * 2], I32)
        ONCE = 7
        to_m = F2.two("to_m", [P, ONCE], I32)
        rec_m = F2.two("rec_m", [P, 2 * ONCE], I32)
        PBB = [F2.ps(f"PBB{s}", [P, D]) for s in range(4)]
        PCT = F2.ps("PCT", [P, D])
        s_in6 = [sem(f"s_in6{s}") for s in range(2)]
        s_small6 = sem("s_small6")
        s_hi6 = sem("s_hi6")
        s_lo6 = sem("s_lo6")
        s_c6 = sem("s_c6")
        s_rows6 = sem("s_rows6")
        s_rows6c = sem("s_rows6c")
        s_fill = sem("s_fill")
        s_exp = sem("s_exp")
        s_tail = sem("s_tail")
        s_cnt = sem("s_cnt")
        s_rt = sem("s_rt")
        s_place = sem("s_place")
        f_slotm = flow("f_slotm", 2)
        scat_m = transfers("scat_m", ONCE, credit=0)
        loads = [(e1_hi, e1_lo, E1, n) for n in range(EXPERTS)] + [(e2_hi, e2_lo, E2, n) for n in range(EXPERTS)]

        with nc.Block() as block:

            @block.sync
            def _(e):
                give_credit(e, [f_slotm])
                e.wait_ge(s_c6, 1)
                e.dma_start(list_d.rearrange("(p t) w -> p (t w)", p=P), nothing[:, :]).then_inc(s_fill, 16)
                e.dma_start(e1b_sb[:, :], e1b).then_inc(s_small6, 16)
                e.dma_start(e2b_sb[:, :], e2b).then_inc(s_small6, 16)
                for i, (_, _, w, n) in enumerate(loads):
                    if i >= 2:
                        e.wait_ge(s_lo6, i - 1)
                    e.dma_start(rawm[i % 2][:, :].rearrange("p (c n) -> p c n", n=w.shape[2]),
                                w[n].rearrange("(c p) n -> p c n", p=P)).then_inc(s_in6[i % 2], 16)

            @block.gpsimd
            def _(e):
                e.memset(nothing[:, :], 0).then_inc(s_c6, 1)
                e.memset(going_on[:, :, :], 1.0).then_inc(s_c6, 1)
                e.memset(row_of[:, :, :], 0.0).then_inc(s_c6, 1)
                e.iota(number[:, :], pattern=[[1, GROUPS]], base=0, channel_multiplier=0,
                       allow_small_or_imprecise_dtypes=True).then_inc(s_c6, 1)
                e.iota(number_past[:, :], pattern=[[1, EXPERTS]], base=EXPERTS, channel_multiplier=0,
                       allow_small_or_imprecise_dtypes=True).then_inc(s_c6, 1)
                e.iota(tile_start[:, :], pattern=[[P, ST]], base=0, channel_multiplier=0,
                       allow_small_or_imprecise_dtypes=True).then_inc(s_c6, 1)
                e.iota(tokens[:, :, 0].rearrange("p (t k) -> p t k", k=2), pattern=[[P, TILES], [0, 2]], base=0,
                       channel_multiplier=1).then_inc(s_c6, 1)
                e.affine_select(out=upper2[:, :], in_=ones[:, :], compare_op=ALU.is_gt, fill=0.0, base=0,
                                pattern=[[1, P]], channel_multiplier=-1).then_inc(s_c6, 1)
                e.wait_ge(s_c6, 8)
                e.memset(going_on[:, :, 0:1], 0.0).then_inc(s_c6, 1)
                e.affine_select(out=row_of[:, :, :], in_=row_of[:, :, :], compare_op=ALU.not_equal, fill=1.0,
                                base=0, pattern=[[-1, EXPERTS], [0, P]], channel_multiplier=1).then_inc(s_c6, 1)
                e.wait_ge(s_rt, CHOSEN)
                e.affine_select(out=choice[:, TILES - 1, :], in_=choice[:, TILES - 1, :], compare_op=ALU.is_ge,
                                fill=float(EXPERTS), base=TAIL - 1, pattern=[[0, 2]], channel_multiplier=-1)\
                    .then_inc(s_tail, 1)
                e.wait_ge(s_place, 1)
                e.wait_ge(s_fill, 16)
                scatter_records(e, list_d, place9, tokens, P, ONCE, to_m, rec_m, 0, J // ONCE, scat_m, f_slotm)

            @block.tensor
            def _(e):
                e.wait_ge(s_small6, 32)
                e.wait_ge(s_c6, 10)
                for i in range(EXPERTS // 2 + EXPERTS):
                    if i >= 4:
                        e.wait_ge(s_rows6c, i - 3)
                    if i < EXPERTS // 2:
                        e.matmul(PBB[i % 4][:, 0:HID], row_of[:, 2 * i, :], e1b_sb[:, :], start=True, stop=True)
                        e.matmul(PBB[i % 4][:, HID:2 * HID], row_of[:, 2 * i + 1, :], e1b_sb[:, :], start=True,
                                 stop=True).then_inc(s_rows6, 1)
                    else:
                        e.matmul(PBB[i % 4][:, :], row_of[:, i - EXPERTS // 2, :], e2b_sb[:, :], start=True,
                                 stop=True).then_inc(s_rows6, 1)
                e.wait_ge(s_rt, COUNTED)
                e.matmul(PCT[:, 0:GROUPS], upper2[:, :], totals[:, :], start=True, stop=True)
                e.matmul(PCT[:, 64:64 + GROUPS], ones[:, :], totals[:, :], start=True, stop=True).then_inc(s_cnt, 1)

            @block.scalar
            def _(e):
                e.wait_ge(s_rt, 4)
                e.activation(prob[:, :, :], prob[:, :, :], ACT.Exp).then_inc(s_exp, 1)
                for i in range(EXPERTS // 2 + EXPERTS):
                    e.wait_ge(s_rows6, i + 1)
                    to = (e1b_rows[:, 2 * i:2 * i + 2, :].rearrange("p e n -> p (e n)") if i < EXPERTS // 2
                          else e2b_rows[:, i - EXPERTS // 2, :])
                    e.activation(to, PBB[i % 4][:, :], ACT.Copy).then_inc(s_rows6c, 1)
                for i, (hi, _, w, n) in enumerate(loads):
                    e.wait_ge(s_in6[i % 2], 16 * (i // 2 + 1))
                    e.activation(hi[:, n, :, :].rearrange("p c n -> p (c n)"), rawm[i % 2][:, :], ACT.Copy)\
                        .then_inc(s_hi6, 1)

            @block.vector
            def _(e):
                done = [0]

                def then(ins):
                    done[0] += 1
                    ins.then_inc(s_rt, 1)
                    e.wait_ge(s_rt, done[0])

                def per_tile(a):
                    return a.unsqueeze(2).broadcast_to([P, TILES, EXPERTS])

                def per_expert(a):
                    return a.unsqueeze(1).broadcast_to([P, TILES, EXPERTS])

                then(e.tensor_tensor(logits[:, :, :], both[:, :, 0:EXPERTS], both[:, :, EXPERTS:2 * EXPERTS],
                                     ALU.add))
                then(e.tensor_tensor(logits[:, :, :], logits[:, :, :], per_expert(br_rows[:, :]), ALU.add))
                then(e.tensor_reduce(most[:, :], logits[:, :, :], AX.X, ALU.max))
                then(e.tensor_tensor(prob[:, :, :], logits[:, :, :], per_tile(most[:, :]), ALU.subtract))
                e.wait_ge(s_exp, 1)
                then(e.tensor_reduce(most[:, :], prob[:, :, :], AX.X, ALU.add))
                then(e.reciprocal(most[:, :], most[:, :]))
                then(e.tensor_tensor(prob[:, :, :], prob[:, :, :], per_tile(most[:, :]), ALU.mult))
                e.wait_ge(s_c6, 10)
                for k in range(2):
                    then(e.tensor_reduce(weight[:, :, k], prob[:, :, :], AX.X, ALU.max))
                    then(e.tensor_tensor(same[:, :, :], prob[:, :, :], per_tile(weight[:, :, k]), ALU.is_equal))
                    then(e.scalar_tensor_tensor(out=place_no[:, :, :], in0=same[:, :, :], scalar=-float(EXPERTS),
                                                in1=per_expert(number_past[:, :]), op0=ALU.mult, op1=ALU.add))
                    then(e.tensor_reduce(choice[:, :, k], place_no[:, :, :], AX.X, ALU.min))
                    if k == 0:
                        then(e.tensor_tensor(same[:, :, :], per_tile(choice[:, :, 0]),
                                             per_expert(number[:, 0:EXPERTS]), ALU.is_equal))
                        then(e.scalar_tensor_tensor(out=prob[:, :, :], in0=same[:, :, :], scalar=-2.0,
                                                    in1=prob[:, :, :], op0=ALU.mult, op1=ALU.add))
                assert done[0] == CHOSEN
                e.wait_ge(s_tail, 1)
                then(e.tensor_tensor(member[:, :, :], choice[:, :, :].rearrange("p t k -> p (t k)").unsqueeze(1)
                                     .broadcast_to([P, GROUPS, J]),
                                     number[:, :].unsqueeze(2).broadcast_to([P, GROUPS, J]), ALU.is_equal))
                then(e.tensor_tensor_scan(running[:, :, :].rearrange("p g j -> p (g j)"),
                                          going_on[:, :, :].rearrange("p g j -> p (g j)"),
                                          member[:, :, :].rearrange("p g j -> p (g j)"), 0.0, ALU.mult, ALU.add))
                then(e.tensor_copy(totals[:, :], running[:, :, J - 1]))
                assert done[0] == COUNTED
                e.wait_ge(s_cnt, 1)
                then(e.tensor_scalar(totals_i[:, :], PCT[:, 64:64 + GROUPS], float(P - 1), None, ALU.add))
                then(e.tensor_scalar(totals_i[:, :], totals_i[:, :], 7, 7, ALU.logical_shift_right,
                                     ALU.logical_shift_left))
                then(e.tensor_copy(totals[:, :], totals_i[:, :]))
                then(e.tensor_tensor_scan(ends9[:, :], going_on[:, 0, 1:1 + GROUPS], totals[:, :], 0.0, ALU.mult,
                                          ALU.add))
                then(e.tensor_tensor(base9[:, :], ends9[:, :], totals[:, :], ALU.subtract))
                then(e.tensor_tensor(base9[:, :], base9[:, :], PCT[:, 0:GROUPS], ALU.add))
                then(e.tensor_tensor(running[:, :, :], running[:, :, :],
                                     base9[:, :].unsqueeze(2).broadcast_to([P, GROUPS, J]), ALU.add))
                then(e.tensor_tensor(running[:, :, :], running[:, :, :], member[:, :, :], ALU.mult))
                then(e.tensor_reduce(slot_f[:, :], running[:, :, :].rearrange("p g j -> p j g"), AX.X, ALU.add))
                then(e.tensor_scalar(slot_i[:, :], slot_f[:, :], -1.0, None, ALU.add))
                then(e.tensor_scalar(high9[:, :], slot_i[:, :], 7, None, ALU.logical_shift_right))
                then(e.tensor_scalar(place9[:, :], slot_i[:, :], P - 1, None, ALU.bitwise_and))
                then(e.scalar_tensor_tensor(out=place9[:, :], in0=place9[:, :], scalar=float(ST),
                                            in1=high9[:, :], op0=ALU.mult, op1=ALU.add))
                e.tensor_copy(tokens[:, :, :].bitcast(F32)[:, :, 1], weight[:, :, :].rearrange("p t k -> p (t k)"))\
                    .then_inc(s_place, 1)
                then(e.tensor_tensor(tile_past[:, :, :],
                                     tile_start[:, :].unsqueeze(2).broadcast_to([1, ST, EXPERTS]),
                                     ends9[0:1, 0:EXPERTS].unsqueeze(1).broadcast_to([1, ST, EXPERTS]), ALU.is_ge))
                then(e.tensor_reduce(tile_expert[:, :], tile_past[:, :, :], AX.X, ALU.add))
                then(e.tensor_scalar(expert_of_tile[:, :], tile_expert[:, :], float(EXPERTS - 1), None, ALU.min))
                for i, (hi, lo, w, n) in enumerate(loads):
                    e.wait_ge(s_hi6, i + 1)
                    e.tensor_tensor(lo[:, n, :, :].rearrange("p c n -> p (c n)"), rawm[i % 2][:, :],
                                    hi[:, n, :, :].rearrange("p c n -> p (c n)").bitcast(F32), ALU.subtract)\
                        .then_inc(s_lo6, 1)
        F2.close()
        clear_semaphores()

        F3 = Scope()
        slots = F3.sb("slots", [P, ST, 2], I32)
        from_m = F3.two("from_m", [P, 2], I32)
        w_m = F3.two("w_m", [P, 2])
        ZG = F3.two("ZG", [P, 2, D])
        ZH = F3.two("ZHm", [P, 2, C, P], F32R)
        ZL = F3.two("ZLm", [P, 2, C, P], F32R)
        HB = F3.sb("HBm", [P, 2, HID])
        HR = F3.sb("HRm", [P, 2, HID])
        HH = F3.sb("HHm", [P, 2, HC, P], F32R)
        HL = F3.sb("HLm", [P, 2, HC, P], F32R)
        YO = F3.two("YOm", [P, 2, D])
        PTZ = F3.ps("PTZm", [P, 2, C, P])
        PH = F3.ps("PHm", [P, 2, HID])
        PHT = F3.ps("PHTm", [P, 2, HC, P])
        PY = [F3.ps(f"PYm{s}", [P, 2, D]) for s in range(2)]
        s_slots = sem("s_slots")
        y_out = transfers("y_out")
        z_in = transfers("z_in", 2, credit=0)
        f_from = flow("f_fromm", 2)
        f_tz = flow("f_tzm", 2)
        f_zh = flow("f_zhm", 2)
        f_zl = flow("f_zlm", 2)
        f_h = flow("f_hm")
        f_hb = flow("f_hbm", 2)
        f_hr = flow("f_hrm", 2)
        f_th = flow("f_thm")
        f_hh = flow("f_hhm")
        f_hl = flow("f_hlm")
        f_y = flow("f_ym")
        f_yo = flow("f_yom", 2)
        flows = [y_out, z_in, f_from, f_tz, f_zh, f_zl, f_h, f_hb, f_hr, f_th, f_hh, f_hl, f_y, f_yo]
        pairs_of_tiles = ST // 2

        def expert(e, t, k):
            return e.value_load(expert_of_tile[0:1, bass.ds(2 * t + k, 1)], min_val=0, max_val=EXPERTS - 1)

        with nc.Block() as block:

            @block.sync
            def _(e):
                give_credit(e, flows)
                e.dma_start(slots[:, :, :].rearrange("p t w -> p (t w)"), list_d.rearrange("(p t) w -> p (t w)", p=P))\
                    .then_inc(s_slots, 16)

                def store(t, s):
                    e.wait_ge(f_yo.sem, f_yo.after(t))
                    e.dma_start(ysl_d[bass.ds(2 * P * t, 2 * P), :].rearrange("(k p) d -> p k d", p=P),
                                YO[s][:, :, :]).then_inc(y_out.sems[s], 16)

                stages(e, pairs_of_tiles, (0, store))
                for s in range(2):
                    last = pairs_of_tiles - 1 - s
                    e.wait_ge(y_out.sems[s], y_out.after(last, last % 2))

            @block.gpsimd
            def _(e):
                e.wait_ge(s_slots, 16)

                def gather(t, s):
                    e.wait_ge(f_tz.sem, f_tz.freed(t))
                    e.wait_ge(f_hr.sem, f_hr.freed(t))
                    e.tensor_copy(from_m[s][:, :], slots[:, bass.ds(2 * t, 2), 0]).then_inc(f_from.sem, 1)
                    e.tensor_copy(w_m[s][:, :], slots[:, :, :].bitcast(F32)[:, bass.ds(2 * t, 2), 1])\
                        .then_inc(f_from.sem, 1)
                    e.wait_ge(f_from.sem, f_from.after(t))
                    e.tensor_tensor(pace[:, 1:2], zeros[:, 0:1], zeros[:, 1:2], ALU.add)
                    for k in range(2):
                        e.indirect_dma_start(ZG[s][:, k, :], None, z_d,
                                             bass.IndirectOffsetOnAxis(from_m[s][:, k:k + 1], 0))\
                            .then_inc(z_in.sems[s], 16)

                stages(e, pairs_of_tiles, (0, gather))

            @block.tensor
            def _(e):
                def first_products(t, s):
                    experts = [expert(e, t, k) for k in range(2)]
                    e.wait_ge(f_hb.sem, f_hb.after(t - 1))
                    for k in range(2):
                        e.wait_ge(f_zl.sem, f_zl.after(t, k + 1))
                        n = experts[k]
                        for c in range(C):
                            for i, (a, b) in enumerate(((ZH, e1_hi), (ZH, e1_lo), (ZL, e1_hi))):
                                mm = e.matmul(PH[:, k, :], a[s][:, k, c, :],
                                              b[:, bass.ds(n, 1), c, :].rearrange("p e n -> p (e n)"),
                                              start=(c == 0 and i == 0), stop=(c == C - 1 and i == 2))
                    mm.then_inc(f_h.sem, 1)

                def turn_rows(t, s):
                    e.wait_ge(z_in.sems[s], z_in.after(t, s))
                    for k in range(2):
                        e.wait_ge(f_zl.sem, f_zl.after(t - 1, k + 1))
                        for c in range(C):
                            mm = e.transpose(PTZ[:, k, c, :], ZG[s][:, k, c * P:(c + 1) * P], ident[:, :])
                        mm.then_inc(f_tz.sem, 1)

                def second_products(t, s):
                    experts = [expert(e, t, k) for k in range(2)]
                    e.wait_ge(f_hl.sem, f_hl.after(t))
                    e.wait_ge(f_yo.sem, f_yo.freed(t))
                    for k in range(2):
                        n = experts[k]
                        for m in range(HC):
                            for i, (a, b) in enumerate(((HH, e2_hi), (HH, e2_lo), (HL, e2_hi))):
                                mm = e.matmul(PY[s][:, k, :], a[:, k, m, :],
                                              b[:, bass.ds(n, 1), m, :].rearrange("p e n -> p (e n)"),
                                              start=(m == 0 and i == 0), stop=(m == HC - 1 and i == 2))
                    mm.then_inc(f_y.sem, 1)

                def turn_hidden(t, s):
                    e.wait_ge(f_hr.sem, f_hr.after(t))
                    e.wait_ge(f_hl.sem, f_hl.after(t - 1))
                    for k in range(2):
                        for m in range(HC):
                            mm = e.transpose(PHT[:, k, m, :], HR[:, k, m * P:(m + 1) * P], ident[:, :])
                    mm.then_inc(f_th.sem, 1)

                stages(e, pairs_of_tiles, (0, first_products), (1, turn_rows), (-1, second_products),
                       (0, turn_hidden))

            @block.scalar
            def _(e):
                def relu(t, s):
                    e.wait_ge(f_from.sem, f_from.after(t))
                    e.wait_ge(f_hb.sem, f_hb.after(t))
                    e.wait_ge(f_th.sem, f_th.after(t - 1))
                    for k in range(2):
                        e.activation(HR[:, k, :], HB[:, k, :], ACT.Relu, scale=w_m[s][:, k:k + 1])\
                            .then_inc(f_hr.sem, 1)

                def high_rows(t, s):
                    e.wait_ge(f_h.sem, f_h.freed(t))
                    for k in range(2):
                        e.wait_ge(f_tz.sem, f_tz.after(t, k + 1))
                        e.activation(ZH[s][:, k, :, :], PTZ[:, k, :, :], ACT.Copy).then_inc(f_zh.sem, 1)

                def high_hidden(t, s):
                    e.wait_ge(f_th.sem, f_th.after(t))
                    e.wait_ge(f_y.sem, f_y.after(t - 1))
                    e.activation(HH[:, :, :, :], PHT[:, :, :, :], ACT.Copy).then_inc(f_hh.sem, 1)

                stages(e, pairs_of_tiles, (0, relu), (1, high_rows), (0, high_hidden))

            @block.vector
            def _(e):
                e.wait_ge(s_slots, 16)

                def bias(t, s):
                    for k in range(2):
                        n = expert(e, t, k)
                        e.wait_ge(f_h.sem, f_h.after(t))
                        e.wait_ge(f_hr.sem, f_hr.after(t - 1))
                        e.tensor_tensor(HB[:, k, :], PH[:, k, :],
                                        e1b_rows[:, bass.ds(n, 1), :].rearrange("p e n -> p (e n)"), ALU.add)\
                            .then_inc(f_hb.sem, 1)

                def low_rows(t, s):
                    for k in range(2):
                        e.wait_ge(f_zh.sem, f_zh.after(t, k + 1))
                        e.tensor_tensor(ZL[s][:, k, :, :], PTZ[:, k, :, :], ZH[s][:, k, :, :].bitcast(F32),
                                        ALU.subtract).then_inc(f_zl.sem, 1)

                def outputs(t, s):
                    for k in range(2):
                        n = expert(e, t, k)
                        e.wait_ge(f_y.sem, f_y.after(t))
                        e.wait_ge(y_out.sems[s], y_out.freed(t, s))
                        e.scalar_tensor_tensor(out=YO[s][:, k, :],
                                               in0=e2b_rows[:, bass.ds(n, 1), :].rearrange("p e n -> p (e n)"),
                                               scalar=slots[:, :, :].bitcast(F32)[:, bass.ds(2 * t + k, 1), 1],
                                               in1=PY[s][:, k, :], op0=ALU.mult,
                                               op1=ALU.add).then_inc(f_yo.sem, 1)

                def low_hidden(t, s):
                    e.wait_ge(f_hh.sem, f_hh.after(t))
                    e.tensor_tensor(HL[:, :, :, :], PHT[:, :, :, :], HH[:, :, :, :].bitcast(F32), ALU.subtract)\
                        .then_inc(f_hl.sem, 1)

                stages(e, pairs_of_tiles, (0, bias), (1, low_rows), (-1, outputs), (0, low_hidden))
        F3.close()
        W.close()
        clear_semaphores()

        F4 = Scope()
        SUM = 7
        sum_turns = TILES // SUM
        from_y = F4.two("from_y", [P, 2 * SUM], I32)
        XS = F4.two("XS", [P, SUM, D])
        YG = F4.two("YG", [P, 2 * SUM, D])
        x_in7 = transfers("x_in7")
        out_out = transfers("out_out")
        y_in7 = transfers("y_in7", 2 * SUM, credit=0)
        f_from7 = flow("f_from7")
        f_sum7 = flow("f_sum7", 2)
        flows = [x_in7, out_out, y_in7, f_from7, f_sum7]
        assert sum_turns * SUM == TILES

        with nc.Block() as block:

            @block.sync
            def _(e):
                give_credit(e, flows)

                def load(t, s):
                    e.wait_ge(out_out.sems[s], out_out.freed(t, s))
                    e.dma_start(XS[s][:, :, :], x1_d[bass.ds(SUM * P * t, SUM * P), :]
                                .rearrange("(g p) d -> p g d", p=P)).then_inc(x_in7.sems[s], 16)

                def store(t, s):
                    e.wait_ge(f_sum7.sem, f_sum7.after(t))
                    if isinstance(t, int) and t == sum_turns - 1:
                        whole = N - TAIL - SUM * P * t
                        e.dma_start(out[SUM * P * t:N - TAIL, :].rearrange("(g p) d -> p g d", p=P),
                                    XS[s][:, 0:whole // P, :]).then_inc(out_out.sems[s], 16)
                        e.dma_start(out[N - TAIL:N, :], XS[s][0:TAIL, SUM - 1, :]).then_inc(out_out.sems[s], 16)
                        return
                    e.dma_start(out[bass.ds(SUM * P * t, SUM * P), :].rearrange("(g p) d -> p g d", p=P),
                                XS[s][:, :, :]).then_inc(out_out.sems[s], 16)

                stages(e, sum_turns, (1, load), (0, store))
                last = sum_turns - 1
                e.wait_ge(out_out.sems[last % 2], out_out.after(last, last % 2) + 16)
                e.wait_ge(out_out.sems[(last - 1) % 2], out_out.after(last - 1, (last - 1) % 2))

            @block.gpsimd
            def _(e):
                def gather(t, s):
                    e.wait_ge(f_sum7.sem, f_sum7.freed(t))
                    e.tensor_copy(from_y[s][:, :], slot_i[:, bass.ds(2 * SUM * t, 2 * SUM)])\
                        .then_inc(f_from7.sem, 1)
                    e.wait_ge(f_from7.sem, f_from7.after(t))
                    e.tensor_tensor(pace[:, 1:2], zeros[:, 0:1], zeros[:, 1:2], ALU.add)
                    for j in range(2 * SUM):
                        e.indirect_dma_start(YG[s][:, j, :], None, ysl_d,
                                             bass.IndirectOffsetOnAxis(from_y[s][:, j:j + 1], 0))\
                            .then_inc(y_in7.sems[s], 16)

                stages(e, sum_turns, (0, gather))

            @block.vector
            def _(e):
                def add(t, s):
                    e.wait_ge(x_in7.sems[s], x_in7.after(t, s))
                    e.wait_ge(y_in7.sems[s], y_in7.after(t, s))
                    for k in range(2):
                        if k:
                            e.wait_ge(f_sum7.sem, f_sum7.after(t, 1))
                        e.tensor_tensor(XS[s][:, :, :], XS[s][:, :, :],
                                        YG[s][:, :, :].rearrange("p (g k) d -> p g k d", k=2)[:, :, k, :], ALU.add)\
                            .then_inc(f_sum7.sem, 1)

                stages(e, sum_turns, (0, add))
        F4.close()
        G.close()


_INS = ['x', 'src', 'dst', 'L0_gnn_self_w', 'L0_gnn_self_b', 'L0_gnn_neigh_w', 'L0_gnn_neigh_b', 'L0_mix_Wq',
        'L0_mix_bq', 'L0_mix_Wk', 'L0_mix_bk', 'L0_mix_Wv', 'L0_mix_bv', 'L0_mix_Wo', 'L0_mix_bo', 'L0_mix_W1',
        'L0_mix_b1', 'L0_mix_W2', 'L0_mix_b2', 'L0_mix_g1', 'L0_mix_be1', 'L0_mix_g2', 'L0_mix_be2', 'L0_ffn_Wr',
        'L0_ffn_br', 'L0_ffn_W1', 'L0_ffn_b1', 'L0_ffn_W2', 'L0_ffn_b2']
_TURNED = ('L0_gnn_self_w', 'L0_gnn_neigh_w')
_COLUMNS = ('L0_mix_g1', 'L0_mix_be1', 'L0_mix_g2', 'L0_mix_be2')


def kernel(**inputs):
    import numpy as _np
    import concourse.bacc as _bacc
    from concourse import mybir as _mybir
    from concourse.bass_utils import run_bass_kernel_spmd as _run

    nc = _bacc.Bacc("TRN2", target_bir_lowering=False, num_devices=1)
    arrays, args = {}, []
    for name in _INS:
        a = _np.asarray(inputs[name])
        if name in _COLUMNS:
            a = a.reshape(-1, P).T
        a = _np.ascontiguousarray(a.T if name in _TURNED else a)
        arrays[f"in_{name}_dram"] = a
        args.append(nc.dram_tensor(f"in_{name}_dram", a.shape, _mybir.dt.from_np(a.dtype), kind="ExternalInput").ap())
    args.append(nc.dram_tensor("out_0_dram", arrays["in_x_dram"].shape, F32, kind="ExternalOutput").ap())
    gps_layer_kernel(nc, *args)
    r = _run(nc, [arrays], core_ids=[0])
    return r.results[0]["out_0_dram"]
```
